# Optimizing a Trainium2 kernel written in Bass

```python
import numpy as np
import jax
import jax.numpy as jnp

def _softmax(x, axis=-1):
    return jax.nn.softmax(x, axis=axis)

def _gelu(x):
    return jax.nn.gelu(x, approximate=True)

def _silu(x):
    return jax.nn.silu(x)

def _sigmoid(x):
    return jax.nn.sigmoid(x)

def _layernorm(x, axis=-1, eps=1e-05):
    m = jnp.mean(x, axis=axis, keepdims=True)
    v = jnp.var(x, axis=axis, keepdims=True)
    return (x - m) / jnp.sqrt(v + eps)

def _scatter_add(tgt, idx, src, axis=0):
    return tgt.at[idx].add(src)

def _segment_sum(src, seg, n):
    return jax.ops.segment_sum(src, seg, n)
kernel_name = 'mk_prb_d2_jaxref_r8_c15732'

def setup_inputs(seed: int=0):
    np.random.seed(seed)
    _w = jnp.asarray

    def _L0_attn_setup():
        import jax, jax.numpy as jnp
        import numpy as np
        D_MODEL = 128
        N_HEAD = 16
        HEAD_DIM = D_MODEL // N_HEAD
        D_INNER = 512
        N_LAYER = 4
        NEG = jnp.finfo(jnp.float32).min

        def _ln(x, w, b):
            m = x.mean(-1, keepdims=True)
            v = ((x - m) ** 2).mean(-1, keepdims=True)
            return (x - m) * jax.lax.rsqrt(v + 1e-06) * w + b

        def _pos_emb(k_len):
            pos = jnp.arange(k_len - 1, -1, -1, dtype=jnp.float32)
            inv = 1.0 / 10000.0 ** (jnp.arange(0, HEAD_DIM, 2, dtype=jnp.float32) / HEAD_DIM)
            s = pos[:, None] * inv[None, :]
            return jnp.concatenate([jnp.sin(s), jnp.cos(s)], axis=-1)

        def _rel_shift(x, q_len, k_len):
            B, H = (x.shape[0], x.shape[1])
            zp = jnp.zeros((B, H, q_len, 1), x.dtype)
            xp = jnp.concatenate([zp, x], axis=-1).reshape(B, H, k_len + 1, q_len)
            return xp[:, :, 1:, :].reshape(B, H, q_len, k_len)

        def _attn(xn, Wq, bq, Wk, bk, Wv, bv, Wo, bo, u):
            B, S, _ = xn.shape
            sh = lambda t: t.reshape(B, S, N_HEAD, HEAD_DIM).transpose(0, 2, 1, 3)
            q = sh(xn @ Wq.T + bq)
            k = sh(xn @ Wk.T + bk)
            v = sh(xn @ Wv.T + bv)
            scores = jnp.einsum('bhqd,bhkd->bhqk', q, k)
            r = _pos_emb(S)
            rel = jnp.einsum('bhqd,ld->bhql', q + u[None, :, None, :], r)
            scores = (scores + _rel_shift(rel, S, S)) * HEAD_DIM ** (-0.5)
            mask = jnp.arange(S)[None, :] > jnp.arange(S)[:, None]
            scores = jnp.where(mask[None, None], NEG, scores)
            p = jax.nn.softmax(scores, axis=-1)
            ctx = jnp.einsum('bhqk,bhkd->bhqd', p, v).transpose(0, 2, 1, 3).reshape(B, S, D_MODEL)
            return ctx @ Wo.T + bo
        key = jax.random.key(seed)
        ks = jax.random.split(key, 20)
        B, S = (4, 128)
        p = lambda k, shp, s=0.02: jax.random.normal(k, shp, dtype=jnp.float32) * s
        L = N_LAYER
        return {'x': jax.random.normal(ks[0], (B, S, D_MODEL), dtype=jnp.float32), 'Wq': p(ks[1], (L, D_MODEL, D_MODEL)), 'bq': jnp.zeros((L, D_MODEL)), 'Wk': p(ks[2], (L, D_MODEL, D_MODEL)), 'bk': jnp.zeros((L, D_MODEL)), 'Wv': p(ks[3], (L, D_MODEL, D_MODEL)), 'bv': jnp.zeros((L, D_MODEL)), 'Wo': p(ks[4], (L, D_MODEL, D_MODEL)), 'bo': jnp.zeros((L, D_MODEL)), 'u_bias': p(ks[5], (L, N_HEAD, HEAD_DIM), 0.02), 'W1': p(ks[6], (L, D_INNER, D_MODEL)), 'b1': jnp.zeros((L, D_INNER)), 'W2': p(ks[7], (L, D_MODEL, D_INNER)), 'b2': jnp.zeros((L, D_MODEL)), 'ln1_w': jnp.ones((L, D_MODEL)), 'ln1_b': jnp.zeros((L, D_MODEL)), 'ln2_w': jnp.ones((L, D_MODEL)), 'ln2_b': jnp.zeros((L, D_MODEL))}
    _L0_attn_in = _L0_attn_setup()

    def _L0_ffn_setup():
        import jax, jax.numpy as jnp
        import numpy as np
        ALPHA = 1.0
        key = jax.random.key(seed)
        ks = jax.random.split(key, 7)
        B, S, IN, OUT = (8, 1024, 128, 128)
        RANK, DDIM, UDIM = (4, 100, 50)
        return {'hidden_states': jax.random.normal(ks[0], (B, S, IN), dtype=jnp.float32), 'W': jax.random.normal(ks[1], (OUT, IN), dtype=jnp.float32) * 0.02, 'b': jax.random.normal(ks[2], (OUT,), dtype=jnp.float32) * 0.02, 'lora_down': jax.random.normal(ks[3], (RANK, DDIM), dtype=jnp.float32) * 0.1, 'lora_up': jax.random.normal(ks[4], (UDIM, RANK), dtype=jnp.float32) * 0.1, 'down_aux': jax.random.normal(ks[5], (DDIM, IN), dtype=jnp.float32) * 0.03, 'up_aux': jax.random.normal(ks[6], (OUT, UDIM), dtype=jnp.float32) * 0.03}
    _L0_ffn_in = _L0_ffn_setup()

    def _L1_attn_setup():
        import jax, jax.numpy as jnp
        import numpy as np
        D_MODEL = 128
        N_HEADS = 16
        D_HEAD = 64
        BATCH = 4
        SEQ = 256
        NEG = -1000000000.0
        key = jax.random.key(seed)
        k1, k2, k3, k4, k5 = jax.random.split(key, 5)
        x = jax.random.normal(k1, (BATCH, SEQ, D_MODEL), dtype=jnp.float32)
        std = 0.02
        wq = jax.random.normal(k2, (N_HEADS, D_HEAD, D_MODEL), dtype=jnp.float32) * std
        wk = jax.random.normal(k3, (N_HEADS, D_HEAD, D_MODEL), dtype=jnp.float32) * std
        wv = jax.random.normal(k4, (N_HEADS, D_HEAD, D_MODEL), dtype=jnp.float32) * std
        wo = jax.random.normal(k5, (D_MODEL, N_HEADS * D_HEAD), dtype=jnp.float32) * std
        return {'x': x, 'wq': wq, 'wk': wk, 'wv': wv, 'wo': wo}
    _L1_attn_in = _L1_attn_setup()

    def _L1_ffn_setup():
        import jax, jax.numpy as jnp
        import numpy as np
        HIDDEN = 128
        N_EXPERTS = 8
        TOP_K = 2
        INTER = 176
        N_SHARED = 2
        SCALE = 1.0
        key = jax.random.key(seed)
        ks = jax.random.split(key, 9)
        s_h = 1.0 / np.sqrt(HIDDEN)
        s_i = 1.0 / np.sqrt(INTER)
        x = jax.random.normal(ks[0], (2, 256, HIDDEN), dtype=jnp.float32)
        gate_w = jax.random.uniform(ks[1], (N_EXPERTS, HIDDEN), jnp.float32, -s_h, s_h)
        wg = jax.random.uniform(ks[2], (N_EXPERTS, HIDDEN, INTER), jnp.float32, -s_h, s_h)
        wu = jax.random.uniform(ks[3], (N_EXPERTS, HIDDEN, INTER), jnp.float32, -s_h, s_h)
        wd = jax.random.uniform(ks[4], (N_EXPERTS, INTER, HIDDEN), jnp.float32, -s_i, s_i)
        si = INTER * N_SHARED
        s_si = 1.0 / np.sqrt(si)
        swg = jax.random.uniform(ks[5], (HIDDEN, si), jnp.float32, -s_h, s_h)
        swu = jax.random.uniform(ks[6], (HIDDEN, si), jnp.float32, -s_h, s_h)
        swd = jax.random.uniform(ks[7], (si, HIDDEN), jnp.float32, -s_si, s_si)
        return {'x': x, 'gate_w': gate_w, 'wg': wg, 'wu': wu, 'wd': wd, 'swg': swg, 'swu': swu, 'swd': swd}
    _L1_ffn_in = _L1_ffn_setup()
    _d = {'L0_attn_x': _L0_attn_in['x'], 'L0_attn_Wq': _L0_attn_in['Wq'], 'L0_attn_bq': _L0_attn_in['bq'], 'L0_attn_Wk': _L0_attn_in['Wk'], 'L0_attn_bk': _L0_attn_in['bk'], 'L0_attn_Wv': _L0_attn_in['Wv'], 'L0_attn_bv': _L0_attn_in['bv'], 'L0_attn_Wo': _L0_attn_in['Wo'], 'L0_attn_bo': _L0_attn_in['bo'], 'L0_attn_u_bias': _L0_attn_in['u_bias'], 'L0_attn_W1': _L0_attn_in['W1'], 'L0_attn_b1': _L0_attn_in['b1'], 'L0_attn_W2': _L0_attn_in['W2'], 'L0_attn_b2': _L0_attn_in['b2'], 'L0_attn_ln1_w': _L0_attn_in['ln1_w'], 'L0_attn_ln1_b': _L0_attn_in['ln1_b'], 'L0_attn_ln2_w': _L0_attn_in['ln2_w'], 'L0_attn_ln2_b': _L0_attn_in['ln2_b'], 'L0_ffn_W': _L0_ffn_in['W'], 'L0_ffn_b': _L0_ffn_in['b'], 'L0_ffn_lora_down': _L0_ffn_in['lora_down'], 'L0_ffn_lora_up': _L0_ffn_in['lora_up'], 'L0_ffn_down_aux': _L0_ffn_in['down_aux'], 'L0_ffn_up_aux': _L0_ffn_in['up_aux'], 'L1_attn_wq': _L1_attn_in['wq'], 'L1_attn_wk': _L1_attn_in['wk'], 'L1_attn_wv': _L1_attn_in['wv'], 'L1_attn_wo': _L1_attn_in['wo'], 'L1_ffn_gate_w': _L1_ffn_in['gate_w'], 'L1_ffn_wg': _L1_ffn_in['wg'], 'L1_ffn_wu': _L1_ffn_in['wu'], 'L1_ffn_wd': _L1_ffn_in['wd'], 'L1_ffn_swg': _L1_ffn_in['swg'], 'L1_ffn_swu': _L1_ffn_in['swu'], 'L1_ffn_swd': _L1_ffn_in['swd']}
    _x0 = _d['L0_attn_x']
    _d['L0_attn_x'] = jax.random.normal(jax.random.fold_in(jax.random.key(seed), 1), (2, 1024, 128), dtype=_x0.dtype)
    del _x0
    return _d

def reference(L0_attn_x, L0_attn_Wq, L0_attn_bq, L0_attn_Wk, L0_attn_bk, L0_attn_Wv, L0_attn_bv, L0_attn_Wo, L0_attn_bo, L0_attn_u_bias, L0_attn_W1, L0_attn_b1, L0_attn_W2, L0_attn_b2, L0_attn_ln1_w, L0_attn_ln1_b, L0_attn_ln2_w, L0_attn_ln2_b, L0_ffn_W, L0_ffn_b, L0_ffn_lora_down, L0_ffn_lora_up, L0_ffn_down_aux, L0_ffn_up_aux, L1_attn_wq, L1_attn_wk, L1_attn_wv, L1_attn_wo, L1_ffn_gate_w, L1_ffn_wg, L1_ffn_wu, L1_ffn_wd, L1_ffn_swg, L1_ffn_swu, L1_ffn_swd):

    def _L0_attn_ref(x, Wq, bq, Wk, bk, Wv, bv, Wo, bo, u_bias, W1, b1, W2, b2, ln1_w, ln1_b, ln2_w, ln2_b):
        import jax, jax.numpy as jnp
        import numpy as np
        D_MODEL = 128
        N_HEAD = 16
        HEAD_DIM = D_MODEL // N_HEAD
        D_INNER = 512
        N_LAYER = 4
        NEG = jnp.finfo(jnp.float32).min

        def _ln(x, w, b):
            m = x.mean(-1, keepdims=True)
            v = ((x - m) ** 2).mean(-1, keepdims=True)
            return (x - m) * jax.lax.rsqrt(v + 1e-06) * w + b

        def _pos_emb(k_len):
            pos = jnp.arange(k_len - 1, -1, -1, dtype=jnp.float32)
            inv = 1.0 / 10000.0 ** (jnp.arange(0, HEAD_DIM, 2, dtype=jnp.float32) / HEAD_DIM)
            s = pos[:, None] * inv[None, :]
            return jnp.concatenate([jnp.sin(s), jnp.cos(s)], axis=-1)

        def _rel_shift(x, q_len, k_len):
            B, H = (x.shape[0], x.shape[1])
            zp = jnp.zeros((B, H, q_len, 1), x.dtype)
            xp = jnp.concatenate([zp, x], axis=-1).reshape(B, H, k_len + 1, q_len)
            return xp[:, :, 1:, :].reshape(B, H, q_len, k_len)

        def _attn(xn, Wq, bq, Wk, bk, Wv, bv, Wo, bo, u):
            B, S, _ = xn.shape
            sh = lambda t: t.reshape(B, S, N_HEAD, HEAD_DIM).transpose(0, 2, 1, 3)
            q = sh(xn @ Wq.T + bq)
            k = sh(xn @ Wk.T + bk)
            v = sh(xn @ Wv.T + bv)
            scores = jnp.einsum('bhqd,bhkd->bhqk', q, k)
            r = _pos_emb(S)
            rel = jnp.einsum('bhqd,ld->bhql', q + u[None, :, None, :], r)
            scores = (scores + _rel_shift(rel, S, S)) * HEAD_DIM ** (-0.5)
            mask = jnp.arange(S)[None, :] > jnp.arange(S)[:, None]
            scores = jnp.where(mask[None, None], NEG, scores)
            p = jax.nn.softmax(scores, axis=-1)
            ctx = jnp.einsum('bhqk,bhkd->bhqd', p, v).transpose(0, 2, 1, 3).reshape(B, S, D_MODEL)
            return ctx @ Wo.T + bo
        h = x
        for l in range(N_LAYER):
            xn = _ln(h, ln1_w[l], ln1_b[l])
            a = _attn(xn, Wq[l], bq[l], Wk[l], bk[l], Wv[l], bv[l], Wo[l], bo[l], u_bias[l])
            h = h + a
            fn = _ln(h, ln2_w[l], ln2_b[l])
            ff = jax.nn.gelu(fn @ W1[l].T + b1[l], approximate=False) @ W2[l].T + b2[l]
            h = h + ff
        return h

    def _L0_ffn_ref(hidden_states, W, b, lora_down, lora_up, down_aux, up_aux):
        import jax, jax.numpy as jnp
        import numpy as np
        ALPHA = 1.0
        lilora_weight = up_aux @ (lora_up @ (lora_down @ down_aux))
        base = jnp.einsum('bsi,oi->bso', hidden_states, W) + b
        delta = jnp.einsum('bsi,oi->bso', hidden_states, lilora_weight)
        return base + ALPHA * delta

    def _L1_attn_ref(x, wq, wk, wv, wo):
        import jax, jax.numpy as jnp
        import numpy as np
        D_MODEL = 128
        N_HEADS = 16
        D_HEAD = 64
        BATCH = 4
        SEQ = 256
        NEG = -1000000000.0
        b, s, _ = x.shape
        scale = jnp.sqrt(jnp.asarray(D_HEAD, x.dtype))
        q = jnp.einsum('bsd,hed->bhse', x, wq)
        k = jnp.einsum('bsd,hed->bhse', x, wk)
        v = jnp.einsum('bsd,hed->bhse', x, wv)
        scores = jnp.einsum('bhse,bhte->bhst', q, k) / scale
        causal_mask = jnp.triu(jnp.ones((s, s), dtype=bool), k=1)
        scores = jnp.where(causal_mask, jnp.asarray(NEG, scores.dtype), scores)
        weights = jax.nn.softmax(scores, axis=-1)
        heads = jnp.einsum('bhst,bhte->bhse', weights, v)
        concat = heads.transpose(0, 2, 1, 3).reshape(b, s, N_HEADS * D_HEAD)
        return concat @ wo.T

    def _L1_ffn_ref(x, gate_w, wg, wu, wd, swg, swu, swd):
        import jax, jax.numpy as jnp
        import numpy as np
        HIDDEN = 128
        N_EXPERTS = 8
        TOP_K = 2
        INTER = 176
        N_SHARED = 2
        SCALE = 1.0
        B, S, H = x.shape
        xf = x.reshape(-1, H)
        T = xf.shape[0]
        logits = xf.astype(jnp.float32) @ gate_w.astype(jnp.float32).T
        scores = jax.nn.softmax(logits, axis=-1)
        topw, topi = jax.lax.top_k(scores, TOP_K)
        denom = topw.sum(axis=-1, keepdims=True) + 1e-20
        topw = topw / denom * SCALE
        wdense = jnp.zeros((T, N_EXPERTS), jnp.float32).at[jnp.arange(T)[:, None], topi].set(topw)
        hg = jnp.einsum('th,ehi->eti', xf, wg)
        hu = jnp.einsum('th,ehi->eti', xf, wu)
        eo = jnp.einsum('eti,eih->eth', jax.nn.silu(hg) * hu, wd)
        y = jnp.einsum('te,eth->th', wdense, eo)
        shared = jax.nn.silu(xf @ swg) * (xf @ swu) @ swd
        return (y + shared).reshape(B, S, H)
    x = L0_attn_x
    xn = _layernorm(x, axis=-1)
    x = x + _L0_attn_ref(xn, L0_attn_Wq, L0_attn_bq, L0_attn_Wk, L0_attn_bk, L0_attn_Wv, L0_attn_bv, L0_attn_Wo, L0_attn_bo, L0_attn_u_bias, L0_attn_W1, L0_attn_b1, L0_attn_W2, L0_attn_b2, L0_attn_ln1_w, L0_attn_ln1_b, L0_attn_ln2_w, L0_attn_ln2_b) + _L0_ffn_ref(xn, L0_ffn_W, L0_ffn_b, L0_ffn_lora_down, L0_ffn_lora_up, L0_ffn_down_aux, L0_ffn_up_aux)
    xn = _layernorm(x, axis=-1)
    x = x + _L1_attn_ref(xn, L1_attn_wq, L1_attn_wk, L1_attn_wv, L1_attn_wo) + _L1_ffn_ref(xn, L1_ffn_gate_w, L1_ffn_wg, L1_ffn_wu, L1_ffn_wd, L1_ffn_swg, L1_ffn_swu, L1_ffn_swd)
    return x

_drawn_inputs = setup_inputs


def setup_inputs(seed=0):
    import zlib

    import numpy as np

    out = dict(_drawn_inputs(seed))
    spreads = {'L0_attn_bq': (0.0, 2.0),
     'L0_attn_bk': (0.0, 2.0),
     'L0_attn_bv': (0.0, 2.0),
     'L0_attn_bo': (0.0, 0.8),
     'L0_attn_b1': (0.0, 2.0),
     'L0_attn_b2': (0.0, 0.8),
     'L0_attn_ln1_w': (1.0, 0.6),
     'L0_attn_ln1_b': (0.0, 2.0),
     'L0_attn_ln2_w': (1.0, 0.6),
     'L0_attn_ln2_b': (0.0, 2.0)}
    factors = {'L0_attn_Wq': 33.446,
     'L0_attn_Wk': 32.954,
     'L0_attn_Wv': 15.959,
     'L0_attn_u_bias': 64.0,
     'L0_ffn_b': 44.496,
     'L0_ffn_lora_down': 7.296,
     'L0_ffn_lora_up': 7.961,
     'L0_ffn_down_aux': 6.922,
     'L0_ffn_up_aux': 7.694,
     'L1_attn_wq': 25.285,
     'L1_attn_wk': 25.428,
     'L1_attn_wv': 4.606,
     'L1_attn_wo': 4.962,
     'L0_attn_Wo': 3.323,
     'L0_attn_W1': 8.0,
     'L0_attn_W2': 7.251,
     'L0_ffn_W': 8.0,
     'L1_ffn_gate_w': 8.0,
     'L1_ffn_wg': 8.0,
     'L1_ffn_wu': 8.0,
     'L1_ffn_wd': 8.0,
     'L1_ffn_swg': 8.0,
     'L1_ffn_swu': 8.0,
     'L1_ffn_swd': 8.0}
    for name, (base, spread) in spreads.items():
        noise = np.random.default_rng([zlib.crc32(name.encode()), seed]).standard_normal(out[name].shape)
        drawn = base * np.exp(spread * noise) if base else spread * noise
        out[name] = jnp.asarray(drawn.astype(out[name].dtype))
    for name, factor in factors.items():
        out[name] = (out[name] * factor).astype(out[name].dtype)
    return out
```

```python
from contextlib import ExitStack

import numpy as np
import concourse.bass as bass
from concourse import mybir

F32 = mybir.dt.float32
BF16 = mybir.dt.bfloat16
ALU = mybir.AluOpType
ACT = mybir.ActivationFunctionType
AX_X = mybir.AxisListType.X

P = 128
NB, S, D = 2, 1024, 128
T = NB * S
NT = T // P
CH = 512
NC = T // CH
TPC = CH // P
LAYERS, H0, HD0, FF = 4, 16, 8, 512
GH = 4
NG = NB * H0 // GH
GPB = NG // NB
NF = FF // P
TERMS = [(0, 0), (0, 1), (0, 2), (1, 0), (1, 1), (2, 0)]
HALF = len(TERMS) * HD0
KROWS = 2 * HALF
KMAX = KROWS + 2
SB_ = S // P
SCALE0 = HD0 ** -0.5
NEG = -1.0e30

H1, HD1 = 16, 64
KFULL = 96
SCALE1 = HD1 ** -0.5
NE, INTER, SHARED = 8, 176, 352
HID = NE * INTER + SHARED
NHC = -(-HID // P)

LORA_R, LORA_D, LORA_U = 4, 100, 50

WQ, WQS, WK, WV, WO = range(5)
VC = ["bq", "bqs", "u", "us", "bk", "ln1w", "ln1b", "ln2w", "ln2b", "b1_0", "b1_1", "b1_2", "b1_3"]
COL = {n: i for i, n in enumerate(VC)}
NVC = len(VC)
VB = {"bv": 0, "bo": 1, "b2": 2}

SB_ = S // P
STEPS = [(c, jb, max(c * CH, jb * P), (c + 1) * CH - max(c * CH, jb * P))
         for c in range(S // CH) for jb in range((c + 1) * TPC)]
NS = len(STEPS)
DIAG = [jb * P >= c * CH for c, jb, _, _ in STEPS]
C_END = [max(s for s in range(NS) if STEPS[s][0] == c) for c in range(S // CH)]
ATILES = [(ib, k0, min((ib + 1) * P - k0, CH), (ib + 1) * P - k0 <= CH)
          for ib in range(SB_) for k0 in range(0, (ib + 1) * P, CH)]

LAG = 2
SLOTS = NS + LAG
A_LIST = [(r, *a) for a in ATILES for r in range(GH)]
NA = len(A_LIST)
A_PER = 4
T_SLOT = [C_END[0] + LAG + 2, SLOTS - 1]
M_SLOT = -(-NA // A_PER) - 1


def group_items(last):
    out = []
    for slot in range(SLOTS):
        if not last:
            out += [(slot, "A", i) for i in range(slot * A_PER, min((slot + 1) * A_PER, NA))]
            if slot == M_SLOT:
                out.append((slot, "M", 0))
        out += [(slot, "T", c) for c in range(S // CH) if T_SLOT[c] == slot]
    return out


V_LN, V_PROJ, V_A = NC, 3 * NC, NA + 1
V_GROUP = V_A + S // CH
V_ATT = V_A + (NG - 1) * V_GROUP + S // CH
V_LAYER = V_LN + V_PROJ + V_ATT + 4 * NC
V_START = 2 * NC + 3
V_G0 = V_LN + V_PROJ + V_A
V_POST = V_LN + V_PROJ + V_ATT
A_K, A_B, A_G = NC // 2, NS * GH // 2, 2 * NF
A_LAYER = A_K + NG * A_B + A_G
USES = [len(range(u, NG, 3)) for u in range(3)]

LAG1 = 2
SLOTS1 = NS + LAG1
A1_LIST = [(b, *a) for a in ATILES for b in range(NB)]
NA1 = len(A1_LIST)
A1_PER = 3
A1_FIRST = 3
P1BUF = 6
OUT_W = D + 1
OUT_SPLIT = [list(range(NB * TPC))[i:i + CH // OUT_W] for i in range(0, NB * TPC, CH // OUT_W)]
O_SLOT = [C_END[0] + LAG1 + 2, SLOTS1 - 1]
M1_SLOT = A1_FIRST - 1 + -(-NA1 // A1_PER)
V_TILES = CH // HD1
V1_PROJ = NC + NT // V_TILES


def head_items(last):
    out = []
    for slot in range(SLOTS1):
        if not last:
            if slot < A1_FIRST:
                out += [(slot, "P", i) for i in range(2 * slot, min(2 * slot + 2, V1_PROJ))]
            else:
                n = (slot - A1_FIRST) * A1_PER
                out += [(slot, "A", i) for i in range(n, min(n + A1_PER, NA1))]
            if slot == M1_SLOT:
                out.append((slot, "M", 0))
        out += [(slot, "O", (c, k)) for c in range(S // CH) if O_SLOT[c] == slot for k in range(len(OUT_SPLIT))]
    return out


V_R = V_START + LAYERS * V_LAYER
V_MOE = V_R + NC + 1 + NC
MOE_J = 2 * NC
MOE_TURNS = NHC // 2
MOE_V = 2 * MOE_J
V_H = V_MOE + MOE_TURNS * MOE_V
V_H0 = V_H + V1_PROJ + NA1 + 1
V1_HEAD = len(head_items(False))
A_MOE = LAYERS * A_LAYER
A_H = A_MOE + MOE_TURNS * MOE_J
PV0 = 3 + LAYERS * NG * NS
CX0 = 2 + LAYERS * NG * (S // CH)
assert V1_PROJ <= 2 * A1_FIRST and M1_SLOT < SLOTS1 and M_SLOT < SLOTS
assert len(group_items(False)) == V_GROUP and V_LAYER % 2 == 0 and A_LAYER % 2 == 0


def at(items, kind, which):
    return [i for i, (_, k, w) in enumerate(items) if (k, w) == (kind, which)][0]


def m_item(g):
    return V_G0 - 1 if g == 0 else V_G0 + (g - 1) * V_GROUP + at(group_items(False), "M", 0)


def t_item(g, c):
    return V_G0 + g * V_GROUP + at(group_items(g == NG - 1), "T", c)


N_ROUTE = 25


def down_at(j):
    return 2 * j + 2 if j < MOE_J - 1 else 2 * MOE_J - 1


def up_at(j):
    return max(2 * j - 1, 0)


def build(nc, x_d, wa_d, w1_d, w2_d, vc_d, vb_d, wt_d, fb_d, ld_d, da_d, lu_d, ua_d, rot_d, pos_d,
          qkv1_d, wo1_d, gate_d, moe_d, out_d):
    q_scr = nc.dram_tensor("q_scr", [NB, H0, KROWS, S], BF16, kind="Internal").ap()
    k_scr = nc.dram_tensor("k_scr", [NB, H0, HALF, S], BF16, kind="Internal").ap()
    p_scr = nc.dram_tensor("p_scr", [3, HD0, S], BF16, kind="Internal").ap()

    with ExitStack() as ctx:
        def sb(name, shape, dt=F32):
            return ctx.enter_context(nc.sbuf_tensor(name, shape, dt))

        def sem(name):
            return ctx.enter_context(nc.semaphore(name))

        vecb = [ctx.enter_context(nc.psum_tensor(f"vecb{i}", [P, CH], F32)) for i in range(2)]
        actb = [ctx.enter_context(nc.psum_tensor(f"actb{i}", [P, 2, CH], F32)) for i in range(2)]
        ctxb = ctx.enter_context(nc.psum_tensor("ctxb", [P, 2, CH], F32))

        h = sb("h", [P, NT, D])
        res = sb("res", [P, NT, D])
        xn = sb("xn", [P, NT, D])
        xnT = sb("xnT", [P, T])
        vtok = sb("vtok", [P, NT, D])
        att = sb("att", [P, NT, D])
        big = sb("big", [P, 4 * T])
        kst = sb("kst", [P, 3, GH, S], BF16)
        pbuf = sb("pbuf", [P, 3 * GH * CH])
        kp = sb("kp", [P, 3, T], BF16)
        vst = sb("vst", [P, 2, SB_, GH, 32])
        rot = sb("rot", [P, 2, S])
        osb = sb("osb", [P, 2, CH])
        wa = sb("wa", [P, 5, D])
        w1 = sb("w1", [P, FF])
        w2 = sb("w2", [P, NF, D])
        vc = sb("vc", [P, NVC])
        vb = sb("vb", [P, 3, D])
        bu = sb("bu", [P, 2])
        ident = sb("ident", [P, P])
        amask = sb("amask", [P, CH])
        identb = sb("identb", [P, P], BF16)
        bmask = sb("bmask", [P, P], BF16)
        half = sb("half", [P, NT])
        stats = sb("stats", [P, NT, 6])
        mv = sb("mv", [P, NT, 2])
        vare = sb("vare", [P, NT])
        rstd = sb("rstd", [P, NT])
        mxa = sb("mxa", [P, GH, SB_])
        mxb = sb("mxb", [P, GH, SB_ - TPC])
        nm = sb("nm", [GH * SB_, 2, P], BF16)
        rz = sb("rz", [P, TPC, GH])
        lw = sb("lw", [P, 3, D])
        lws = sb("lws", [P, LORA_R + LORA_U + D])
        nm1 = sb("nm1", [NB * SB_, P])
        wt9 = sb("wt9", [P, NT, NE + 1])

        hid = big[:, :].rearrange("p (m t) -> p m t", m=NF)
        qf, rf, rtmp, kf = (hid[:, i, :] for i in range(4))
        qst = big[:, 0:3 * GH * S // 2].bitcast(BF16).rearrange("p (u h t) -> p u h t", u=3, h=GH)
        prob = pbuf[:, :].rearrange("p (u h t) -> p u h t", u=3, h=GH)
        pparts = pbuf[:, :].bitcast(BF16).rearrange("p (x k t) -> p x k t", x=2, k=3)
        parts = {"k": kp[:, :, :], "q": pparts[:, 0], "r": pparts[:, 1]}
        whole = {"k": kf, "q": qf, "r": rf}
        mw = vst[:, :, :, :, :].rearrange("p u a b c -> p (u a b c)")[:, 0:2 * 4 * P].rearrange("p (u d) -> p u d", u=2)
        wT = hid[0:KFULL, 3, :]
        moeb = pbuf[:, 0:6 * CH].rearrange("p (x u t) -> p x u t", x=3, u=2)
        prob1 = pbuf[:, :].rearrange("p (u b t) -> p u b t", u=P1BUF, b=NB)
        osb1 = att[:, :, :].rearrange("p t d -> p (t d)").rearrange("p (c b t) -> p c b t", c=2, b=NB)
        wof = wa[:, :, :].rearrange("p a d -> p (a d)")[:, 0:2 * OUT_W].rearrange("p (u d) -> p u d", u=2)
        vh = [vtok[:, :, :], xn[:, :, :]]
        wr = kst[:, :, :, :].rearrange("p u h t -> p (u h t)").bitcast(F32)[:, 0:14 * NT * NE]\
            .rearrange("p (k t e) -> p k t e", k=14, t=NT)

        names = {}

        def s(name):
            if name not in names:
                names[name] = sem(name)
            return names[name]

        def vec_read(idx):
            return idx + 3

        act_read = vec_read

        def alone(eng, name):
            eng.sem_inc(s(name), 1)

        block = ctx.enter_context(nc.Block())

        UNITS = [(b, w) for b in range(NB) for w in ("k", "q", "r")]
        NU = len(UNITS)
        SCR = NB * 3 * len(TERMS)
        POS_DMAS = 1 + 3 * GH * len(TERMS)

        @block.sync
        def _(sp):
            def load(dst, src, name):
                sp.dma_start(dst, src).then_inc(s(name), 16)

            tok = "(t p) d -> p t d"
            load(h[:, :, :], x_d.rearrange(tok, p=P), "x_in")
            load(res[:, :, :], x_d.rearrange(tok, p=P), "res_in")
            load(kf[0:HD0, 0:S], pos_d, "pos_in")
            load(rot[:, :, :], rot_d, "rot_in")
            load(lws[0:LORA_D, 0:LORA_R], ld_d, "lora_in")
            load(lws[0:LORA_R, LORA_R:LORA_R + LORA_U], lu_d, "lora_in")
            load(lws[0:LORA_U, LORA_R + LORA_U:], ua_d, "lora_in")
            load(lw[0:LORA_D, 0, :], da_d, "lora_in")
            load(w2[:, 0, :], wt_d, "lora_in")
            load(vb[:, 0, :], fb_d.partition_broadcast(P), "lora_in")
            sp.wait_ge(s("pos_part3"), 1)
            load(p_scr.rearrange("k d t -> d k t"), kp[0:HD0, :, 0:S], "pos_out")
            sp.wait_ge(s("pos_out"), 16)
            for t, (_, kpart) in enumerate(TERMS):
                for u in range(3):
                    for r in range(GH):
                        load(kst[t * HD0:(t + 1) * HD0, u, r, :], p_scr[kpart], "pos_in")

            def stack_load(g):
                u, (b, hg) = g % 3, divmod(g, GPB)
                hs = slice(hg * GH, (hg + 1) * GH)
                load(qst[0:KROWS, u], q_scr[b, hs].rearrange("h r t -> r h t"), f"stack_in{u}")
                load(kst[HALF:KROWS, u], k_scr[b, hs].rearrange("h r t -> r h t"), f"stack_in{u}")

            with sp.Fori(0, LAYERS) as l:
                sp.wait_ge(s("vec_read"), V_START + 2 + l * V_LAYER)
                for dst, src in ((vc[:, :], vc_d), (wa[:, :, :], wa_d), (vb[:, :, :], vb_d), (w1[:, :], w1_d),
                                 (w2[:, :, :], w2_d)):
                    load(dst, src[l], "weights_in")
                for n, (b, w) in enumerate(UNITS):
                    col = slice(b * S, (b + 1) * S)
                    for part in range(3):
                        sp.wait_ge(s(("part1", "part2", "part3")[part]), l * NU + n + 1)
                        for t, (qpart, kpart) in enumerate(TERMS):
                            if (kpart if w == "k" else qpart) == part:
                                row = t * HD0 + (HALF if w == "q" else 0)
                                load((k_scr if w == "k" else q_scr)[b, :, row:row + HD0, :],
                                     parts[w][:, part, col], "scr_out")
                sp.wait_ge(s("scr_out"), 16 * SCR * (l + 1))
                for g in range(3):
                    stack_load(g)
                for g in range(NG):
                    sp.wait_ge(s("vec_read"), vec_read(V_START + l * V_LAYER + m_item(g)))
                    for k in range(2):
                        load(qst[KROWS + k:KROWS + k + 1, g % 3].rearrange("p h (i t) -> p (h i) t", t=P),
                             nm[:, k, :], "maxrow_in")
                    if 1 <= g and g + 2 < NG:
                        sp.wait_ge(s("act_full"), l * A_LAYER + A_K + g * A_B)
                        stack_load(g + 2)

            sp.wait_ge(s("vec_read"), vec_read(V_R - 1))
            load(vc[:, 0:NE], gate_d, "gate_in")
            for u in range(2):
                load(mw[:, u, :], moe_d[u], f"moe_in{u}")
            with sp.Fori(1, MOE_TURNS) as i:
                for u in range(2):
                    sp.wait_ge(s("vec_full"), V_MOE + (i - 1) * MOE_V + down_at((u + 1) * NC - 1) + 1)
                    load(mw[:, u, :], moe_d[i * 2 + u], f"moe_in{u}")

            def head_weights(hd, par):
                load(w1[:, par * 3 * HD1:(par + 1) * 3 * HD1], qkv1_d[hd], f"head_in{par}")
                load(wof[0:HD1 + 1, par, :], wo1_d[hd], f"head_in{par}")

            def max_row(hd, par, m_idx):
                sp.wait_ge(s("vec_read"), vec_read(m_idx))
                load(hid[HD1:HD1 + 1, 2 * par, :].rearrange("p (i t) -> p i t", t=P), nm1[:, :], "maxrow1_in")

            for u in range(2):
                head_weights(u, u)
            max_row(0, 0, V_H0 - 1)
            full = head_items(False)
            m_at, o_at = at(full, "M", 0), at(full, "O", (S // CH - 1, len(OUT_SPLIT) - 1))
            with sp.Fori(0, H1 // 2 - 1) as i:
                for u in range(2):
                    base = V_H0 + (2 * i + u) * V1_HEAD
                    max_row(2 * i + u + 1, 1 - u, base + m_at)
                    sp.wait_ge(s("vec_full"), base + o_at + 1)
                    head_weights(2 * i + u + 2, u)
            max_row(H1 - 1, 1, V_H0 + (H1 - 2) * V1_HEAD + m_at)
            sp.wait_ge(s("vec_read"), vec_read(V_H0 + (H1 - 1) * V1_HEAD + len(head_items(True)) - 1))
            load(out_d.rearrange(tok, p=P), res[:, :, :], "out_done")
            sp.wait_ge(s("out_done"), 16)

        @block.gpsimd
        def _(pool):
            pool.memset(ident[:, :], 0.0).then_inc(s("pool_zero"), 1)
            pool.memset(amask[:, :], 0.0).then_inc(s("pool_zero"), 1)
            pool.memset(vst[:, :, :, :, :], 0.0).then_inc(s("pool_zero"), 1)
            pool.memset(half[:, :], -0.5).then_inc(s("half_set"), 1)
            pool.memset(identb[:, :], 0.0).then_inc(s("pool_zero"), 1)
            pool.memset(bmask[:, :], 0.0).then_inc(s("pool_zero"), 1)
            pool.wait_ge(s("pool_zero"), 5)
            pool.affine_select(out=identb[:, :], in_=identb[:, :], compare_op=ALU.not_equal, fill=1.0, base=0,
                               pattern=[[-1, P]], channel_multiplier=1).then_inc(s("ident_set"), 1)
            pool.affine_select(out=bmask[:, :], in_=bmask[:, :], compare_op=ALU.is_ge, fill=NEG, base=0,
                               pattern=[[1, P]], channel_multiplier=-1).then_inc(s("ident_set"), 1)
            pool.affine_select(out=ident[:, :], in_=ident[:, :], compare_op=ALU.not_equal, fill=1.0, base=0,
                               pattern=[[-1, P]], channel_multiplier=1).then_inc(s("ident_set"), 1)
            pool.affine_select(out=amask[:, CH - P:CH], in_=amask[:, CH - P:CH], compare_op=ALU.is_ge, fill=NEG,
                               base=0, pattern=[[-1, P]], channel_multiplier=1).then_inc(s("amask_set"), 1)
            pool.memset(vst[:, :, :, :, HD0:HD0 + 1].rearrange("p u a h o -> p (u a h) o"), 1.0)\
                .then_inc(s("ones_set"), 1)
            pool.wait_ge(s("half_set"), 1)

            def ln_rstd(n, eps):
                pool.wait_ge(s("ln_aggr"), NT * (n + 1))
                alone(pool, "pool_seen")
                pool.tensor_scalar(vare[:, :], mv[:, :, 1], eps, None, ALU.add).then_inc(s("ln_eps"), 1)
                pool.wait_ge(s("ln_eps"), n + 1)
                pool.tensor_tensor(rstd[:, :], vare[:, :], half[:, :], ALU.pow).then_inc(s("ln_rstd"), 1)

            ln_rstd(0, 1e-5)
            pool.wait_ge(s("pos_part1"), 1)
            pool.tensor_tensor(kf[0:HD0, 0:S], kf[0:HD0, 0:S], kp[0:HD0, 0, 0:S],
                               ALU.subtract).then_inc(s("pos_remainder"), 1)
            pool.wait_ge(s("pos_part2"), 1)
            pool.tensor_tensor(kp[0:HD0, 2, 0:S], kf[0:HD0, 0:S], kp[0:HD0, 1, 0:S],
                               ALU.subtract).then_inc(s("pos_part3"), 1)

            with pool.Fori(0, LAYERS) as l:
                ln_rstd(1 + 2 * l, 1e-6)
                for n in range(NU + 1):
                    if n < NU:
                        b, w = UNITS[n]
                        col = slice(b * S, (b + 1) * S)
                        pool.wait_ge(s("part1"), l * NU + n + 1)
                        pool.tensor_tensor(whole[w][:, col], whole[w][:, col], parts[w][:, 0, col],
                                           ALU.subtract).then_inc(s("remainder"), 1)
                    if n:
                        b, w = UNITS[n - 1]
                        col = slice(b * S, (b + 1) * S)
                        pool.wait_ge(s("part2"), l * NU + n)
                        pool.tensor_tensor(parts[w][:, 2, col], whole[w][:, col], parts[w][:, 1, col],
                                           ALU.subtract).then_inc(s("part3"), 1)

                def add_row(which, n_ln):
                    pool.wait_ge(s("ln_xn"), NT * (n_ln + 1))
                    row = vb[:, which:which + 1, :].to_broadcast([P, NT, D])
                    pool.tensor_tensor(h[:, :, :], h[:, :, :], row, ALU.add).then_inc(s("bias_added"), 1)

                def stage_v(g):
                    b, hg = divmod(g, GPB)
                    pool.wait_ge(s("prob_read"), 3 + (l * NG + max(g - 1, 0)) * NS)
                    alone(pool, "pool_seen")
                    src = vtok[:, b * SB_:(b + 1) * SB_, hg * GH * HD0:(hg + 1) * GH * HD0]
                    pool.tensor_copy(vst[:, g % 2, :, :, 0:HD0],
                                     src.rearrange("p t (h d) -> p t h d", h=GH)).then_inc(s("vst_ready"), 1)

                pool.wait_ge(s("vec_read"), vec_read(V_START + l * V_LAYER + V_LN + V_PROJ - 1))
                for g in range(2):
                    stage_v(g)
                pool.wait_ge(s("weights_in"), 80 * (l + 1))
                add_row(VB["bo"], 1 + 2 * l)
                for g in range(2, NG):
                    stage_v(g)
                ln_rstd(2 + 2 * l, 1e-6)
                add_row(VB["b2"], 2 + 2 * l)
            ln_rstd(1 + 2 * LAYERS, 1e-5)

            pool.wait_ge(s("zeros1_set"), 4)
            with pool.Fori(0, H1 // 2) as i:
                for u in range(2):
                    pool.wait_ge(s("act_full"), A_H + (2 * i + u) * NS)
                    alone(pool, "pool_seen")
                    pool.memset(hid[HD1:HD1 + 1, 2 * (1 - u), :], 0.0).then_inc(s("maxrow1_zero"), 1)

        @block.scalar
        def _(act):
            act.sem_inc(s("act_read"), 2)
            act.sem_inc(s("ctx_read"), 2)
            act.wait_ge(s("pos_in"), 16)
            act.activation(kp[0:HD0, 0, 0:S], kf[0:HD0, 0:S], ACT.Copy).then_inc(s("pos_part1"), 1)
            act.wait_ge(s("pos_remainder"), 1)
            act.activation(kp[0:HD0, 1, 0:S], kf[0:HD0, 0:S], ACT.Copy).then_inc(s("pos_part2"), 1)
            act.wait_ge(s("pos_out"), 16)

            with act.Fori(0, LAYERS) as l:
                base = l * A_LAYER
                vbase = V_START + l * V_LAYER
                act.wait_ge(s("weights_in"), 80 * (l + 1))
                for b in range(NB):
                    act.wait_ge(s("act_full"), base + b + 1)
                    act.activation(kf[:, b * S:(b + 1) * S], actb[b % 2][:, :, :].rearrange("p a t -> p (a t)"),
                                   ACT.Identity, bias=vc[:, COL["bk"]:COL["bk"] + 1]).then_inc(s("act_read"), 1)
                for n in range(NU + 1):
                    if n < NU:
                        b, w = UNITS[n]
                        col = slice(b * S, (b + 1) * S)
                        if w == "k":
                            act.wait_ge(s("act_read"), act_read(base + b))
                        else:
                            act.wait_ge(s("vec_read"), vec_read(vbase + V_LN + (b + 1) * NC - 1))
                        act.activation(parts[w][:, 0, col], whole[w][:, col], ACT.Copy).then_inc(s("part1"), 1)
                    if n:
                        b, w = UNITS[n - 1]
                        col = slice(b * S, (b + 1) * S)
                        act.wait_ge(s("remainder"), l * NU + n)
                        act.activation(parts[w][:, 1, col], whole[w][:, col], ACT.Copy).then_inc(s("part2"), 1)

                for g in range(NG):
                    def evacuate(c):
                        act.wait_ge(s("prob_read"), 3 + (l * NG + g) * NS + C_END[c] + 1)
                        if g:
                            act.wait_ge(s("vec_full"), vbase + t_item(g - 1, c) + 1)
                        act.activation(osb[:, c, :], ctxb[:, c, :], ACT.Copy).then_inc(s("ctx_read"), 1)

                    for st, (c, jb, i0, w) in enumerate(STEPS):
                        act.wait_ge(s("prob_read"), (l * NG + g) * NS + st + 1)
                        for pr in range(GH // 2):
                            k = A_K + g * A_B + st * (GH // 2) + pr
                            act.wait_ge(s("act_full"), base + k + 1)
                            act.activation(prob[:, (g * NS + st) % 3, 2 * pr:2 * pr + 2, 0:w],
                                           actb[k % 2][:, :, 0:w], ACT.Exp, scale=SCALE0).then_inc(s("act_read"), 1)
                        if st == C_END[0] + LAG:
                            evacuate(0)
                    evacuate(1)

                for n in range(A_G):
                    cp, m = divmod(n, NF)
                    k = A_K + NG * A_B + n
                    act.wait_ge(s("act_full"), base + k + 1)
                    act.activation(hid[:, m, cp * 2 * CH:(cp + 1) * 2 * CH],
                                   actb[k % 2][:, :, :].rearrange("p a t -> p (a t)"), ACT.Gelu,
                                   bias=vc[:, COL["b1_0"] + m:COL["b1_0"] + m + 1]).then_inc(s("act_read"), 1)

            act.wait_ge(s("route"), 3)
            act.activation(wr[:, 1], wr[:, 1], ACT.Exp).then_inc(s("route_exp"), 1)
            with act.Fori(0, MOE_TURNS) as i:
                for j in range(MOE_J):
                    act.wait_ge(s("act_full"), A_MOE + i * MOE_J + j + 1)
                    act.activation(moeb[:, 0, j % 2, :], actb[j % 2][:, 0, :], ACT.Silu).then_inc(s("silu"), 1)
                    act.activation(moeb[:, 1, j % 2, :], actb[j % 2][:, 1, :], ACT.Copy).then_inc(s("act_read"), 1)

            def head(hd, last):
                items = head_items(last)
                for st, (c, jb, i0, w) in enumerate(STEPS):
                    k = hd * NS + st
                    act.wait_ge(s("act_full"), A_H + k + 1)
                    act.wait_ge(s("prob_read"), PV0 + k - P1BUF + 1)
                    act.activation(prob1[:, st % P1BUF, :, 0:w], actb[st % 2][:, :, 0:w], ACT.Exp,
                                   scale=SCALE1).then_inc(s("act_read"), 1)
                    if st == C_END[0] + LAG1:
                        evacuate1(hd, 0)
                evacuate1(hd, 1)

            def evacuate1(hd, c):
                act.wait_ge(s("prob_read"), PV0 + hd * NS + C_END[c] + 1)
                o_at = at(head_items(False), "O", (c, len(OUT_SPLIT) - 1))
                act.wait_ge(s("vec_full"), V_H0 + (hd - 1) * V1_HEAD + o_at + 1)
                act.activation(osb1[0:HD1 + 1, c, :, :], ctxb[0:HD1 + 1, :, :], ACT.Copy).then_inc(s("ctx_read"), 1)

            with act.Fori(0, H1) as hd:
                head(hd, False)

        @block.tensor
        def _(pe):
            pe.sem_inc(s("prob_read"), 3)
            pe.wait_ge(s("ident_set"), 3)

            def vec_bank(idx, par):
                pe.wait_ge(s("vec_read"), idx + 1)
                return vecb[par % 2]

            def transposes(idx, par, src, c, n_ln):
                pe.wait_ge(s("ln_xn"), NT * n_ln + TPC * (c + 1))
                bank = vec_bank(idx, par)
                for j in range(TPC):
                    mm = pe.transpose(bank[:, j * P:(j + 1) * P], src[:, c * TPC + j, :], ident[:, :])
                mm.then_inc(s("vec_full"), 1)

            def add_mask(scores):
                return pe.matmul(scores, identb[:, :], bmask[:, :], start=False, stop=True)

            for c in range(NC):
                transposes(c, c, h, c, 0)
            pe.wait_ge(s("lora_in"), 96)
            k = NC
            bank = vec_bank(k, k)
            pe.matmul(bank[0:LORA_R, 0:D], lws[0:LORA_D, 0:LORA_R], lw[0:LORA_D, 0, :], start=True,
                      stop=True).then_inc(s("vec_full"), 1)
            bank = vec_bank(k + 1, k + 1)
            pe.wait_ge(s("vec_read"), vec_read(k))
            pe.matmul(bank[0:LORA_U, 0:D], lws[0:LORA_R, LORA_R:LORA_R + LORA_U], lw[0:LORA_R, 1, :], start=True,
                      stop=True).then_inc(s("vec_full"), 1)
            bank = vec_bank(k + 2, k + 2)
            pe.wait_ge(s("vec_read"), vec_read(k + 1))
            pe.matmul(bank[:, 0:D], lw[0:LORA_U, 2, :], lws[0:LORA_U, LORA_R + LORA_U:], start=True,
                      stop=True).then_inc(s("vec_full"), 1)
            pe.wait_ge(s("vec_read"), vec_read(k + 2))
            for c in range(NC):
                idx = k + 3 + c
                bank = vec_bank(idx, idx)
                for j in range(TPC):
                    t = c * TPC + j
                    mm = pe.matmul(bank[:, j * P:(j + 1) * P], xnT[:, t * P:(t + 1) * P], lw[:, 0, :],
                                   start=True, stop=True)
                mm.then_inc(s("vec_full"), 1)
            pe.wait_ge(s("pos_in"), 16 * POS_DMAS)
            pe.wait_ge(s("ones_set"), 2)

            with pe.Fori(0, LAYERS) as l:
                vbase = V_START + l * V_LAYER
                abase = l * A_LAYER

                def vbank(k):
                    return vec_bank(vbase + k, V_START + k)

                def dense(k, w, c):
                    bank = vbank(k)
                    pe.matmul(bank[:, :], w, xnT[:, c * CH:(c + 1) * CH], start=True,
                              stop=True).then_inc(s("vec_full"), 1)

                for c in range(NC):
                    transposes(vbase + c, V_START + c, xn, c, 1 + 2 * l)
                pe.wait_ge(s("weights_in"), 80 * (l + 1))
                for b in range(NB):
                    pe.wait_ge(s("vec_read"), vec_read(vbase + (b + 1) * NC // 2 - 1))
                    pe.wait_ge(s("act_read"), abase + b + 1)
                    for x in range(2):
                        c = b * 2 + x
                        mm = pe.matmul(actb[b % 2][:, x, :], wa[:, WK, :], xnT[:, c * CH:(c + 1) * CH],
                                       start=True, stop=True)
                    mm.then_inc(s("act_full"), 1)
                    for x in range(2):
                        c = b * 2 + x
                        dense(V_LN + 2 * c, wa[:, WQ, :], c)
                        dense(V_LN + 2 * c + 1, wa[:, WQS, :], c)
                for c in range(NC):
                    bank = vbank(V_LN + 2 * NC + c)
                    for j in range(TPC):
                        t = c * TPC + j
                        mm = pe.matmul(bank[:, j * P:(j + 1) * P], xnT[:, t * P:(t + 1) * P], wa[:, WV, :],
                                       start=True, stop=True)
                    mm.then_inc(s("vec_full"), 1)

                def pass_a(g, k, i):
                    r, ib, k0, w, _ = A_LIST[i]
                    if i == 0:
                        pe.wait_ge(s(f"stack_in{g % 3}"), 32 * (l * USES[g % 3] + g // 3 + 1))
                    bank = vbank(k)
                    pe.matmul(bank[:, 0:w], qst[0:KROWS, g % 3, r, ib * P:(ib + 1) * P],
                              kst[0:KROWS, g % 3, r, k0:k0 + w], start=True, stop=True).then_inc(s("vec_full"), 1)

                def maxima(g, k):
                    bank = vbank(k)
                    pe.wait_ge(s("max_ready"), l * NG + g + 1)
                    pe.transpose(bank[0:GH * SB_, 0:P], mxa[:, :, :].rearrange("p h i -> p (h i)"),
                                 ident[:, :]).then_inc(s("vec_full"), 1)

                def pass_b(g, st, pr):
                    c, jb, i0, w = STEPS[st]
                    if st == 0 and pr == 0:
                        pe.wait_ge(s("maxrow_in"), 32 * (l * NG + g + 1))
                    if True:
                        k = A_K + g * A_B + st * (GH // 2) + pr
                        pe.wait_ge(s("act_read"), abase + k + 1)
                        for x in range(2):
                            r = 2 * pr + x
                            mm = pe.matmul(actb[k % 2][:, x, 0:w], kst[0:KMAX, g % 3, r, jb * P:(jb + 1) * P],
                                           qst[0:KMAX, g % 3, r, i0:i0 + w], start=True, stop=not DIAG[st])
                            if DIAG[st]:
                                mm = add_mask(actb[k % 2][:, x, 0:P])
                        mm.then_inc(s("act_full"), 1)

                def pv(g, st):
                    c, jb, i0, w = STEPS[st]
                    if st == 0:
                        pe.wait_ge(s("vst_ready"), l * NG + g + 1)
                    if jb == 0:
                        pe.wait_ge(s("ctx_read"), (l * NG + g) * (S // CH) + c + 1)
                    pe.wait_ge(s("act_read"), act_read(abase + A_K + g * A_B + 2 * st + 1))
                    for r in range(GH):
                        mm = pe.matmul(ctxb[32 * r:32 * r + 32, c, i0 - c * CH:CH], vst[:, g % 2, jb, r, :],
                                       prob[:, (g * NS + st) % 3, r, 0:w], start=(jb == 0), stop=(st == C_END[c]))
                    mm.then_inc(s("prob_read"), 1)

                def turn(g, k, c):
                    bank = vbank(k)
                    pe.wait_ge(s("ctx_read"), 2 + (l * NG + g) * (S // CH) + c + 1)
                    for j in range(TPC):
                        mm = pe.transpose(bank[:, j * P:(j + 1) * P], osb[:, c, j * P:(j + 1) * P], ident[:, :])
                    mm.then_inc(s("vec_full"), 1)

                for i in range(NA):
                    pass_a(0, V_LN + V_PROJ + i, i)
                maxima(0, V_LN + V_PROJ + NA)
                for g in range(NG):
                    items = group_items(g == NG - 1)
                    for slot in range(SLOTS):
                        vec = [(k, kind, x) for k, (sl, kind, x) in enumerate(items) if sl == slot]

                        def vec_item(n):
                            for k, kind, x in vec[n:n + 1]:
                                k += V_G0 + g * V_GROUP
                                if kind == "A":
                                    pass_a(g + 1, k, x)
                                if kind == "M":
                                    maxima(g + 1, k)
                                if kind == "T":
                                    turn(g, k, x)

                        last_turn = bool(vec) and vec[-1][1:] == ("T", 1)
                        for pr in range(GH // 2):
                            if slot < NS:
                                pass_b(g, slot, pr)
                            vec_item(pr) if not (last_turn and pr == len(vec) - 1) else None
                        early = min(GH // 2, len(vec) - last_turn)
                        if not last_turn:
                            vec_item(2)
                        if slot >= LAG:
                            pv(g, slot - LAG)
                        for n in range(early + (not last_turn), len(vec)):
                            vec_item(n)

                for c in range(NC):
                    k = V_POST + c
                    bank = vbank(k)
                    if c == 0:
                        pe.wait_ge(s("vec_read"), vec_read(vbase + V_POST - 1))
                    for j in range(TPC):
                        mm = pe.transpose(bank[:, j * P:(j + 1) * P], att[:, c * TPC + j, :], ident[:, :])
                    mm.then_inc(s("vec_full"), 1)
                for c in range(NC):
                    k = V_POST + NC + c
                    bank = vbank(k)
                    pe.wait_ge(s("vec_read"), vec_read(vbase + V_POST + c))
                    for j in range(TPC):
                        t = c * TPC + j
                        mm = pe.matmul(bank[:, j * P:(j + 1) * P], xnT[:, t * P:(t + 1) * P], wa[:, WO, :],
                                       start=True, stop=True)
                    mm.then_inc(s("vec_full"), 1)
                for c in range(NC):
                    k = V_POST + 2 * NC + c
                    transposes(vbase + k, V_START + k, xn, c, 2 + 2 * l)
                for cp in range(2):
                    pe.wait_ge(s("vec_read"), vec_read(vbase + V_POST + 2 * NC + 2 * cp + 1))
                    for m in range(NF):
                        k = A_K + NG * A_B + cp * NF + m
                        pe.wait_ge(s("act_read"), abase + k + 1)
                        for x in range(2):
                            c = 2 * cp + x
                            mm = pe.matmul(actb[k % 2][:, x, :], w1[:, m * P:(m + 1) * P],
                                           xnT[:, c * CH:(c + 1) * CH], start=True, stop=True)
                        mm.then_inc(s("act_full"), 1)
                for c in range(NC):
                    bank = vbank(V_POST + 3 * NC + c)
                    pe.wait_ge(s("act_read"), act_read(abase + A_K + NG * A_B + (c // 2) * NF + NF - 1))
                    for j in range(TPC):
                        t = c * TPC + j
                        for m in range(NF):
                            mm = pe.matmul(bank[:, j * P:(j + 1) * P], hid[:, m, t * P:(t + 1) * P], w2[:, m, :],
                                           start=(m == 0), stop=(m == NF - 1))
                    mm.then_inc(s("vec_full"), 1)

            for c in range(NC):
                transposes(V_R + c, V_R + c, xn, c, 1 + 2 * LAYERS)
            pe.wait_ge(s("vec_read"), vec_read(V_R + NC - 1))
            pe.wait_ge(s("gate_in"), 16)
            bank = vec_bank(V_R + NC, V_R + NC)
            for t in range(NT):
                mm = pe.matmul(bank[:, t * NE:(t + 1) * NE], xnT[:, t * P:(t + 1) * P], vc[:, 0:NE],
                               start=True, stop=True)
            mm.then_inc(s("vec_full"), 1)
            pe.wait_ge(s("route"), N_ROUTE)
            for c in range(NC):
                idx = V_R + NC + 1 + c
                bank = vec_bank(idx, idx)
                for j in range(TPC):
                    mm = pe.transpose(bank[0:NE + 1, j * P:(j + 1) * P], wt9[:, c * TPC + j, :], ident[:, :])
                mm.then_inc(s("vec_full"), 1)
            pe.wait_ge(s("vec_read"), vec_read(V_MOE - 1))

            with pe.Fori(0, MOE_TURNS) as i:
                def down(j):
                    u, c = divmod(j, NC)
                    k = down_at(j)
                    bank = vec_bank(V_MOE + i * MOE_V + k, V_MOE + k)
                    pe.wait_ge(s("vec_read"), vec_read(V_MOE + i * MOE_V + up_at(j)))
                    for x in range(TPC):
                        mm = pe.matmul(bank[:, x * P:(x + 1) * P], moeb[:, 2, j % 2, x * P:(x + 1) * P],
                                       mw[:, u, 2 * P:3 * P], start=True, stop=True)
                    mm.then_inc(s("vec_full"), 1)

                for j in range(MOE_J):
                    u, c = divmod(j, NC)
                    if c == 0:
                        pe.wait_ge(s(f"moe_in{u}"), 16 * (i + 1))
                    tokens = xnT[:, c * CH:(c + 1) * CH]
                    pe.wait_ge(s("act_read"), A_MOE + i * MOE_J + j + 1)
                    pe.matmul(actb[j % 2][:, 0, :], mw[:, u, 0:P], tokens, start=True, stop=True)
                    pe.matmul(actb[j % 2][:, 1, :], mw[0:KFULL, u, 3 * P:4 * P], wT[:, c * CH:(c + 1) * CH],
                              start=True, stop=True).then_inc(s("act_full"), 1)
                    k = up_at(j)
                    bank = vec_bank(V_MOE + i * MOE_V + k, V_MOE + k)
                    pe.matmul(bank[:, :], mw[:, u, P:2 * P], tokens, start=True, stop=True)\
                        .then_inc(s("vec_full"), 1)
                    if j:
                        down(j - 1)
                down(MOE_J - 1)

            def project(idx, par_v, par, hd, n):
                wt = w1[:, par * 3 * HD1:(par + 1) * 3 * HD1]
                if n == 0:
                    pe.wait_ge(s(f"head_in{par}"), 32 * (hd_turn(hd) + 1))
                bank = vec_bank(idx, par_v)
                if n < NC:
                    mm = pe.matmul(bank[:, :], wt[:, 0:2 * HD1], xnT[:, n * CH:(n + 1) * CH], start=True, stop=True)
                else:
                    for j in range(V_TILES):
                        t = (n - NC) * V_TILES + j
                        mm = pe.matmul(bank[:, j * HD1:(j + 1) * HD1], xnT[:, t * P:(t + 1) * P],
                                       wt[:, 2 * HD1:3 * HD1], start=True, stop=True)
                mm.then_inc(s("vec_full"), 1)

            def hd_turn(hd):
                return hd

            def pass_a1(idx, par_v, par, i, proj_done, zeroed):
                b, ib, k0, w, _ = A1_LIST[i]
                bank = vec_bank(idx, par_v)
                if i == 0:
                    pe.wait_ge(s("vec_read"), proj_done)
                    if zeroed is not None:
                        pe.wait_ge(s("maxrow1_zero"), zeroed)
                pe.matmul(bank[:, 0:w], hid[0:KFULL, 2 * par, b * S + ib * P:b * S + (ib + 1) * P],
                          hid[0:KFULL, 2 * par + 1, b * S + k0:b * S + k0 + w], start=True,
                          stop=True).then_inc(s("vec_full"), 1)

            def maxima1(idx, par_v, hd):
                bank = vec_bank(idx, par_v)
                pe.wait_ge(s("max1_ready"), hd + 1)
                pe.transpose(bank[0:NB * SB_, 0:P], mxa[:, 0:2, :].rearrange("p b i -> p (b i)"),
                             ident[:, :]).then_inc(s("vec_full"), 1)

            pe.wait_ge(s("ones1_set"), 3)
            for n in range(V1_PROJ):
                project(V_H + n, V_H + n, 0, 0, n)
            for i in range(NA1):
                k = V_H + V1_PROJ + i
                pass_a1(k, k, 0, i, vec_read(V_H + V1_PROJ - 1), None)
            maxima1(V_H0 - 1, V_H0 - 1, 0)

            def head(hd, turn_, par, last):
                base, items = V_H0 + hd * V1_HEAD, head_items(last)
                pbase = V_H0 + par * V1_HEAD
                for slot in range(SLOTS1):
                    if slot < NS:
                        c, jb, i0, w = STEPS[slot]
                        if slot == 0:
                            pe.wait_ge(s("maxrow1_in"), 16 * (hd + 1))
                        pe.wait_ge(s("act_read"), A_H + hd * NS + slot + 1)
                        for b in range(NB):
                            mm = pe.matmul(actb[slot % 2][:, b, 0:w],
                                           hid[0:KFULL, 2 * par + 1, b * S + jb * P:b * S + (jb + 1) * P],
                                           hid[0:KFULL, 2 * par, b * S + i0:b * S + i0 + w],
                                           start=True, stop=not DIAG[slot])
                            if DIAG[slot]:
                                mm = add_mask(actb[slot % 2][:, b, 0:P])
                        mm.then_inc(s("act_full"), 1)
                    late = []
                    for k, (sl, kind, x) in enumerate(items):
                        if sl != slot:
                            continue
                        if kind == "P":
                            project(base + k, pbase + k, 1 - par, turn_ + par, x)
                        if kind == "A":
                            pass_a1(base + k, pbase + k, 1 - par, x, vec_read(base + V1_PROJ - 1), hd + 1)
                        if kind == "M":
                            maxima1(base + k, pbase + k, hd + 1)
                        if kind == "O":
                            if x[0] == 0:
                                project_out(base + k, pbase + k, hd, par, x)
                            else:
                                late.append((k, x))
                    if slot >= LAG1:
                        st = slot - LAG1
                        c, jb, i0, w = STEPS[st]
                        if jb == 0:
                            pe.wait_ge(s("ctx_read"), CX0 + hd * 2 + c)
                        pe.wait_ge(s("act_read"), act_read(A_H + hd * NS + st))
                        for b in range(NB):
                            mm = pe.matmul(ctxb[0:HD1 + 1, b, i0 - c * CH:CH], vh[par][:, b * SB_ + jb, 0:HD1 + 1],
                                           prob1[:, st % P1BUF, b, 0:w], start=(jb == 0), stop=(st == C_END[c]))
                        mm.then_inc(s("prob_read"), 1)
                    for k, x in late:
                        project_out(base + k, pbase + k, hd, par, x)

            def project_out(idx, par_v, hd, par, x):
                c, part = x
                bank = vec_bank(idx, par_v)
                pe.wait_ge(s("ctx_read"), CX0 + hd * 2 + c + 1)
                for j, n in enumerate(OUT_SPLIT[part]):
                    b, ti = divmod(n, TPC)
                    mm = pe.matmul(bank[:, j * OUT_W:(j + 1) * OUT_W], osb1[0:HD1 + 1, c, b, ti * P:(ti + 1) * P],
                                   wof[0:HD1 + 1, par, :], start=True, stop=True)
                mm.then_inc(s("vec_full"), 1)

            with pe.Fori(0, H1 // 2 - 1) as i:
                for u in range(2):
                    head(2 * i + u, i, u, False)
            for u in range(2):
                head(H1 - 2 + u, H1 // 2 - 1, u, u == 1)

        @block.vector
        def _(dve):
            dve.sem_inc(s("vec_read"), 2)
            dve.memset(kst[KROWS:KMAX, :, :, :].rearrange("p u h t -> p (u h t)"), 1.0).then_inc(s("ones_set"), 1)

            def full(idx):
                dve.wait_ge(s("vec_full"), idx + 1)

            def own(idx):
                dve.wait_ge(s("vec_read"), idx + 2)

            def layer_norm(n, src, dst):
                if not isinstance(n, int) or n:
                    dve.wait_ge(s("ln_xn"), NT * n)
                for t in range(NT):
                    dve.bn_stats(stats[:, t, :], src[:, t, :]).then_inc(s("ln_stat"), 1)
                dve.wait_ge(s("ln_stat"), NT * (n + 1))
                alone(dve, "dve_seen")
                for t in range(NT):
                    dve.bn_aggr(mv[:, t, :], stats[:, t, :]).then_inc(s("ln_aggr"), 1)
                dve.wait_ge(s("ln_rstd"), n + 1)
                for t in range(NT):
                    dve.tensor_scalar(dst[:, t, :], src[:, t, :], mv[:, t, 0:1], rstd[:, t:t + 1],
                                      ALU.subtract, ALU.mult).then_inc(s("ln_xn"), 1)

            dve.wait_ge(s("x_in"), 16)
            layer_norm(0, h, h)
            for c in range(NC):
                full(c)
                dve.tensor_copy(xnT[:, c * CH:(c + 1) * CH], vecb[c % 2][:, :]).then_inc(s("vec_read"), 1)
            k = NC
            full(k)
            dve.tensor_copy(lw[0:LORA_R, 1, :], vecb[k % 2][0:LORA_R, 0:D]).then_inc(s("vec_read"), 1)
            full(k + 1)
            dve.tensor_copy(lw[0:LORA_U, 2, :], vecb[(k + 1) % 2][0:LORA_U, 0:D]).then_inc(s("vec_read"), 1)
            full(k + 2)
            dve.wait_ge(s("lora_in"), 96)
            dve.tensor_tensor(lw[:, 0, :], vecb[k % 2][:, 0:D], w2[:, 0, :], ALU.add).then_inc(s("vec_read"), 1)
            dve.wait_ge(s("res_in"), 16)
            dve.tensor_tensor(res[:, :, :], res[:, :, :], vb[:, 0:1, :].to_broadcast([P, NT, D]),
                              ALU.add).then_inc(s("res_bias"), 1)
            dve.wait_ge(s("res_bias"), 1)
            for c in range(NC):
                idx = k + 3 + c
                full(idx)
                part = res[:, c * TPC:(c + 1) * TPC, :]
                dve.tensor_tensor(part, vecb[idx % 2][:, :].rearrange("p (t d) -> p t d", t=TPC), part,
                                  ALU.add).then_inc(s("vec_read"), 1)
            dve.wait_ge(s("rot_in"), 16)
            dve.wait_ge(s("amask_set"), 1)

            def row_max(bank, out, w, diagonal, last):
                if diagonal:
                    alone(dve, "dve_seen")
                    return dve.tensor_tensor_reduce(bank[:, 0:w], bank[:, 0:w], amask[:, CH - w:CH], 1.0, NEG,
                                                    ALU.add, ALU.max, out)
                return dve.tensor_reduce(out, bank[:, 0:w], AX_X, ALU.max)

            with dve.Fori(0, LAYERS) as l:
                vbase = V_START + l * V_LAYER

                def bank_of(k):
                    return vecb[(V_START + k) % 2]

                def affine(k, c, w, b):
                    full(vbase + k)
                    dve.tensor_scalar(xnT[:, c * CH:(c + 1) * CH], bank_of(k)[:, :], vc[:, COL[w]:COL[w] + 1],
                                      vc[:, COL[b]:COL[b] + 1], ALU.mult, ALU.add).then_inc(s("vec_read"), 1)

                own(vbase)
                layer_norm(1 + 2 * l, h, xn)
                dve.wait_ge(s("weights_in"), 80 * (l + 1))
                for j, (x, y) in enumerate((("bq", "u"), ("bqs", "us"))):
                    dve.tensor_tensor(bu[:, j:j + 1], vc[:, COL[x]:COL[x] + 1], vc[:, COL[y]:COL[y] + 1],
                                      ALU.add).then_inc(s("bu_ready"), 1)
                dve.wait_ge(s("bu_ready"), 2 * (l + 1))
                for c in range(NC):
                    affine(c, c, "ln1w", "ln1b")
                for c in range(NC):
                    k = V_LN + 2 * c
                    col = slice(c * CH, (c + 1) * CH)
                    pos = slice(c * CH % S, c * CH % S + CH)
                    full(vbase + k)
                    dve.tensor_scalar(qf[:, col], bank_of(k)[:, :], vc[:, COL["bq"]:COL["bq"] + 1], None, ALU.add)
                    dve.scalar_tensor_tensor(out=rf[:, col], in0=bank_of(k)[:, :], scalar=bu[:, 0:1],
                                             in1=rot[:, 0, pos], op0=ALU.add, op1=ALU.mult)\
                        .then_inc(s("vec_read"), 1)
                    full(vbase + k + 1)
                    dve.scalar_tensor_tensor(out=rtmp[:, col], in0=bank_of(k + 1)[:, :], scalar=bu[:, 1:2],
                                             in1=rot[:, 1, pos], op0=ALU.add, op1=ALU.mult)\
                        .then_inc(s("rot_half"), 1)
                    dve.wait_ge(s("rot_half"), l * NC + c + 1)
                    dve.tensor_tensor(rf[:, col], rf[:, col], rtmp[:, col], ALU.add).then_inc(s("vec_read"), 1)
                for c in range(NC):
                    k = V_LN + 2 * NC + c
                    full(vbase + k)
                    dve.tensor_tensor(vtok[:, c * TPC:(c + 1) * TPC, :],
                                      bank_of(k)[:, :].rearrange("p (t d) -> p t d", t=TPC),
                                      vb[:, VB["bv"]:VB["bv"] + 1, :].to_broadcast([P, TPC, D]),
                                      ALU.add).then_inc(s("vec_read"), 1)

                def maximum(k, i):
                    r, ib, k0, w, diagonal = A_LIST[i]
                    full(vbase + k)
                    out = mxa[:, r, ib:ib + 1] if diagonal else mxb[:, r, ib - TPC:ib - TPC + 1]
                    row_max(bank_of(k), out, w, diagonal, False).then_inc(s("vec_read"), 1)

                def combine(g, k):
                    own(vbase + k)
                    dve.tensor_tensor(mxa[:, :, TPC:SB_], mxa[:, :, TPC:SB_], mxb[:, :, :],
                                      ALU.max).then_inc(s("max_ready"), 1)

                def negate(g, k):
                    full(vbase + k)
                    if g:
                        dve.wait_ge(s("maxrow_in"), 32 * (l * NG + g))
                    rows = bank_of(k)[0:GH * SB_, 0:P]
                    dve.tensor_scalar(nm[:, 0, :], rows, -1.0, None, ALU.mult).then_inc(s("nm_high"), 1)
                    dve.wait_ge(s("nm_high"), l * NG + g + 1)
                    dve.scalar_tensor_tensor(out=nm[:, 1, :], in0=rows, scalar=-1.0, in1=nm[:, 0, :],
                                             op0=ALU.mult, op1=ALU.subtract).then_inc(s("vec_read"), 1)

                def context(g, k, c):
                    full(vbase + k)
                    b, hg = divmod(g, GPB)
                    t = b * SB_ + c * TPC
                    v = bank_of(k)[:, :].rearrange("p (t h d) -> p t h d", t=TPC, h=GH)
                    own(vbase + k)
                    dve.reciprocal(rz[:, :, :], v[:, :, :, HD0]).then_inc(s("rz_ready"), 1)
                    dve.wait_ge(s("rz_ready"), (l * NG + g) * 2 + c + 1)
                    dve.tensor_tensor(
                        att[:, t:t + TPC, hg * GH * HD0:(hg + 1) * GH * HD0].rearrange("p t (h d) -> p t h d", h=GH),
                        v[:, :, :, 0:HD0], rz[:, :, :].unsqueeze(3).to_broadcast([P, TPC, GH, HD0]),
                        ALU.mult).then_inc(s("vec_read"), 1)

                for i in range(NA):
                    maximum(V_LN + V_PROJ + i, i)
                combine(0, V_LN + V_PROJ + NA)
                negate(0, V_LN + V_PROJ + NA)
                for g in range(NG):
                    for k, (_, kind, x) in enumerate(group_items(g == NG - 1)):
                        k += V_G0 + g * V_GROUP
                        if kind == "A":
                            maximum(k, x)
                        if kind == "M":
                            combine(g + 1, k)
                            negate(g + 1, k)
                        if kind == "T":
                            context(g, k, x)

                for c in range(NC):
                    full(vbase + V_POST + c)
                    dve.tensor_copy(xnT[:, c * CH:(c + 1) * CH], bank_of(V_POST + c)[:, :])\
                        .then_inc(s("vec_read"), 1)

                def add_to_h(k, c):
                    full(vbase + k)
                    part = h[:, c * TPC:(c + 1) * TPC, :]
                    dve.tensor_tensor(part, bank_of(k)[:, :].rearrange("p (t d) -> p t d", t=TPC), part,
                                      ALU.add).then_inc(s("vec_read"), 1)

                dve.wait_ge(s("bias_added"), 2 * l + 1)
                for c in range(NC):
                    add_to_h(V_POST + NC + c, c)
                own(vbase + V_POST + 2 * NC)
                layer_norm(2 + 2 * l, h, xn)
                for c in range(NC):
                    affine(V_POST + 2 * NC + c, c, "ln2w", "ln2b")
                dve.wait_ge(s("bias_added"), 2 * l + 2)
                for c in range(NC):
                    add_to_h(V_POST + 3 * NC + c, c)

            own(V_R)
            dve.tensor_tensor(res[:, :, :], res[:, :, :], h[:, :, :], ALU.add).then_inc(s("res_ready"), 1)
            dve.wait_ge(s("res_ready"), 1)
            layer_norm(1 + 2 * LAYERS, res, xn)
            for c in range(NC):
                full(V_R + c)
                dve.tensor_copy(xnT[:, c * CH:(c + 1) * CH], vecb[(V_R + c) % 2][:, :]).then_inc(s("vec_read"), 1)

            n_route = [0]

            def route(ins):
                n_route[0] += 1
                ins.then_inc(s("route"), 1)
                dve.wait_ge(s("route"), n_route[0])

            idx = V_R + NC
            full(idx)
            lg, e, e2, rank, key, sel1, sel2 = (wr[:, i] for i in range(7))

            def one(i):
                return wr[:, 7 + i // NE, :, i % NE]

            def wide(x):
                return x.unsqueeze(2).to_broadcast([P, NT, NE])

            mx, sm, rs, m1, km, m2, ds, rd = (one(i) for i in range(8))
            dve.tensor_copy(lg, vecb[idx % 2][:, 0:NT * NE].rearrange("p (t e) -> p t e", e=NE))\
                .then_inc(s("vec_read"), 1)
            own(idx + 1)
            for x in range(NE):
                ins = dve.memset(rank[:, :, x:x + 1], float(NE - x))
            route(ins)
            route(dve.tensor_reduce(mx, lg, AX_X, ALU.max))
            route(dve.tensor_tensor(e, lg, wide(mx), ALU.subtract))
            dve.wait_ge(s("route_exp"), 1)
            route(dve.tensor_reduce(sm, e, AX_X, ALU.add))
            route(dve.reciprocal(rs, sm))
            route(dve.tensor_tensor(e, e, wide(rs), ALU.mult))
            route(dve.tensor_reduce(m1, e, AX_X, ALU.max))

            def first_of(sel, vals, mval):
                route(dve.tensor_tensor(sel, vals, wide(mval), ALU.is_equal))
                route(dve.tensor_tensor(key, sel, rank, ALU.mult))
                route(dve.tensor_reduce(km, key, AX_X, ALU.max))
                route(dve.tensor_tensor(sel, key, wide(km), ALU.is_equal))

            first_of(sel1, e, m1)
            route(dve.scalar_tensor_tensor(out=e2, in0=sel1, scalar=-2.0, in1=e, op0=ALU.mult, op1=ALU.add))
            route(dve.tensor_reduce(m2, e2, AX_X, ALU.max))
            first_of(sel2, e2, m2)
            route(dve.tensor_tensor(ds, m1, m2, ALU.add))
            route(dve.tensor_scalar(ds, ds, 1e-20, None, ALU.add))
            route(dve.reciprocal(rd, ds))
            route(dve.tensor_tensor(sel1, sel1, sel2, ALU.add))
            route(dve.tensor_tensor(e, e, wide(rd), ALU.mult))
            route(dve.tensor_tensor(wt9[:, :, 0:NE], e, sel1, ALU.mult))
            route(dve.memset(wt9[:, :, NE:NE + 1], 1.0))
            route(dve.memset(wT, 0.0))
            assert n_route[0] == N_ROUTE, n_route[0]
            for c in range(NC):
                idx = V_R + NC + 1 + c
                full(idx)
                dve.tensor_copy(wT[0:NE + 1, c * CH:(c + 1) * CH], vecb[idx % 2][0:NE + 1, :]).then_inc(s("vec_read"), 1)

            with dve.Fori(0, MOE_TURNS) as i:
                def add_down(j):
                    c = j % NC
                    k = down_at(j)
                    full(V_MOE + i * MOE_V + k)
                    part = res[:, c * TPC:(c + 1) * TPC, :]
                    own(V_MOE + i * MOE_V + k - 1)
                    dve.tensor_tensor(part, vecb[(V_MOE + k) % 2][:, :].rearrange("p (t d) -> p t d", t=TPC), part,
                                      ALU.add).then_inc(s("vec_read"), 1)

                for j in range(MOE_J):
                    k = up_at(j)
                    full(V_MOE + i * MOE_V + k)
                    dve.wait_ge(s("act_read"), act_read(A_MOE + i * MOE_J + j))
                    hb = moeb[:, 2, j % 2, :]
                    dve.tensor_tensor(hb, moeb[:, 0, j % 2, :], vecb[(V_MOE + k) % 2][:, :],
                                      ALU.mult).then_inc(s("moe_hidden"), 1)
                    dve.wait_ge(s("moe_hidden"), i * MOE_J + j + 1)
                    dve.tensor_tensor(hb, hb, moeb[:, 1, j % 2, :], ALU.mult).then_inc(s("vec_read"), 1)
                    if j:
                        add_down(j - 1)
                add_down(MOE_J - 1)

            own(V_H)
            for par in range(2):
                dve.memset(vh[par][:, :, HD1:HD1 + 1], 1.0).then_inc(s("ones1_set"), 1)
            for par in range(4):
                dve.memset(hid[HD1:KFULL, par, :], 0.0).then_inc(s("zeros1_set"), 1)
            dve.wait_ge(s("zeros1_set"), 4)
            dve.memset(hid[HD1:HD1 + 1, 1:4:2, :], 1.0).then_inc(s("ones1_set"), 1)

            def project(idx, par_v, par, n):
                full(idx)
                bank = vecb[par_v % 2]
                if n < NC:
                    col = slice(n * CH, (n + 1) * CH)
                    dve.tensor_copy(hid[0:HD1, 2 * par, col], bank[0:HD1, :])
                    dve.tensor_copy(hid[0:HD1, 2 * par + 1, col], bank[HD1:2 * HD1, :]).then_inc(s("vec_read"), 1)
                else:
                    t = (n - NC) * V_TILES
                    dve.tensor_copy(vh[par][:, t:t + V_TILES, 0:HD1],
                                    bank[:, :].rearrange("p (t d) -> p t d", d=HD1)).then_inc(s("vec_read"), 1)

            def maximum1(idx, par_v, i):
                b, ib, k0, w, diagonal = A1_LIST[i]
                full(idx)
                out = mxa[:, b, ib:ib + 1] if diagonal else mxb[:, b, ib - TPC:ib - TPC + 1]
                row_max(vecb[par_v % 2], out, w, diagonal, False).then_inc(s("vec_read"), 1)

            def negate1(idx, par_v, hd, first):
                own(idx)
                dve.tensor_tensor(mxa[:, 0:NB, TPC:SB_], mxa[:, 0:NB, TPC:SB_], mxb[:, 0:NB, :],
                                  ALU.max).then_inc(s("max1_ready"), 1)
                full(idx)
                if not first:
                    dve.wait_ge(s("maxrow1_in"), 16 * hd)
                dve.tensor_scalar(nm1[:, :], vecb[par_v % 2][0:NB * SB_, 0:P], -1.0, None,
                                  ALU.mult).then_inc(s("vec_read"), 1)

            def output(idx, par_v, hd, x):
                c, part = x
                tiles = OUT_SPLIT[part]
                full(idx)
                bank = vecb[par_v % 2][:, 0:len(tiles) * OUT_W].rearrange("p (t d) -> p t d", d=OUT_W)
                own(idx)
                dve.reciprocal(rz[:, 0:len(tiles), 0], bank[:, :, D]).then_inc(s("rz1_ready"), 1)
                dve.wait_ge(s("rz1_ready"), hd * 2 * len(OUT_SPLIT) + c * len(OUT_SPLIT) + part + 1)
                for j, n in enumerate(tiles):
                    b, ti = divmod(n, TPC)
                    dst = res[:, b * SB_ + c * TPC + ti, :]
                    ins = dve.scalar_tensor_tensor(out=dst, in0=bank[:, j, 0:D], scalar=rz[:, j, 0:1], in1=dst,
                                                   op0=ALU.mult, op1=ALU.add)
                ins.then_inc(s("vec_read"), 1)

            for n in range(V1_PROJ):
                project(V_H + n, V_H + n, 0, n)
            for i in range(NA1):
                k = V_H + V1_PROJ + i
                maximum1(k, k, i)
            negate1(V_H0 - 1, V_H0 - 1, 0, True)

            def head(hd, par, last):
                base = V_H0 + hd * V1_HEAD
                pbase = V_H0 + par * V1_HEAD
                for k, (_, kind, x) in enumerate(head_items(last)):
                    if kind == "P":
                        project(base + k, pbase + k, 1 - par, x)
                    if kind == "A":
                        maximum1(base + k, pbase + k, x)
                    if kind == "M":
                        negate1(base + k, pbase + k, hd + 1, False)
                    if kind == "O":
                        output(base + k, pbase + k, hd, x)

            with dve.Fori(0, H1 // 2 - 1) as i:
                for u in range(2):
                    head(2 * i + u, u, False)
            for u in range(2):
                head(H1 - 2 + u, u, u == 1)


def _rotations():
    m = HD0 // 2
    inv = (1.0 / 10000.0 ** (np.arange(0, HD0, 2, dtype=np.float32) / np.float32(HD0))).astype(np.float32)
    angle = inv.astype(np.float64)[:, None] * np.arange(S)[None, :]
    sin, cos = np.sin(angle), np.cos(angle)
    queries = np.stack([np.concatenate([sin, sin]), np.concatenate([cos, -cos])], 1)
    queries = np.tile(queries, (P // HD0, 1, 1))
    assert m * 2 == HD0
    return queries.astype(np.float32), np.concatenate([cos, sin]).astype(np.float32)


def kernel(**inputs):
    import concourse.bacc as bacc
    from concourse.bass_utils import run_bass_kernel_spmd

    a = {k: np.asarray(v) for k, v in inputs.items()}
    swap = np.arange(D).reshape(H0, 2, HD0 // 2)[:, ::-1].reshape(-1)

    def turned(name):
        return np.transpose(a["L0_attn_" + name], (0, 2, 1))

    wq = turned("Wq")
    u = a["L0_attn_u_bias"].reshape(LAYERS, D)
    bq = a["L0_attn_bq"]
    rows = [bq, bq[:, swap], u, u[:, swap]] + [a["L0_attn_" + n] for n in ("bk", "ln1_w", "ln1_b", "ln2_w", "ln2_b")]
    b1 = a["L0_attn_b1"].reshape(LAYERS, NF, P)
    rows += [b1[:, m] for m in range(NF)]
    queries, keys = _rotations()

    def experts(w, shared):
        out = np.zeros((D, NHC * P), np.float32)
        out[:, :NE * INTER] = np.transpose(w, (1, 0, 2)).reshape(D, NE * INTER)
        out[:, NE * INTER:HID] = shared
        return out.reshape(D, NHC, P).transpose(1, 0, 2)

    moe = np.zeros((NHC, P, 4 * P), np.float32)
    moe[:, :, 0:P] = experts(a["L1_ffn_wg"], a["L1_ffn_swg"])
    moe[:, :, P:2 * P] = experts(a["L1_ffn_wu"], a["L1_ffn_swu"])
    down = np.zeros((NHC * P, D), np.float32)
    down[:NE * INTER] = a["L1_ffn_wd"].reshape(NE * INTER, D)
    down[NE * INTER:HID] = a["L1_ffn_swd"]
    moe[:, :, 2 * P:3 * P] = down.reshape(NHC, P, D)
    owner = np.zeros((NE + 1, NHC * P), np.float32)
    owner[np.minimum(np.arange(NHC * P) // INTER, NE), np.arange(NHC * P)] = 1.0
    moe[:, 0:NE + 1, 3 * P:4 * P] = owner.reshape(NE + 1, NHC, P).transpose(1, 0, 2)

    qkv1 = np.concatenate([np.transpose(a["L1_attn_" + n], (0, 2, 1)) for n in ("wq", "wk", "wv")], 2)
    wo1 = np.zeros((H1, HD1 + 1, OUT_W), np.float32)
    wo1[:, 0:HD1, 0:D] = a["L1_attn_wo"].T.reshape(H1, HD1, D)
    wo1[:, HD1, D] = 1.0

    arrays = {
        "x": a["L0_attn_x"].reshape(T, D),
        "wa": np.stack([wq, wq[:, :, swap], turned("Wk"), turned("Wv"), turned("Wo")], 2),
        "w1": turned("W1"),
        "w2": turned("W2").reshape(LAYERS, NF, P, D).transpose(0, 2, 1, 3),
        "vc": np.stack(rows, 2),
        "vb": np.broadcast_to(np.stack([a["L0_attn_" + n] for n in ("bv", "bo", "b2")], 1)[:, None],
                              (LAYERS, P, 3, D)),
        "wt": a["L0_ffn_W"].T,
        "fb": a["L0_ffn_b"],
        "ld": a["L0_ffn_lora_down"].T,
        "da": a["L0_ffn_down_aux"],
        "lu": a["L0_ffn_lora_up"].T,
        "ua": a["L0_ffn_up_aux"].T,
        "rot": queries,
        "pos": keys,
        "qkv1": qkv1,
        "wo1": wo1,
        "gate": a["L1_ffn_gate_w"].T,
        "moe": moe,
    }
    nc = bacc.Bacc("TRN2", target_bir_lowering=False, num_devices=1)
    feeds, args = {}, []
    for name, array in arrays.items():
        array = np.ascontiguousarray(array)
        feeds[f"in_{name}"] = array
        args.append(nc.dram_tensor(f"in_{name}", array.shape, mybir.dt.from_np(array.dtype),
                                   kind="ExternalInput").ap())
    args.append(nc.dram_tensor("out", [T, D], F32, kind="ExternalOutput").ap())
    build(nc, *args)
    r = run_bass_kernel_spmd(nc, [feeds], core_ids=[0])
    return r.results[0]["out"].reshape(NB, S, D)
```

```python
from contextlib import ExitStack

import numpy as np
import concourse.bass as bass
from concourse import mybir

F32 = mybir.dt.float32
BF16 = mybir.dt.bfloat16
ALU = mybir.AluOpType
ACT = mybir.ActivationFunctionType
AX_X = mybir.AxisListType.X

P = 128
NB, S, D = 2, 1024, 128
T = NB * S
NT = T // P
CH = 512
NC = T // CH
TPC = CH // P
LAYERS, H0, HD0, FF = 4, 16, 8, 512
GH = 4
NG = NB * H0 // GH
GPB = NG // NB
NF = FF // P
TERMS = [(0, 0), (0, 1), (0, 2), (1, 0), (1, 1), (2, 0)]
HALF = len(TERMS) * HD0
KROWS = 2 * HALF
KMAX = KROWS + 2
SB_ = S // P
SCALE0 = HD0 ** -0.5
NEG = -1.0e30

H1, HD1 = 16, 64
KFULL = 96
SCALE1 = HD1 ** -0.5
NE, INTER, SHARED = 8, 176, 352
HID = NE * INTER + SHARED
NHC = -(-HID // P)

LORA_R, LORA_D, LORA_U = 4, 100, 50

WQ, WQS, WK, WV, WO = range(5)
VC = ["bq", "bqs", "u", "us", "bk", "ln1w", "ln1b", "ln2w", "ln2b", "b1_0", "b1_1", "b1_2", "b1_3"]
COL = {n: i for i, n in enumerate(VC)}
NVC = len(VC)
VB = {"bv": 0, "bo": 1, "b2": 2}

SB_ = S // P
STEPS = [(c, jb, max(c * CH, jb * P), (c + 1) * CH - max(c * CH, jb * P))
         for c in range(S // CH) for jb in range((c + 1) * TPC)]
NS = len(STEPS)
DIAG = [jb * P >= c * CH for c, jb, _, _ in STEPS]
C_END = [max(s for s in range(NS) if STEPS[s][0] == c) for c in range(S // CH)]
ATILES = [(ib, k0, min((ib + 1) * P - k0, CH), (ib + 1) * P - k0 <= CH)
          for ib in range(SB_) for k0 in range(0, (ib + 1) * P, CH)]

LAG = 2
SLOTS = NS + LAG
A_LIST = [(r, *a) for a in ATILES for r in range(GH)]
NA = len(A_LIST)
A_PER = 4
T_SLOT = [C_END[0] + LAG + 2, SLOTS - 1]
M_SLOT = -(-NA // A_PER) - 1


def group_items(last):
    out = []
    for slot in range(SLOTS):
        if not last:
            out += [(slot, "A", i) for i in range(slot * A_PER, min((slot + 1) * A_PER, NA))]
            if slot == M_SLOT:
                out.append((slot, "M", 0))
        out += [(slot, "T", c) for c in range(S // CH) if T_SLOT[c] == slot]
    return out


V_LN, V_PROJ, V_A = NC, 3 * NC, NA + 1
V_GROUP = V_A + S // CH
V_ATT = V_A + (NG - 1) * V_GROUP + S // CH
V_LAYER = V_LN + V_PROJ + V_ATT + 4 * NC
V_START = 2 * NC + 3
V_G0 = V_LN + V_PROJ + V_A
V_POST = V_LN + V_PROJ + V_ATT
A_K, A_B, A_G = NC // 2, NS * GH // 2, 2 * NF
A_LAYER = A_K + NG * A_B + A_G
USES = [len(range(u, NG, 3)) for u in range(3)]

STEPS1 = [[(b, ib) for b in range(NB)] for ib in range(TPC)] + [[(b, ib)] for b in range(NB) for ib in range(TPC, SB_)]
NS1 = len(STEPS1)
BUF1 = 3
LAG_T, LAG_V = 2, 3
V_TILES = CH // HD1
V1_PROJ = NC + NT // V_TILES
P_SLOT = LAG_V
HALVES = S // CH
POST1 = {("X", 0): 7, ("Y", 0): 8, ("X", HALVES): 9, ("Y", HALVES): 10, ("X", 1): 11, ("Y", 1): 12,
         ("X", HALVES + 1): 15, ("Y", HALVES + 1): 16}
X_BUF = {0: 0, HALVES: 1, 1: 0, HALVES + 1: 1}


def blocks1(n):
    return [(b, kb, (i * TPC + kb) * P) for i, (b, ib) in enumerate(STEPS1[n]) for kb in range(ib + 1)]


def pair_items(first, last):
    out = []
    for u in range(2):
        for slot in range(NS1 + (max(POST1.values()) + 1 - NS1 if last and u else 0)):
            def step(lag):
                n = slot - lag
                return None if n >= NS1 or (n < 0 and first and not u) else (u - (n < 0), n % NS1)
            t, v = step(LAG_T), step(LAG_V)
            banks = [] if t is None else [("T", t[0], (t[1], x)) for x in range(-(-len(blocks1(t[1])) // TPC))]
            out += banks[:1]
            if slot < NS1:
                out.append(("S", u, slot))
            out += banks[1:]
            if v is not None:
                out.append(("V", v[0], v[1]))
            if P_SLOT <= slot < P_SLOT + V1_PROJ and not (last and u):
                out.append(("P", u, slot - P_SLOT))
            for (kind, c), at_ in POST1.items():
                if u and slot == at_ or not u and not first and slot + NS1 == at_:
                    out.append((kind, u - (slot + NS1 == at_ and not u), c))
    return out


def vec_only(items):
    return [x for x in items if x[0] != "S"]


def place(first, last, kind, u, which):
    own, before = vec_only(pair_items(first, last)), vec_only(pair_items(False, False))
    if (kind, u, which) in own:
        return own.index((kind, u, which))
    return before.index((kind, u + 2, which)) - len(before)


V_R = V_START + LAYERS * V_LAYER
V_MOE = V_R + NC + 1 + NC
MOE_J = 2 * NC
MOE_TURNS = NHC // 2
MOE_V = 2 * MOE_J
V_H = V_MOE + MOE_TURNS * MOE_V
V_P0 = V_H + V1_PROJ
V_P1 = V_P0 + len(vec_only(pair_items(True, False)))
V_PAIR = len(vec_only(pair_items(False, False)))
A_MOE = LAYERS * A_LAYER
A_H = A_MOE + MOE_TURNS * MOE_J
PV0 = 3 + LAYERS * NG * NS
CX0 = 2 + LAYERS * NG * (S // CH)
assert V_PAIR % 2 == 0 and NS1 % BUF1 == 0 and P_SLOT + V1_PROJ <= NS1 and M_SLOT < SLOTS
assert len(group_items(False)) == V_GROUP and V_LAYER % 2 == 0 and A_LAYER % 2 == 0


def at(items, kind, which):
    return [i for i, (_, k, w) in enumerate(items) if (k, w) == (kind, which)][0]


def m_item(g):
    return V_G0 - 1 if g == 0 else V_G0 + (g - 1) * V_GROUP + at(group_items(False), "M", 0)


def t_item(g, c):
    return V_G0 + g * V_GROUP + at(group_items(g == NG - 1), "T", c)


N_ROUTE = 25


def down_at(j):
    return 2 * j + 2 if j < MOE_J - 1 else 2 * MOE_J - 1


def up_at(j):
    return max(2 * j - 1, 0)


def build(nc, x_d, wa_d, w1_d, w2_d, vc_d, vb_d, wt_d, fb_d, ld_d, da_d, lu_d, ua_d, rot_d, pos_d,
          qkv1_d, wo1_d, gate_d, moe_d, out_d):
    q_scr = nc.dram_tensor("q_scr", [NB, H0, KROWS, S], BF16, kind="Internal").ap()
    k_scr = nc.dram_tensor("k_scr", [NB, H0, HALF, S], BF16, kind="Internal").ap()
    p_scr = nc.dram_tensor("p_scr", [3, HD0, S], BF16, kind="Internal").ap()

    with ExitStack() as ctx:
        def sb(name, shape, dt=F32):
            return ctx.enter_context(nc.sbuf_tensor(name, shape, dt))

        def sem(name):
            return ctx.enter_context(nc.semaphore(name))

        vecb = [ctx.enter_context(nc.psum_tensor(f"vecb{i}", [P, CH], F32)) for i in range(2)]
        actb = [ctx.enter_context(nc.psum_tensor(f"actb{i}", [P, 2, CH], F32)) for i in range(2)]
        ctxb = ctx.enter_context(nc.psum_tensor("ctxb", [P, 2, CH], F32))

        h = sb("h", [P, NT, D])
        res = sb("res", [P, NT, D])
        xn = sb("xn", [P, NT, D])
        xnT = sb("xnT", [P, T])
        vtok = sb("vtok", [P, NT, D])
        att = sb("att", [P, NT, D])
        big = sb("big", [P, 4 * T])
        kst = sb("kst", [P, 3, GH, S], BF16)
        pbuf = sb("pbuf", [P, 3 * GH * CH])
        kp = sb("kp", [P, 3, T], BF16)
        vst = sb("vst", [P, 2, SB_, GH, 32])
        rot = sb("rot", [P, 2, S])
        osb = sb("osb", [P, 2, CH])
        wa = sb("wa", [P, 5, D])
        w1 = sb("w1", [P, FF])
        w2 = sb("w2", [P, NF, D])
        vc = sb("vc", [P, NVC])
        vb = sb("vb", [P, 3, D])
        bu = sb("bu", [P, 2])
        ident = sb("ident", [P, P])
        amask = sb("amask", [P, CH])
        identb = sb("identb", [P, P], BF16)
        bmask = sb("bmask", [P, P], BF16)
        half = sb("half", [P, NT])
        stats = sb("stats", [P, NT, 6])
        mv = sb("mv", [P, NT, 2])
        vare = sb("vare", [P, NT])
        rstd = sb("rstd", [P, NT])
        mxa = sb("mxa", [P, GH, SB_])
        mxb = sb("mxb", [P, GH, SB_ - TPC])
        nm = sb("nm", [GH * SB_, 2, P], BF16)
        rz = sb("rz", [P, TPC, GH])
        lw = sb("lw", [P, 3, D])
        lws = sb("lws", [P, LORA_R + LORA_U + D])
        nmax = sb("nmax", [P, NS1, NB])
        zsum = sb("zsum", [P, NS1, NB])
        wt9 = sb("wt9", [P, NT, NE + 1])

        hid = big[:, :].rearrange("p (m t) -> p m t", m=NF)
        qf, rf, rtmp, kf = (hid[:, i, :] for i in range(4))
        qst = big[:, 0:3 * GH * S // 2].bitcast(BF16).rearrange("p (u h t) -> p u h t", u=3, h=GH)
        prob = pbuf[:, :].rearrange("p (u h t) -> p u h t", u=3, h=GH)
        pparts = pbuf[:, :].bitcast(BF16).rearrange("p (x k t) -> p x k t", x=2, k=3)
        parts = {"k": kp[:, :, :], "q": pparts[:, 0], "r": pparts[:, 1]}
        whole = {"k": kf, "q": qf, "r": rf}
        mw = vst[:, :, :, :, :].rearrange("p u a b c -> p (u a b c)")[:, 0:2 * 4 * P].rearrange("p (u d) -> p u d", u=2)
        wT = hid[0:KFULL, 3, :]
        moeb = pbuf[:, 0:6 * CH].rearrange("p (x u t) -> p x u t", x=3, u=2)
        prob1 = pbuf[:, 0:BUF1 * S].rearrange("p (u t) -> p u t", u=BUF1)
        probT = pbuf[:, BUF1 * S:2 * BUF1 * S].rearrange("p (u t) -> p u t", u=BUF1)
        pairs = [actb[0], actb[1], ctxb]
        vh = [vtok[:, :, :], xn[:, :, :]]
        wr = kst[:, :, :, :].rearrange("p u h t -> p (u h t)").bitcast(F32)[:, 0:14 * NT * NE]\
            .rearrange("p (k t e) -> p k t e", k=14, t=NT)

        names = {}

        def s(name):
            if name not in names:
                names[name] = sem(name)
            return names[name]

        def vec_read(idx):
            return idx + 3

        act_read = vec_read

        def alone(eng, name):
            eng.sem_inc(s(name), 1)

        block = ctx.enter_context(nc.Block())

        UNITS = [(b, w) for b in range(NB) for w in ("k", "q", "r")]
        NU = len(UNITS)
        SCR = NB * 3 * len(TERMS)
        POS_DMAS = 1 + 3 * GH * len(TERMS)

        @block.sync
        def _(sp):
            def load(dst, src, name):
                sp.dma_start(dst, src).then_inc(s(name), 16)

            tok = "(t p) d -> p t d"
            load(h[:, :, :], x_d.rearrange(tok, p=P), "x_in")
            load(res[:, :, :], x_d.rearrange(tok, p=P), "res_in")
            load(kf[0:HD0, 0:S], pos_d, "pos_in")
            load(rot[:, :, :], rot_d, "rot_in")
            load(lws[0:LORA_D, 0:LORA_R], ld_d, "lora_in")
            load(lws[0:LORA_R, LORA_R:LORA_R + LORA_U], lu_d, "lora_in")
            load(lws[0:LORA_U, LORA_R + LORA_U:], ua_d, "lora_in")
            load(lw[0:LORA_D, 0, :], da_d, "lora_in")
            load(w2[:, 0, :], wt_d, "lora_in")
            load(vb[:, 0, :], fb_d.partition_broadcast(P), "lora_in")
            sp.wait_ge(s("pos_part3"), 1)
            load(p_scr.rearrange("k d t -> d k t"), kp[0:HD0, :, 0:S], "pos_out")
            sp.wait_ge(s("pos_out"), 16)
            for t, (_, kpart) in enumerate(TERMS):
                for u in range(3):
                    for r in range(GH):
                        load(kst[t * HD0:(t + 1) * HD0, u, r, :], p_scr[kpart], "pos_in")

            def stack_load(g):
                u, (b, hg) = g % 3, divmod(g, GPB)
                hs = slice(hg * GH, (hg + 1) * GH)
                load(qst[0:KROWS, u], q_scr[b, hs].rearrange("h r t -> r h t"), f"stack_in{u}")
                load(kst[HALF:KROWS, u], k_scr[b, hs].rearrange("h r t -> r h t"), f"stack_in{u}")

            with sp.Fori(0, LAYERS) as l:
                sp.wait_ge(s("vec_read"), V_START + 2 + l * V_LAYER)
                for dst, src in ((vc[:, :], vc_d), (wa[:, :, :], wa_d), (vb[:, :, :], vb_d), (w1[:, :], w1_d),
                                 (w2[:, :, :], w2_d)):
                    load(dst, src[l], "weights_in")
                for n, (b, w) in enumerate(UNITS):
                    col = slice(b * S, (b + 1) * S)
                    for part in range(3):
                        sp.wait_ge(s(("part1", "part2", "part3")[part]), l * NU + n + 1)
                        for t, (qpart, kpart) in enumerate(TERMS):
                            if (kpart if w == "k" else qpart) == part:
                                row = t * HD0 + (HALF if w == "q" else 0)
                                load((k_scr if w == "k" else q_scr)[b, :, row:row + HD0, :],
                                     parts[w][:, part, col], "scr_out")
                sp.wait_ge(s("scr_out"), 16 * SCR * (l + 1))
                for g in range(3):
                    stack_load(g)
                for g in range(NG):
                    sp.wait_ge(s("vec_read"), vec_read(V_START + l * V_LAYER + m_item(g)))
                    for k in range(2):
                        load(qst[KROWS + k:KROWS + k + 1, g % 3].rearrange("p h (i t) -> p (h i) t", t=P),
                             nm[:, k, :], "maxrow_in")
                    if 1 <= g and g + 2 < NG:
                        sp.wait_ge(s("act_full"), l * A_LAYER + A_K + g * A_B)
                        stack_load(g + 2)

            sp.wait_ge(s("vec_read"), vec_read(V_R - 1))
            load(vc[:, 0:NE], gate_d, "gate_in")
            for u in range(2):
                load(mw[:, u, :], moe_d[u], f"moe_in{u}")
            with sp.Fori(1, MOE_TURNS) as i:
                for u in range(2):
                    sp.wait_ge(s("vec_full"), V_MOE + (i - 1) * MOE_V + down_at((u + 1) * NC - 1) + 1)
                    load(mw[:, u, :], moe_d[i * 2 + u], f"moe_in{u}")

            def head_weights(hd, par):
                load(w1[:, par * 3 * HD1:(par + 1) * 3 * HD1], qkv1_d[hd], f"head_in{par}")

            def pair_weights(j, base, first, last):
                for u in range(2):
                    if not last:
                        sp.wait_ge(s("vec_full"), V_P0 if first and not u else
                                   base + place(first, last, "P", u - 1, V1_PROJ - 1) + 1)
                        head_weights(2 * j + u + 2, u)
                    if not u:
                        if not first:
                            sp.wait_ge(s("vec_full"), base + place(first, last, "Y", -1, HALVES + 1) + 1)
                        load(wa[:, 0, :], wo1_d[j], "wo_in")

            for u in range(2):
                head_weights(u, u)
            pair_weights(0, V_P0, True, False)
            with sp.Fori(1, H1 // 2 - 1) as j:
                pair_weights(j, V_P1 + (j - 1) * V_PAIR, False, False)
            pair_weights(H1 // 2 - 1, V_P1 + (H1 // 2 - 2) * V_PAIR, False, True)
            sp.wait_ge(s("vec_read"), vec_read(V_P1 + (H1 // 2 - 2) * V_PAIR + len(vec_only(pair_items(False, True))) - 1))
            load(out_d.rearrange(tok, p=P), res[:, :, :], "out_done")
            sp.wait_ge(s("out_done"), 16)

        @block.gpsimd
        def _(pool):
            pool.memset(ident[:, :], 0.0).then_inc(s("pool_zero"), 1)
            pool.memset(amask[:, :], 0.0).then_inc(s("pool_zero"), 1)
            pool.memset(vst[:, :, :, :, :], 0.0).then_inc(s("pool_zero"), 1)
            pool.memset(half[:, :], -0.5).then_inc(s("half_set"), 1)
            pool.memset(identb[:, :], 0.0).then_inc(s("pool_zero"), 1)
            pool.memset(bmask[:, :], 0.0).then_inc(s("pool_zero"), 1)
            pool.wait_ge(s("pool_zero"), 5)
            pool.affine_select(out=identb[:, :], in_=identb[:, :], compare_op=ALU.not_equal, fill=1.0, base=0,
                               pattern=[[-1, P]], channel_multiplier=1).then_inc(s("ident_set"), 1)
            pool.affine_select(out=bmask[:, :], in_=bmask[:, :], compare_op=ALU.is_ge, fill=NEG, base=0,
                               pattern=[[1, P]], channel_multiplier=-1).then_inc(s("ident_set"), 1)
            pool.affine_select(out=ident[:, :], in_=ident[:, :], compare_op=ALU.not_equal, fill=1.0, base=0,
                               pattern=[[-1, P]], channel_multiplier=1).then_inc(s("ident_set"), 1)
            pool.affine_select(out=amask[:, CH - P:CH], in_=amask[:, CH - P:CH], compare_op=ALU.is_ge, fill=NEG,
                               base=0, pattern=[[-1, P]], channel_multiplier=1).then_inc(s("amask_set"), 1)
            pool.memset(vst[:, :, :, :, HD0:HD0 + 1].rearrange("p u a h o -> p (u a h) o"), 1.0)\
                .then_inc(s("ones_set"), 1)
            pool.wait_ge(s("half_set"), 1)

            def ln_rstd(n, eps):
                pool.wait_ge(s("ln_aggr"), NT * (n + 1))
                alone(pool, "pool_seen")
                pool.tensor_scalar(vare[:, :], mv[:, :, 1], eps, None, ALU.add).then_inc(s("ln_eps"), 1)
                pool.wait_ge(s("ln_eps"), n + 1)
                pool.tensor_tensor(rstd[:, :], vare[:, :], half[:, :], ALU.pow).then_inc(s("ln_rstd"), 1)

            ln_rstd(0, 1e-5)
            pool.wait_ge(s("pos_part1"), 1)
            pool.tensor_tensor(kf[0:HD0, 0:S], kf[0:HD0, 0:S], kp[0:HD0, 0, 0:S],
                               ALU.subtract).then_inc(s("pos_remainder"), 1)
            pool.wait_ge(s("pos_part2"), 1)
            pool.tensor_tensor(kp[0:HD0, 2, 0:S], kf[0:HD0, 0:S], kp[0:HD0, 1, 0:S],
                               ALU.subtract).then_inc(s("pos_part3"), 1)

            with pool.Fori(0, LAYERS) as l:
                ln_rstd(1 + 2 * l, 1e-6)
                for n in range(NU + 1):
                    if n < NU:
                        b, w = UNITS[n]
                        col = slice(b * S, (b + 1) * S)
                        pool.wait_ge(s("part1"), l * NU + n + 1)
                        pool.tensor_tensor(whole[w][:, col], whole[w][:, col], parts[w][:, 0, col],
                                           ALU.subtract).then_inc(s("remainder"), 1)
                    if n:
                        b, w = UNITS[n - 1]
                        col = slice(b * S, (b + 1) * S)
                        pool.wait_ge(s("part2"), l * NU + n)
                        pool.tensor_tensor(parts[w][:, 2, col], whole[w][:, col], parts[w][:, 1, col],
                                           ALU.subtract).then_inc(s("part3"), 1)

                def add_row(which, n_ln):
                    pool.wait_ge(s("ln_xn"), NT * (n_ln + 1))
                    row = vb[:, which:which + 1, :].to_broadcast([P, NT, D])
                    pool.tensor_tensor(h[:, :, :], h[:, :, :], row, ALU.add).then_inc(s("bias_added"), 1)

                def stage_v(g):
                    b, hg = divmod(g, GPB)
                    pool.wait_ge(s("prob_read"), 3 + (l * NG + max(g - 1, 0)) * NS)
                    alone(pool, "pool_seen")
                    src = vtok[:, b * SB_:(b + 1) * SB_, hg * GH * HD0:(hg + 1) * GH * HD0]
                    pool.tensor_copy(vst[:, g % 2, :, :, 0:HD0],
                                     src.rearrange("p t (h d) -> p t h d", h=GH)).then_inc(s("vst_ready"), 1)

                pool.wait_ge(s("vec_read"), vec_read(V_START + l * V_LAYER + V_LN + V_PROJ - 1))
                for g in range(2):
                    stage_v(g)
                pool.wait_ge(s("weights_in"), 80 * (l + 1))
                add_row(VB["bo"], 1 + 2 * l)
                for g in range(2, NG):
                    stage_v(g)
                ln_rstd(2 + 2 * l, 1e-6)
                add_row(VB["b2"], 2 + 2 * l)
            ln_rstd(1 + 2 * LAYERS, 1e-5)

        @block.scalar
        def _(act):
            act.sem_inc(s("act_read"), 2)
            act.sem_inc(s("ctx_read"), 2)
            act.wait_ge(s("pos_in"), 16)
            act.activation(kp[0:HD0, 0, 0:S], kf[0:HD0, 0:S], ACT.Copy).then_inc(s("pos_part1"), 1)
            act.wait_ge(s("pos_remainder"), 1)
            act.activation(kp[0:HD0, 1, 0:S], kf[0:HD0, 0:S], ACT.Copy).then_inc(s("pos_part2"), 1)
            act.wait_ge(s("pos_out"), 16)

            with act.Fori(0, LAYERS) as l:
                base = l * A_LAYER
                vbase = V_START + l * V_LAYER
                act.wait_ge(s("weights_in"), 80 * (l + 1))
                for b in range(NB):
                    act.wait_ge(s("act_full"), base + b + 1)
                    act.activation(kf[:, b * S:(b + 1) * S], actb[b % 2][:, :, :].rearrange("p a t -> p (a t)"),
                                   ACT.Identity, bias=vc[:, COL["bk"]:COL["bk"] + 1]).then_inc(s("act_read"), 1)
                for n in range(NU + 1):
                    if n < NU:
                        b, w = UNITS[n]
                        col = slice(b * S, (b + 1) * S)
                        if w == "k":
                            act.wait_ge(s("act_read"), act_read(base + b))
                        else:
                            act.wait_ge(s("vec_read"), vec_read(vbase + V_LN + (b + 1) * NC - 1))
                        act.activation(parts[w][:, 0, col], whole[w][:, col], ACT.Copy).then_inc(s("part1"), 1)
                    if n:
                        b, w = UNITS[n - 1]
                        col = slice(b * S, (b + 1) * S)
                        act.wait_ge(s("remainder"), l * NU + n)
                        act.activation(parts[w][:, 1, col], whole[w][:, col], ACT.Copy).then_inc(s("part2"), 1)

                for g in range(NG):
                    def evacuate(c):
                        act.wait_ge(s("prob_read"), 3 + (l * NG + g) * NS + C_END[c] + 1)
                        if g:
                            act.wait_ge(s("vec_full"), vbase + t_item(g - 1, c) + 1)
                        act.activation(osb[:, c, :], ctxb[:, c, :], ACT.Copy).then_inc(s("ctx_read"), 1)

                    for st, (c, jb, i0, w) in enumerate(STEPS):
                        act.wait_ge(s("prob_read"), (l * NG + g) * NS + st + 1)
                        for pr in range(GH // 2):
                            k = A_K + g * A_B + st * (GH // 2) + pr
                            act.wait_ge(s("act_full"), base + k + 1)
                            act.activation(prob[:, (g * NS + st) % 3, 2 * pr:2 * pr + 2, 0:w],
                                           actb[k % 2][:, :, 0:w], ACT.Exp, scale=SCALE0).then_inc(s("act_read"), 1)
                        if st == C_END[0] + LAG:
                            evacuate(0)
                    evacuate(1)

                for n in range(A_G):
                    cp, m = divmod(n, NF)
                    k = A_K + NG * A_B + n
                    act.wait_ge(s("act_full"), base + k + 1)
                    act.activation(hid[:, m, cp * 2 * CH:(cp + 1) * 2 * CH],
                                   actb[k % 2][:, :, :].rearrange("p a t -> p (a t)"), ACT.Gelu,
                                   bias=vc[:, COL["b1_0"] + m:COL["b1_0"] + m + 1]).then_inc(s("act_read"), 1)

            act.wait_ge(s("route"), 3)
            act.activation(wr[:, 1], wr[:, 1], ACT.Exp).then_inc(s("route_exp"), 1)
            with act.Fori(0, MOE_TURNS) as i:
                for j in range(MOE_J):
                    act.wait_ge(s("act_full"), A_MOE + i * MOE_J + j + 1)
                    act.activation(moeb[:, 0, j % 2, :], actb[j % 2][:, 0, :], ACT.Silu).then_inc(s("silu"), 1)
                    act.activation(moeb[:, 1, j % 2, :], actb[j % 2][:, 1, :], ACT.Copy).then_inc(s("act_read"), 1)

            def pair_exp(j, base, first, last):
                for kind, u, n in pair_items(first, last):
                    if kind != "S":
                        continue
                    k = (2 * j + u) * NS1 + n
                    act.wait_ge(s("max1_ready"), k + 1)
                    if n >= BUF1 or u or not first:
                        un, m = u - (n < BUF1), (n - BUF1) % NS1
                        x = -(-len(blocks1(m)) // TPC) - 1
                        act.wait_ge(s("vec_full"), base + place(first, last, "T", un, (m, x)) + 1)
                    if u or not first:
                        act.wait_ge(s("vec_read"), vec_read(base + place(first, last, "V", u - 1, n)))
                    src, dst = pairs[n % BUF1][:, :, :].rearrange("p u t -> p (u t)"), prob1[:, n % BUF1, :]
                    for i, (b, ib) in enumerate(STEPS1[n]):
                        col = slice(i * CH, i * CH + (ib + 1) * P)
                        ins = act.activation(dst[:, col], src[:, col], ACT.Exp, bias=nmax[:, n, i:i + 1],
                                             accum_out=zsum[:, n, i:i + 1])
                    ins.then_inc(s("act_read"), 1)

            pair_exp(0, V_P0, True, False)
            with act.Fori(1, H1 // 2 - 1) as j:
                pair_exp(j, V_P1 + (j - 1) * V_PAIR, False, False)
            pair_exp(H1 // 2 - 1, V_P1 + (H1 // 2 - 2) * V_PAIR, False, True)

        @block.tensor
        def _(pe):
            pe.sem_inc(s("prob_read"), 3)
            pe.wait_ge(s("ident_set"), 3)

            def vec_bank(idx, par):
                pe.wait_ge(s("vec_read"), idx + 1)
                return vecb[par % 2]

            def transposes(idx, par, src, c, n_ln):
                pe.wait_ge(s("ln_xn"), NT * n_ln + TPC * (c + 1))
                bank = vec_bank(idx, par)
                for j in range(TPC):
                    mm = pe.transpose(bank[:, j * P:(j + 1) * P], src[:, c * TPC + j, :], ident[:, :])
                mm.then_inc(s("vec_full"), 1)

            def add_mask(scores):
                return pe.matmul(scores, identb[:, :], bmask[:, :], start=False, stop=True)

            for c in range(NC):
                transposes(c, c, h, c, 0)
            pe.wait_ge(s("lora_in"), 96)
            k = NC
            bank = vec_bank(k, k)
            pe.matmul(bank[0:LORA_R, 0:D], lws[0:LORA_D, 0:LORA_R], lw[0:LORA_D, 0, :], start=True,
                      stop=True).then_inc(s("vec_full"), 1)
            bank = vec_bank(k + 1, k + 1)
            pe.wait_ge(s("vec_read"), vec_read(k))
            pe.matmul(bank[0:LORA_U, 0:D], lws[0:LORA_R, LORA_R:LORA_R + LORA_U], lw[0:LORA_R, 1, :], start=True,
                      stop=True).then_inc(s("vec_full"), 1)
            bank = vec_bank(k + 2, k + 2)
            pe.wait_ge(s("vec_read"), vec_read(k + 1))
            pe.matmul(bank[:, 0:D], lw[0:LORA_U, 2, :], lws[0:LORA_U, LORA_R + LORA_U:], start=True,
                      stop=True).then_inc(s("vec_full"), 1)
            pe.wait_ge(s("vec_read"), vec_read(k + 2))
            for c in range(NC):
                idx = k + 3 + c
                bank = vec_bank(idx, idx)
                for j in range(TPC):
                    t = c * TPC + j
                    mm = pe.matmul(bank[:, j * P:(j + 1) * P], xnT[:, t * P:(t + 1) * P], lw[:, 0, :],
                                   start=True, stop=True)
                mm.then_inc(s("vec_full"), 1)
            pe.wait_ge(s("pos_in"), 16 * POS_DMAS)
            pe.wait_ge(s("ones_set"), 2)

            with pe.Fori(0, LAYERS) as l:
                vbase = V_START + l * V_LAYER
                abase = l * A_LAYER

                def vbank(k):
                    return vec_bank(vbase + k, V_START + k)

                def dense(k, w, c):
                    bank = vbank(k)
                    pe.matmul(bank[:, :], w, xnT[:, c * CH:(c + 1) * CH], start=True,
                              stop=True).then_inc(s("vec_full"), 1)

                for c in range(NC):
                    transposes(vbase + c, V_START + c, xn, c, 1 + 2 * l)
                pe.wait_ge(s("weights_in"), 80 * (l + 1))
                for b in range(NB):
                    pe.wait_ge(s("vec_read"), vec_read(vbase + (b + 1) * NC // 2 - 1))
                    pe.wait_ge(s("act_read"), abase + b + 1)
                    for x in range(2):
                        c = b * 2 + x
                        mm = pe.matmul(actb[b % 2][:, x, :], wa[:, WK, :], xnT[:, c * CH:(c + 1) * CH],
                                       start=True, stop=True)
                    mm.then_inc(s("act_full"), 1)
                    for x in range(2):
                        c = b * 2 + x
                        dense(V_LN + 2 * c, wa[:, WQ, :], c)
                        dense(V_LN + 2 * c + 1, wa[:, WQS, :], c)
                for c in range(NC):
                    bank = vbank(V_LN + 2 * NC + c)
                    for j in range(TPC):
                        t = c * TPC + j
                        mm = pe.matmul(bank[:, j * P:(j + 1) * P], xnT[:, t * P:(t + 1) * P], wa[:, WV, :],
                                       start=True, stop=True)
                    mm.then_inc(s("vec_full"), 1)

                def pass_a(g, k, i):
                    r, ib, k0, w, _ = A_LIST[i]
                    if i == 0:
                        pe.wait_ge(s(f"stack_in{g % 3}"), 32 * (l * USES[g % 3] + g // 3 + 1))
                    bank = vbank(k)
                    pe.matmul(bank[:, 0:w], qst[0:KROWS, g % 3, r, ib * P:(ib + 1) * P],
                              kst[0:KROWS, g % 3, r, k0:k0 + w], start=True, stop=True).then_inc(s("vec_full"), 1)

                def maxima(g, k):
                    bank = vbank(k)
                    pe.wait_ge(s("max_ready"), l * NG + g + 1)
                    pe.transpose(bank[0:GH * SB_, 0:P], mxa[:, :, :].rearrange("p h i -> p (h i)"),
                                 ident[:, :]).then_inc(s("vec_full"), 1)

                def pass_b(g, st, pr):
                    c, jb, i0, w = STEPS[st]
                    if st == 0 and pr == 0:
                        pe.wait_ge(s("maxrow_in"), 32 * (l * NG + g + 1))
                    if True:
                        k = A_K + g * A_B + st * (GH // 2) + pr
                        pe.wait_ge(s("act_read"), abase + k + 1)
                        for x in range(2):
                            r = 2 * pr + x
                            mm = pe.matmul(actb[k % 2][:, x, 0:w], kst[0:KMAX, g % 3, r, jb * P:(jb + 1) * P],
                                           qst[0:KMAX, g % 3, r, i0:i0 + w], start=True, stop=not DIAG[st])
                            if DIAG[st]:
                                mm = add_mask(actb[k % 2][:, x, 0:P])
                        mm.then_inc(s("act_full"), 1)

                def pv(g, st):
                    c, jb, i0, w = STEPS[st]
                    if st == 0:
                        pe.wait_ge(s("vst_ready"), l * NG + g + 1)
                    if jb == 0:
                        pe.wait_ge(s("ctx_read"), (l * NG + g) * (S // CH) + c + 1)
                    pe.wait_ge(s("act_read"), act_read(abase + A_K + g * A_B + 2 * st + 1))
                    for r in range(GH):
                        mm = pe.matmul(ctxb[32 * r:32 * r + 32, c, i0 - c * CH:CH], vst[:, g % 2, jb, r, :],
                                       prob[:, (g * NS + st) % 3, r, 0:w], start=(jb == 0), stop=(st == C_END[c]))
                    mm.then_inc(s("prob_read"), 1)

                def turn(g, k, c):
                    bank = vbank(k)
                    pe.wait_ge(s("ctx_read"), 2 + (l * NG + g) * (S // CH) + c + 1)
                    for j in range(TPC):
                        mm = pe.transpose(bank[:, j * P:(j + 1) * P], osb[:, c, j * P:(j + 1) * P], ident[:, :])
                    mm.then_inc(s("vec_full"), 1)

                for i in range(NA):
                    pass_a(0, V_LN + V_PROJ + i, i)
                maxima(0, V_LN + V_PROJ + NA)
                for g in range(NG):
                    items = group_items(g == NG - 1)
                    for slot in range(SLOTS):
                        vec = [(k, kind, x) for k, (sl, kind, x) in enumerate(items) if sl == slot]

                        def vec_item(n):
                            for k, kind, x in vec[n:n + 1]:
                                k += V_G0 + g * V_GROUP
                                if kind == "A":
                                    pass_a(g + 1, k, x)
                                if kind == "M":
                                    maxima(g + 1, k)
                                if kind == "T":
                                    turn(g, k, x)

                        last_turn = bool(vec) and vec[-1][1:] == ("T", 1)
                        for pr in range(GH // 2):
                            if slot < NS:
                                pass_b(g, slot, pr)
                            vec_item(pr) if not (last_turn and pr == len(vec) - 1) else None
                        early = min(GH // 2, len(vec) - last_turn)
                        if not last_turn:
                            vec_item(2)
                        if slot >= LAG:
                            pv(g, slot - LAG)
                        for n in range(early + (not last_turn), len(vec)):
                            vec_item(n)

                for c in range(NC):
                    k = V_POST + c
                    bank = vbank(k)
                    if c == 0:
                        pe.wait_ge(s("vec_read"), vec_read(vbase + V_POST - 1))
                    for j in range(TPC):
                        mm = pe.transpose(bank[:, j * P:(j + 1) * P], att[:, c * TPC + j, :], ident[:, :])
                    mm.then_inc(s("vec_full"), 1)
                for c in range(NC):
                    k = V_POST + NC + c
                    bank = vbank(k)
                    pe.wait_ge(s("vec_read"), vec_read(vbase + V_POST + c))
                    for j in range(TPC):
                        t = c * TPC + j
                        mm = pe.matmul(bank[:, j * P:(j + 1) * P], xnT[:, t * P:(t + 1) * P], wa[:, WO, :],
                                       start=True, stop=True)
                    mm.then_inc(s("vec_full"), 1)
                for c in range(NC):
                    k = V_POST + 2 * NC + c
                    transposes(vbase + k, V_START + k, xn, c, 2 + 2 * l)
                for cp in range(2):
                    pe.wait_ge(s("vec_read"), vec_read(vbase + V_POST + 2 * NC + 2 * cp + 1))
                    for m in range(NF):
                        k = A_K + NG * A_B + cp * NF + m
                        pe.wait_ge(s("act_read"), abase + k + 1)
                        for x in range(2):
                            c = 2 * cp + x
                            mm = pe.matmul(actb[k % 2][:, x, :], w1[:, m * P:(m + 1) * P],
                                           xnT[:, c * CH:(c + 1) * CH], start=True, stop=True)
                        mm.then_inc(s("act_full"), 1)
                for c in range(NC):
                    bank = vbank(V_POST + 3 * NC + c)
                    pe.wait_ge(s("act_read"), act_read(abase + A_K + NG * A_B + (c // 2) * NF + NF - 1))
                    for j in range(TPC):
                        t = c * TPC + j
                        for m in range(NF):
                            mm = pe.matmul(bank[:, j * P:(j + 1) * P], hid[:, m, t * P:(t + 1) * P], w2[:, m, :],
                                           start=(m == 0), stop=(m == NF - 1))
                    mm.then_inc(s("vec_full"), 1)

            for c in range(NC):
                transposes(V_R + c, V_R + c, xn, c, 1 + 2 * LAYERS)
            pe.wait_ge(s("vec_read"), vec_read(V_R + NC - 1))
            pe.wait_ge(s("gate_in"), 16)
            bank = vec_bank(V_R + NC, V_R + NC)
            for t in range(NT):
                mm = pe.matmul(bank[:, t * NE:(t + 1) * NE], xnT[:, t * P:(t + 1) * P], vc[:, 0:NE],
                               start=True, stop=True)
            mm.then_inc(s("vec_full"), 1)
            pe.wait_ge(s("route"), N_ROUTE)
            for c in range(NC):
                idx = V_R + NC + 1 + c
                bank = vec_bank(idx, idx)
                for j in range(TPC):
                    mm = pe.transpose(bank[0:NE + 1, j * P:(j + 1) * P], wt9[:, c * TPC + j, :], ident[:, :])
                mm.then_inc(s("vec_full"), 1)
            pe.wait_ge(s("vec_read"), vec_read(V_MOE - 1))

            with pe.Fori(0, MOE_TURNS) as i:
                def down(j):
                    u, c = divmod(j, NC)
                    k = down_at(j)
                    bank = vec_bank(V_MOE + i * MOE_V + k, V_MOE + k)
                    pe.wait_ge(s("vec_read"), vec_read(V_MOE + i * MOE_V + up_at(j)))
                    for x in range(TPC):
                        mm = pe.matmul(bank[:, x * P:(x + 1) * P], moeb[:, 2, j % 2, x * P:(x + 1) * P],
                                       mw[:, u, 2 * P:3 * P], start=True, stop=True)
                    mm.then_inc(s("vec_full"), 1)

                for j in range(MOE_J):
                    u, c = divmod(j, NC)
                    if c == 0:
                        pe.wait_ge(s(f"moe_in{u}"), 16 * (i + 1))
                    tokens = xnT[:, c * CH:(c + 1) * CH]
                    pe.wait_ge(s("act_read"), A_MOE + i * MOE_J + j + 1)
                    pe.matmul(actb[j % 2][:, 0, :], mw[:, u, 0:P], tokens, start=True, stop=True)
                    pe.matmul(actb[j % 2][:, 1, :], mw[0:KFULL, u, 3 * P:4 * P], wT[:, c * CH:(c + 1) * CH],
                              start=True, stop=True).then_inc(s("act_full"), 1)
                    k = up_at(j)
                    bank = vec_bank(V_MOE + i * MOE_V + k, V_MOE + k)
                    pe.matmul(bank[:, :], mw[:, u, P:2 * P], tokens, start=True, stop=True)\
                        .then_inc(s("vec_full"), 1)
                    if j:
                        down(j - 1)
                down(MOE_J - 1)

            def project(idx, par_v, par, turn, n):
                wt = w1[:, par * 3 * HD1:(par + 1) * 3 * HD1]
                if n == 0:
                    pe.wait_ge(s(f"head_in{par}"), 16 * (turn + 1))
                bank = vec_bank(idx, par_v)
                if n < NC:
                    mm = pe.matmul(bank[:, :], wt[:, 0:2 * HD1], xnT[:, n * CH:(n + 1) * CH], start=True, stop=True)
                else:
                    for j in range(V_TILES):
                        t = (n - NC) * V_TILES + j
                        mm = pe.matmul(bank[:, j * HD1:(j + 1) * HD1], xnT[:, t * P:(t + 1) * P],
                                       wt[:, 2 * HD1:3 * HD1], start=True, stop=True)
                mm.then_inc(s("vec_full"), 1)

            def scores1(k, par, n):
                pe.wait_ge(s("act_read"), A_H + k + 3 - BUF1)
                pair = pairs[n % BUF1][:, :, :].rearrange("p u t -> p (u t)")
                for i, (b, ib) in enumerate(STEPS1[n]):
                    q = hid[0:KFULL, 2 * par, b * S + ib * P:b * S + (ib + 1) * P]
                    for k0 in range(0, (ib + 1) * P, CH):
                        k1 = min(k0 + CH, (ib + 1) * P)
                        mm = pe.matmul(pair[:, i * CH + k0:i * CH + k1], q, hid[0:KFULL, 2 * par + 1, b * S + k0:b * S + k1],
                                       start=True, stop=k1 <= ib * P)
                    mm = pe.matmul(pair[:, i * CH + ib * P:i * CH + (ib + 1) * P], bmask[:, :], identb[:, :],
                                   start=False, stop=True)
                mm.then_inc(s("act_full"), 1)

            pe.wait_ge(s("zeros1_set"), 1)
            pe.wait_ge(s("ctx_read"), CX0)
            pe.wait_ge(s("act_read"), A_H + 2)
            for n in range(V1_PROJ):
                project(V_H + n, V_H + n, 0, 0, n)

            def pair(j, base, pbase, first, last):
                v = 0
                for kind, u, x in pair_items(first, last):
                    par = u % 2
                    if kind == "S":
                        if x == 0:
                            pe.wait_ge(s("vec_read"), vec_read(V_P0 - 1 if first and not u else
                                                               base + place(first, last, "P", u - 1, NC - 1)))
                        scores1((2 * j + u) * NS1 + x, par, x)
                        continue
                    bank = None if kind == "P" else vec_bank(base + v, pbase + v)
                    if kind == "P":
                        project(base + v, pbase + v, 1 - par, j + u, x)
                    if kind == "T":
                        n, part = x
                        pe.wait_ge(s("act_read"), act_read(A_H + (2 * j + u) * NS1 + n))
                        for i, (_, _, col) in enumerate(blocks1(n)[part * TPC:(part + 1) * TPC]):
                            mm = pe.transpose(bank[:, i * P:(i + 1) * P], prob1[:, n % BUF1, col:col + P], ident[:, :])
                        mm.then_inc(s("vec_full"), 1)
                    if kind == "V":
                        m = -(-len(blocks1(x)) // TPC) - 1
                        pe.wait_ge(s("vec_read"), vec_read(base + place(first, last, "T", u, (x, m))))
                        for i, (b, kb, _) in enumerate(blocks1(x)):
                            slot = [y for y, (bb, _) in enumerate(STEPS1[x]) if bb == b][0]
                            mm = pe.matmul(bank[:, slot * HD1:(slot + 1) * HD1], probT[:, x % BUF1, i * P:(i + 1) * P],
                                           vh[par][:, b * SB_ + kb, 0:HD1], start=(kb == 0),
                                           stop=(kb == STEPS1[x][slot][1]))
                        mm.then_inc(s("vec_full"), 1)
                    if kind == "X":
                        n = [n for n in range(NS1) for b, ib in STEPS1[n] if (b * SB_ + ib) // TPC == x][-1]
                        pe.wait_ge(s("vec_read"), vec_read(base + place(first, last, "V", u, n)))
                        for i in range(TPC):
                            mm = pe.transpose(bank[:, i * P:(i + 1) * P], att[:, x * TPC + i, :], ident[:, :])
                        mm.then_inc(s("vec_full"), 1)
                    if kind == "Y":
                        pe.wait_ge(s("vec_read"), vec_read(base + place(first, last, "X", u, x)))
                        if u > 0:
                            pe.wait_ge(s("wo_in"), 16 * (j + 1))
                        for i in range(TPC):
                            mm = pe.matmul(bank[:, i * P:(i + 1) * P], osb[:, X_BUF[x], i * P:(i + 1) * P], wa[:, 0, :],
                                           start=True, stop=True)
                        mm.then_inc(s("vec_full"), 1)
                    v += 1

            pair(0, V_P0, V_P0, True, False)
            with pe.Fori(1, H1 // 2 - 1) as j:
                pair(j, V_P1 + (j - 1) * V_PAIR, V_P1, False, False)
            pair(H1 // 2 - 1, V_P1 + (H1 // 2 - 2) * V_PAIR, V_P1, False, True)

        @block.vector
        def _(dve):
            dve.sem_inc(s("vec_read"), 2)
            dve.memset(kst[KROWS:KMAX, :, :, :].rearrange("p u h t -> p (u h t)"), 1.0).then_inc(s("ones_set"), 1)

            def full(idx):
                dve.wait_ge(s("vec_full"), idx + 1)

            def own(idx):
                dve.wait_ge(s("vec_read"), idx + 2)

            def layer_norm(n, src, dst):
                if not isinstance(n, int) or n:
                    dve.wait_ge(s("ln_xn"), NT * n)
                for t in range(NT):
                    dve.bn_stats(stats[:, t, :], src[:, t, :]).then_inc(s("ln_stat"), 1)
                dve.wait_ge(s("ln_stat"), NT * (n + 1))
                alone(dve, "dve_seen")
                for t in range(NT):
                    dve.bn_aggr(mv[:, t, :], stats[:, t, :]).then_inc(s("ln_aggr"), 1)
                dve.wait_ge(s("ln_rstd"), n + 1)
                for t in range(NT):
                    dve.tensor_scalar(dst[:, t, :], src[:, t, :], mv[:, t, 0:1], rstd[:, t:t + 1],
                                      ALU.subtract, ALU.mult).then_inc(s("ln_xn"), 1)

            dve.wait_ge(s("x_in"), 16)
            layer_norm(0, h, h)
            for c in range(NC):
                full(c)
                dve.tensor_copy(xnT[:, c * CH:(c + 1) * CH], vecb[c % 2][:, :]).then_inc(s("vec_read"), 1)
            k = NC
            full(k)
            dve.tensor_copy(lw[0:LORA_R, 1, :], vecb[k % 2][0:LORA_R, 0:D]).then_inc(s("vec_read"), 1)
            full(k + 1)
            dve.tensor_copy(lw[0:LORA_U, 2, :], vecb[(k + 1) % 2][0:LORA_U, 0:D]).then_inc(s("vec_read"), 1)
            full(k + 2)
            dve.wait_ge(s("lora_in"), 96)
            dve.tensor_tensor(lw[:, 0, :], vecb[k % 2][:, 0:D], w2[:, 0, :], ALU.add).then_inc(s("vec_read"), 1)
            dve.wait_ge(s("res_in"), 16)
            dve.tensor_tensor(res[:, :, :], res[:, :, :], vb[:, 0:1, :].to_broadcast([P, NT, D]),
                              ALU.add).then_inc(s("res_bias"), 1)
            dve.wait_ge(s("res_bias"), 1)
            for c in range(NC):
                idx = k + 3 + c
                full(idx)
                part = res[:, c * TPC:(c + 1) * TPC, :]
                dve.tensor_tensor(part, vecb[idx % 2][:, :].rearrange("p (t d) -> p t d", t=TPC), part,
                                  ALU.add).then_inc(s("vec_read"), 1)
            dve.wait_ge(s("rot_in"), 16)
            dve.wait_ge(s("amask_set"), 1)

            def row_max(bank, out, w, diagonal, last):
                if diagonal:
                    alone(dve, "dve_seen")
                    return dve.tensor_tensor_reduce(bank[:, 0:w], bank[:, 0:w], amask[:, CH - w:CH], 1.0, NEG,
                                                    ALU.add, ALU.max, out)
                return dve.tensor_reduce(out, bank[:, 0:w], AX_X, ALU.max)

            with dve.Fori(0, LAYERS) as l:
                vbase = V_START + l * V_LAYER

                def bank_of(k):
                    return vecb[(V_START + k) % 2]

                def affine(k, c, w, b):
                    full(vbase + k)
                    dve.tensor_scalar(xnT[:, c * CH:(c + 1) * CH], bank_of(k)[:, :], vc[:, COL[w]:COL[w] + 1],
                                      vc[:, COL[b]:COL[b] + 1], ALU.mult, ALU.add).then_inc(s("vec_read"), 1)

                own(vbase)
                layer_norm(1 + 2 * l, h, xn)
                dve.wait_ge(s("weights_in"), 80 * (l + 1))
                for j, (x, y) in enumerate((("bq", "u"), ("bqs", "us"))):
                    dve.tensor_tensor(bu[:, j:j + 1], vc[:, COL[x]:COL[x] + 1], vc[:, COL[y]:COL[y] + 1],
                                      ALU.add).then_inc(s("bu_ready"), 1)
                dve.wait_ge(s("bu_ready"), 2 * (l + 1))
                for c in range(NC):
                    affine(c, c, "ln1w", "ln1b")
                for c in range(NC):
                    k = V_LN + 2 * c
                    col = slice(c * CH, (c + 1) * CH)
                    pos = slice(c * CH % S, c * CH % S + CH)
                    full(vbase + k)
                    dve.tensor_scalar(qf[:, col], bank_of(k)[:, :], vc[:, COL["bq"]:COL["bq"] + 1], None, ALU.add)
                    dve.scalar_tensor_tensor(out=rf[:, col], in0=bank_of(k)[:, :], scalar=bu[:, 0:1],
                                             in1=rot[:, 0, pos], op0=ALU.add, op1=ALU.mult)\
                        .then_inc(s("vec_read"), 1)
                    full(vbase + k + 1)
                    dve.scalar_tensor_tensor(out=rtmp[:, col], in0=bank_of(k + 1)[:, :], scalar=bu[:, 1:2],
                                             in1=rot[:, 1, pos], op0=ALU.add, op1=ALU.mult)\
                        .then_inc(s("rot_half"), 1)
                    dve.wait_ge(s("rot_half"), l * NC + c + 1)
                    dve.tensor_tensor(rf[:, col], rf[:, col], rtmp[:, col], ALU.add).then_inc(s("vec_read"), 1)
                for c in range(NC):
                    k = V_LN + 2 * NC + c
                    full(vbase + k)
                    dve.tensor_tensor(vtok[:, c * TPC:(c + 1) * TPC, :],
                                      bank_of(k)[:, :].rearrange("p (t d) -> p t d", t=TPC),
                                      vb[:, VB["bv"]:VB["bv"] + 1, :].to_broadcast([P, TPC, D]),
                                      ALU.add).then_inc(s("vec_read"), 1)

                def maximum(k, i):
                    r, ib, k0, w, diagonal = A_LIST[i]
                    full(vbase + k)
                    out = mxa[:, r, ib:ib + 1] if diagonal else mxb[:, r, ib - TPC:ib - TPC + 1]
                    row_max(bank_of(k), out, w, diagonal, False).then_inc(s("vec_read"), 1)

                def combine(g, k):
                    own(vbase + k)
                    dve.tensor_tensor(mxa[:, :, TPC:SB_], mxa[:, :, TPC:SB_], mxb[:, :, :],
                                      ALU.max).then_inc(s("max_ready"), 1)

                def negate(g, k):
                    full(vbase + k)
                    if g:
                        dve.wait_ge(s("maxrow_in"), 32 * (l * NG + g))
                    rows = bank_of(k)[0:GH * SB_, 0:P]
                    dve.tensor_scalar(nm[:, 0, :], rows, -1.0, None, ALU.mult).then_inc(s("nm_high"), 1)
                    dve.wait_ge(s("nm_high"), l * NG + g + 1)
                    dve.scalar_tensor_tensor(out=nm[:, 1, :], in0=rows, scalar=-1.0, in1=nm[:, 0, :],
                                             op0=ALU.mult, op1=ALU.subtract).then_inc(s("vec_read"), 1)

                def context(g, k, c):
                    full(vbase + k)
                    b, hg = divmod(g, GPB)
                    t = b * SB_ + c * TPC
                    v = bank_of(k)[:, :].rearrange("p (t h d) -> p t h d", t=TPC, h=GH)
                    own(vbase + k)
                    dve.reciprocal(rz[:, :, :], v[:, :, :, HD0]).then_inc(s("rz_ready"), 1)
                    dve.wait_ge(s("rz_ready"), (l * NG + g) * 2 + c + 1)
                    dve.tensor_tensor(
                        att[:, t:t + TPC, hg * GH * HD0:(hg + 1) * GH * HD0].rearrange("p t (h d) -> p t h d", h=GH),
                        v[:, :, :, 0:HD0], rz[:, :, :].unsqueeze(3).to_broadcast([P, TPC, GH, HD0]),
                        ALU.mult).then_inc(s("vec_read"), 1)

                for i in range(NA):
                    maximum(V_LN + V_PROJ + i, i)
                combine(0, V_LN + V_PROJ + NA)
                negate(0, V_LN + V_PROJ + NA)
                for g in range(NG):
                    for k, (_, kind, x) in enumerate(group_items(g == NG - 1)):
                        k += V_G0 + g * V_GROUP
                        if kind == "A":
                            maximum(k, x)
                        if kind == "M":
                            combine(g + 1, k)
                            negate(g + 1, k)
                        if kind == "T":
                            context(g, k, x)

                for c in range(NC):
                    full(vbase + V_POST + c)
                    dve.tensor_copy(xnT[:, c * CH:(c + 1) * CH], bank_of(V_POST + c)[:, :])\
                        .then_inc(s("vec_read"), 1)

                def add_to_h(k, c):
                    full(vbase + k)
                    part = h[:, c * TPC:(c + 1) * TPC, :]
                    dve.tensor_tensor(part, bank_of(k)[:, :].rearrange("p (t d) -> p t d", t=TPC), part,
                                      ALU.add).then_inc(s("vec_read"), 1)

                dve.wait_ge(s("bias_added"), 2 * l + 1)
                for c in range(NC):
                    add_to_h(V_POST + NC + c, c)
                own(vbase + V_POST + 2 * NC)
                layer_norm(2 + 2 * l, h, xn)
                for c in range(NC):
                    affine(V_POST + 2 * NC + c, c, "ln2w", "ln2b")
                dve.wait_ge(s("bias_added"), 2 * l + 2)
                for c in range(NC):
                    add_to_h(V_POST + 3 * NC + c, c)

            own(V_R)
            dve.tensor_tensor(res[:, :, :], res[:, :, :], h[:, :, :], ALU.add).then_inc(s("res_ready"), 1)
            dve.wait_ge(s("res_ready"), 1)
            layer_norm(1 + 2 * LAYERS, res, xn)
            for c in range(NC):
                full(V_R + c)
                dve.tensor_copy(xnT[:, c * CH:(c + 1) * CH], vecb[(V_R + c) % 2][:, :]).then_inc(s("vec_read"), 1)

            n_route = [0]

            def route(ins):
                n_route[0] += 1
                ins.then_inc(s("route"), 1)
                dve.wait_ge(s("route"), n_route[0])

            idx = V_R + NC
            full(idx)
            lg, e, e2, rank, key, sel1, sel2 = (wr[:, i] for i in range(7))

            def one(i):
                return wr[:, 7 + i // NE, :, i % NE]

            def wide(x):
                return x.unsqueeze(2).to_broadcast([P, NT, NE])

            mx, sm, rs, m1, km, m2, ds, rd = (one(i) for i in range(8))
            dve.tensor_copy(lg, vecb[idx % 2][:, 0:NT * NE].rearrange("p (t e) -> p t e", e=NE))\
                .then_inc(s("vec_read"), 1)
            own(idx + 1)
            for x in range(NE):
                ins = dve.memset(rank[:, :, x:x + 1], float(NE - x))
            route(ins)
            route(dve.tensor_reduce(mx, lg, AX_X, ALU.max))
            route(dve.tensor_tensor(e, lg, wide(mx), ALU.subtract))
            dve.wait_ge(s("route_exp"), 1)
            route(dve.tensor_reduce(sm, e, AX_X, ALU.add))
            route(dve.reciprocal(rs, sm))
            route(dve.tensor_tensor(e, e, wide(rs), ALU.mult))
            route(dve.tensor_reduce(m1, e, AX_X, ALU.max))

            def first_of(sel, vals, mval):
                route(dve.tensor_tensor(sel, vals, wide(mval), ALU.is_equal))
                route(dve.tensor_tensor(key, sel, rank, ALU.mult))
                route(dve.tensor_reduce(km, key, AX_X, ALU.max))
                route(dve.tensor_tensor(sel, key, wide(km), ALU.is_equal))

            first_of(sel1, e, m1)
            route(dve.scalar_tensor_tensor(out=e2, in0=sel1, scalar=-2.0, in1=e, op0=ALU.mult, op1=ALU.add))
            route(dve.tensor_reduce(m2, e2, AX_X, ALU.max))
            first_of(sel2, e2, m2)
            route(dve.tensor_tensor(ds, m1, m2, ALU.add))
            route(dve.tensor_scalar(ds, ds, 1e-20, None, ALU.add))
            route(dve.reciprocal(rd, ds))
            route(dve.tensor_tensor(sel1, sel1, sel2, ALU.add))
            route(dve.tensor_tensor(e, e, wide(rd), ALU.mult))
            route(dve.tensor_tensor(wt9[:, :, 0:NE], e, sel1, ALU.mult))
            route(dve.memset(wt9[:, :, NE:NE + 1], 1.0))
            route(dve.memset(wT, 0.0))
            assert n_route[0] == N_ROUTE, n_route[0]
            for c in range(NC):
                idx = V_R + NC + 1 + c
                full(idx)
                dve.tensor_copy(wT[0:NE + 1, c * CH:(c + 1) * CH], vecb[idx % 2][0:NE + 1, :]).then_inc(s("vec_read"), 1)

            with dve.Fori(0, MOE_TURNS) as i:
                def add_down(j):
                    c = j % NC
                    k = down_at(j)
                    full(V_MOE + i * MOE_V + k)
                    part = res[:, c * TPC:(c + 1) * TPC, :]
                    own(V_MOE + i * MOE_V + k - 1)
                    dve.tensor_tensor(part, vecb[(V_MOE + k) % 2][:, :].rearrange("p (t d) -> p t d", t=TPC), part,
                                      ALU.add).then_inc(s("vec_read"), 1)

                for j in range(MOE_J):
                    k = up_at(j)
                    full(V_MOE + i * MOE_V + k)
                    dve.wait_ge(s("act_read"), act_read(A_MOE + i * MOE_J + j))
                    hb = moeb[:, 2, j % 2, :]
                    dve.tensor_tensor(hb, moeb[:, 0, j % 2, :], vecb[(V_MOE + k) % 2][:, :],
                                      ALU.mult).then_inc(s("moe_hidden"), 1)
                    dve.wait_ge(s("moe_hidden"), i * MOE_J + j + 1)
                    dve.tensor_tensor(hb, hb, moeb[:, 1, j % 2, :], ALU.mult).then_inc(s("vec_read"), 1)
                    if j:
                        add_down(j - 1)
                add_down(MOE_J - 1)

            own(V_H)
            dve.memset(hid[HD1:KFULL, :, :], 0.0).then_inc(s("zeros1_set"), 1)

            def project(idx, par_v, par, n):
                full(idx)
                bank = vecb[par_v % 2]
                if n < NC:
                    col = slice(n * CH, (n + 1) * CH)
                    dve.tensor_scalar(hid[0:HD1, 2 * par, col], bank[0:HD1, :], SCALE1, None, ALU.mult)
                    dve.tensor_copy(hid[0:HD1, 2 * par + 1, col], bank[HD1:2 * HD1, :]).then_inc(s("vec_read"), 1)
                else:
                    t = (n - NC) * V_TILES
                    dve.tensor_copy(vh[par][:, t:t + V_TILES, 0:HD1],
                                    bank[:, :].rearrange("p (t d) -> p t d", d=HD1)).then_inc(s("vec_read"), 1)

            for n in range(V1_PROJ):
                project(V_H + n, V_H + n, 0, n)
            att_bi = att[:, :, :].rearrange("p (b i) d -> p b i d", b=NB)

            def pair(j, base, pbase, first, last):
                v = 0
                for kind, u, x in pair_items(first, last):
                    par = u % 2
                    if kind == "S":
                        k = (2 * j + u) * NS1 + x
                        dve.wait_ge(s("act_full"), A_H + k + 1)
                        w = (STEPS1[x][0][1] + 1) * P
                        src = pairs[x % BUF1]
                        src = src[:, :, 0:w] if len(STEPS1[x]) > 1 else src[:, :, :].rearrange("p u t -> p (u t)")[:, 0:w]
                        dve.tensor_reduce(nmax[:, x, 0:len(STEPS1[x])], src, AX_X, ALU.max,
                                          negate=True).then_inc(s("max1_ready"), 1)
                        continue
                    idx, bank = base + v, vecb[(pbase + v) % 2]
                    if kind == "P":
                        project(idx, pbase + v, 1 - par, x)
                    if kind == "T":
                        full(idx)
                        n, part = x
                        w = len(blocks1(n)[part * TPC:(part + 1) * TPC]) * P
                        dve.tensor_copy(probT[:, n % BUF1, part * CH:part * CH + w],
                                        bank[:, 0:w]).then_inc(s("vec_read"), 1)
                    if kind == "V":
                        full(idx)
                        m, ib = len(STEPS1[x]), STEPS1[x][0][1]
                        b0 = STEPS1[x][0][0]
                        dve.reciprocal(zsum[:, x, 0:m], zsum[:, x, 0:m]).then_inc(s("rz1_ready"), 1)
                        dve.wait_ge(s("rz1_ready"), (2 * j + u) * NS1 + x + 1)
                        dve.tensor_tensor(att_bi[:, b0:b0 + m, ib, par * HD1:(par + 1) * HD1],
                                          bank[:, 0:m * HD1].rearrange("p (b d) -> p b d", b=m),
                                          zsum[:, x, 0:m].unsqueeze(2).to_broadcast([P, m, HD1]),
                                          ALU.mult).then_inc(s("vec_read"), 1)
                    if kind == "X":
                        full(idx)
                        dve.tensor_copy(osb[:, X_BUF[x], :], bank[:, :]).then_inc(s("vec_read"), 1)
                    if kind == "Y":
                        full(idx)
                        part = res[:, x * TPC:(x + 1) * TPC, :]
                        dve.tensor_tensor(part, bank[:, :].rearrange("p (t d) -> p t d", t=TPC), part,
                                          ALU.add).then_inc(s("vec_read"), 1)
                    v += 1

            pair(0, V_P0, V_P0, True, False)
            with dve.Fori(1, H1 // 2 - 1) as j:
                pair(j, V_P1 + (j - 1) * V_PAIR, V_P1, False, False)
            pair(H1 // 2 - 1, V_P1 + (H1 // 2 - 2) * V_PAIR, V_P1, False, True)


def _rotations():
    m = HD0 // 2
    inv = (1.0 / 10000.0 ** (np.arange(0, HD0, 2, dtype=np.float32) / np.float32(HD0))).astype(np.float32)
    angle = inv.astype(np.float64)[:, None] * np.arange(S)[None, :]
    sin, cos = np.sin(angle), np.cos(angle)
    queries = np.stack([np.concatenate([sin, sin]), np.concatenate([cos, -cos])], 1)
    queries = np.tile(queries, (P // HD0, 1, 1))
    assert m * 2 == HD0
    return queries.astype(np.float32), np.concatenate([cos, sin]).astype(np.float32)


def kernel(**inputs):
    import concourse.bacc as bacc
    from concourse.bass_utils import run_bass_kernel_spmd

    a = {k: np.asarray(v) for k, v in inputs.items()}
    swap = np.arange(D).reshape(H0, 2, HD0 // 2)[:, ::-1].reshape(-1)

    def turned(name):
        return np.transpose(a["L0_attn_" + name], (0, 2, 1))

    wq = turned("Wq")
    u = a["L0_attn_u_bias"].reshape(LAYERS, D)
    bq = a["L0_attn_bq"]
    rows = [bq, bq[:, swap], u, u[:, swap]] + [a["L0_attn_" + n] for n in ("bk", "ln1_w", "ln1_b", "ln2_w", "ln2_b")]
    b1 = a["L0_attn_b1"].reshape(LAYERS, NF, P)
    rows += [b1[:, m] for m in range(NF)]
    queries, keys = _rotations()

    def experts(w, shared):
        out = np.zeros((D, NHC * P), np.float32)
        out[:, :NE * INTER] = np.transpose(w, (1, 0, 2)).reshape(D, NE * INTER)
        out[:, NE * INTER:HID] = shared
        return out.reshape(D, NHC, P).transpose(1, 0, 2)

    moe = np.zeros((NHC, P, 4 * P), np.float32)
    moe[:, :, 0:P] = experts(a["L1_ffn_wg"], a["L1_ffn_swg"])
    moe[:, :, P:2 * P] = experts(a["L1_ffn_wu"], a["L1_ffn_swu"])
    down = np.zeros((NHC * P, D), np.float32)
    down[:NE * INTER] = a["L1_ffn_wd"].reshape(NE * INTER, D)
    down[NE * INTER:HID] = a["L1_ffn_swd"]
    moe[:, :, 2 * P:3 * P] = down.reshape(NHC, P, D)
    owner = np.zeros((NE + 1, NHC * P), np.float32)
    owner[np.minimum(np.arange(NHC * P) // INTER, NE), np.arange(NHC * P)] = 1.0
    moe[:, 0:NE + 1, 3 * P:4 * P] = owner.reshape(NE + 1, NHC, P).transpose(1, 0, 2)

    qkv1 = np.concatenate([np.transpose(a["L1_attn_" + n], (0, 2, 1)) for n in ("wq", "wk", "wv")], 2)
    wo1 = a["L1_attn_wo"].T.reshape(H1 // 2, 2 * HD1, D)

    arrays = {
        "x": a["L0_attn_x"].reshape(T, D),
        "wa": np.stack([wq, wq[:, :, swap], turned("Wk"), turned("Wv"), turned("Wo")], 2),
        "w1": turned("W1"),
        "w2": turned("W2").reshape(LAYERS, NF, P, D).transpose(0, 2, 1, 3),
        "vc": np.stack(rows, 2),
        "vb": np.broadcast_to(np.stack([a["L0_attn_" + n] for n in ("bv", "bo", "b2")], 1)[:, None],
                              (LAYERS, P, 3, D)),
        "wt": a["L0_ffn_W"].T,
        "fb": a["L0_ffn_b"],
        "ld": a["L0_ffn_lora_down"].T,
        "da": a["L0_ffn_down_aux"],
        "lu": a["L0_ffn_lora_up"].T,
        "ua": a["L0_ffn_up_aux"].T,
        "rot": queries,
        "pos": keys,
        "qkv1": qkv1,
        "wo1": wo1,
        "gate": a["L1_ffn_gate_w"].T,
        "moe": moe,
    }
    nc = bacc.Bacc("TRN2", target_bir_lowering=False, num_devices=1)
    feeds, args = {}, []
    for name, array in arrays.items():
        array = np.ascontiguousarray(array)
        feeds[f"in_{name}"] = array
        args.append(nc.dram_tensor(f"in_{name}", array.shape, mybir.dt.from_np(array.dtype),
                                   kind="ExternalInput").ap())
    args.append(nc.dram_tensor("out", [T, D], F32, kind="ExternalOutput").ap())
    build(nc, *args)
    r = run_bass_kernel_spmd(nc, [feeds], core_ids=[0])
    return r.results[0]["out"].reshape(NB, S, D)
```

```python
from contextlib import ExitStack

import numpy as np
import concourse.bass as bass
from concourse import mybir

F32 = mybir.dt.float32
BF16 = mybir.dt.bfloat16
ALU = mybir.AluOpType
ACT = mybir.ActivationFunctionType
AX_X = mybir.AxisListType.X

P = 128
NB, S, D = 2, 1024, 128
T = NB * S
NT = T // P
CH = 512
NC = T // CH
TPC = CH // P
LAYERS, H0, HD0, FF = 4, 16, 8, 512
NTB, CB = NT // NB, NC // NB
GH = 4
NG = NB * H0 // GH
GPB = NG // NB
NF = FF // P
TERMS = [(0, 0), (0, 1), (0, 2), (1, 0), (1, 1), (2, 0)]
HALF = len(TERMS) * HD0
KROWS = 2 * HALF
KMAX = KROWS + 2
SB_ = S // P
SCALE0 = HD0 ** -0.5
NEG = -1.0e30

H1, HD1 = 16, 64
KFULL = 96
SCALE1 = HD1 ** -0.5
NE, INTER, SHARED = 8, 176, 352
HID = NE * INTER + SHARED
NHC = -(-HID // P)

LORA_R, LORA_D, LORA_U = 4, 100, 50

WQ, WQS, WK, WV, WO = range(5)
VC = ["bq", "bqs", "u", "us", "bk", "ln1w", "ln1b", "ln2w", "ln2b", "b1_0", "b1_1", "b1_2", "b1_3"]
COL = {n: i for i, n in enumerate(VC)}
NVC = len(VC)
VB = {"bv": 0, "bo": 1, "b2": 2}

SB_ = S // P
STEPS = [(c, jb, max(c * CH, jb * P), (c + 1) * CH - max(c * CH, jb * P))
         for c in range(S // CH) for jb in range((c + 1) * TPC)]
NS = len(STEPS)
DIAG = [jb * P >= c * CH for c, jb, _, _ in STEPS]
C_END = [max(s for s in range(NS) if STEPS[s][0] == c) for c in range(S // CH)]
ATILES = [(ib, k0, min((ib + 1) * P - k0, CH), (ib + 1) * P - k0 <= CH)
          for ib in range(SB_) for k0 in range(0, (ib + 1) * P, CH)]

LAG = 2
SLOTS = NS + LAG
A_LIST = [(r, *a) for a in ATILES for r in range(GH)]
NA = len(A_LIST)
A_PER = 4
T_SLOT = [C_END[0] + LAG + 2, SLOTS - 1]
M_SLOT = -(-NA // A_PER) - 1


def group_items(last):
    out = []
    for slot in range(SLOTS):
        if not last:
            out += [(slot, "A", i) for i in range(slot * A_PER, min((slot + 1) * A_PER, NA))]
            if slot == M_SLOT:
                out.append((slot, "M", 0))
        out += [(slot, "T", c) for c in range(S // CH) if T_SLOT[c] == slot]
    return out


V_LN, V_PROJ, V_A = NC, 3 * NC, NA + 1
V_GROUP = V_A + S // CH
V_ATT = V_A + (NG - 1) * V_GROUP + S // CH
V_LAYER = V_LN + V_PROJ + V_ATT + 4 * NC
V_START = 2 * NC + 3
LN_AT = [b * 3 * CB + x for b in range(NB) for x in range(CB)]
Q_AT = [b * 3 * CB + CB + 2 * x for b in range(NB) for x in range(CB)]
X_AT = [b * 2 * CB + x for b in range(NB) for x in range(CB)]
O_AT = [b * 2 * CB + CB + x for b in range(NB) for x in range(CB)]
V_G0 = V_LN + V_PROJ + V_A
V_POST = V_LN + V_PROJ + V_ATT
A_K, A_B, A_G = NC // 2, NS * GH // 2, 2 * NF
A_LAYER = A_K + NG * A_B + A_G
USES = [len(range(u, NG, 3)) for u in range(3)]

STEPS1 = [[(b, ib) for b in range(NB)] for ib in range(TPC)] + [[(b, ib)] for b in range(NB) for ib in range(TPC, SB_)]
NS1 = len(STEPS1)
BUF1 = 3
LAG_T, LAG_V = 2, 3
V_TILES = CH // HD1
V1_PROJ = NC + NT // V_TILES
P_SLOT = LAG_V
HALVES = S // CH
POST1 = {("X", 0): 7, ("Y", 0): 8, ("X", HALVES): 9, ("Y", HALVES): 10, ("X", 1): 11, ("Y", 1): 12,
         ("X", HALVES + 1): 15, ("Y", HALVES + 1): 16}
X_BUF = {0: 0, HALVES: 1, 1: 0, HALVES + 1: 1}


def blocks1(n):
    return [(b, kb, (i * TPC + kb) * P) for i, (b, ib) in enumerate(STEPS1[n]) for kb in range(ib + 1)]


def pair_items(first, last):
    out = []
    for u in range(2):
        for slot in range(NS1 + (max(POST1.values()) + 1 - NS1 if last and u else 0)):
            def step(lag):
                n = slot - lag
                return None if n >= NS1 or (n < 0 and first and not u) else (u - (n < 0), n % NS1)
            t, v = step(LAG_T), step(LAG_V)
            banks = [] if t is None else [("T", t[0], (t[1], x)) for x in range(-(-len(blocks1(t[1])) // TPC))]
            out += banks[:1]
            if slot < NS1:
                out.append(("S", u, slot))
            out += banks[1:]
            if v is not None:
                out.append(("V", v[0], v[1]))
            if P_SLOT <= slot < P_SLOT + V1_PROJ and not (last and u):
                out.append(("P", u, slot - P_SLOT))
            for (kind, c), at_ in POST1.items():
                if u and slot == at_ or not u and not first and slot + NS1 == at_:
                    out.append((kind, u - (slot + NS1 == at_ and not u), c))
    return out


def vec_only(items):
    return [x for x in items if x[0] != "S"]


def place(first, last, kind, u, which):
    own, before = vec_only(pair_items(first, last)), vec_only(pair_items(False, False))
    if (kind, u, which) in own:
        return own.index((kind, u, which))
    return before.index((kind, u + 2, which)) - len(before)


V_R = V_START + LAYERS * V_LAYER
V_MOE = V_R + NC + 1 + NC
MOE_J = 2 * NC
MOE_TURNS = NHC // 2
assert NE + 1 <= 32
MOE_V = 2 * MOE_J
V_H = V_MOE + MOE_TURNS * MOE_V
V_P0 = V_H + V1_PROJ
V_P1 = V_P0 + len(vec_only(pair_items(True, False)))
V_PAIR = len(vec_only(pair_items(False, False)))
A_MOE = LAYERS * A_LAYER
A_H = A_MOE + MOE_TURNS * MOE_J
PV0 = 3 + LAYERS * NG * NS
CX0 = 2 + LAYERS * NG * (S // CH)
assert V_PAIR % 2 == 0 and NS1 % BUF1 == 0 and P_SLOT + V1_PROJ <= NS1 and M_SLOT < SLOTS
assert len(group_items(False)) == V_GROUP and V_LAYER % 2 == 0 and A_LAYER % 2 == 0


def at(items, kind, which):
    return [i for i, (_, k, w) in enumerate(items) if (k, w) == (kind, which)][0]


def m_item(g):
    return V_G0 - 1 if g == 0 else V_G0 + (g - 1) * V_GROUP + at(group_items(False), "M", 0)


def t_item(g, c):
    return V_G0 + g * V_GROUP + at(group_items(g == NG - 1), "T", c)


LN_LAST = "last"
N_ROUTE = 31


def down_at(j):
    return 2 * j + 2 if j < MOE_J - 1 else 2 * MOE_J - 1


def up_at(j):
    return max(2 * j - 1, 0)


def build(nc, x_d, wa_d, w1_d, w2_d, vc_d, vb_d, wt_d, fb_d, ld_d, da_d, lu_d, ua_d, rot_d, pos_d,
          qkv1_d, wo1_d, gate_d, moe_d, out_d):
    q_scr = nc.dram_tensor("q_scr", [NB, H0, KROWS, S], BF16, kind="Internal").ap()
    k_scr = nc.dram_tensor("k_scr", [NB, H0, HALF, S], BF16, kind="Internal").ap()
    p_scr = nc.dram_tensor("p_scr", [3, HD0, S], BF16, kind="Internal").ap()

    with ExitStack() as ctx:
        def sb(name, shape, dt=F32):
            return ctx.enter_context(nc.sbuf_tensor(name, shape, dt))

        def sem(name):
            return ctx.enter_context(nc.semaphore(name))

        vecb = [ctx.enter_context(nc.psum_tensor(f"vecb{i}", [P, CH], F32)) for i in range(2)]
        actb = [ctx.enter_context(nc.psum_tensor(f"actb{i}", [P, 2, CH], F32)) for i in range(2)]
        ctxb = ctx.enter_context(nc.psum_tensor("ctxb", [P, 2, CH], F32))

        h = sb("h", [P, NT, D])
        res = sb("res", [P, NT, D])
        xn = sb("xn", [P, NT, D])
        xnT = sb("xnT", [P, T])
        vtok = sb("vtok", [P, NT, D])
        att = sb("att", [P, NT, D])
        big = sb("big", [P, 4 * T])
        kst = sb("kst", [P, 3, GH, S], BF16)
        pbuf = sb("pbuf", [P, 3 * GH * CH])
        kp = sb("kp", [P, 3, T], BF16)
        vst = sb("vst", [P, 2, SB_, GH, 32])
        rot = sb("rot", [P, 2, S])
        osb = sb("osb", [P, 2, CH])
        wa = sb("wa", [P, 5, D])
        w1 = sb("w1", [P, FF])
        w2 = sb("w2", [P, NF, D])
        vc = sb("vc", [P, NVC])
        vb = sb("vb", [P, 3, D])
        bu = sb("bu", [P, 2])
        ident = sb("ident", [P, P])
        amask = sb("amask", [P, CH])
        identb = sb("identb", [P, P], BF16)
        bmask = sb("bmask", [P, P], BF16)
        half = sb("half", [P, NT])
        stats = sb("stats", [P, NT, 6])
        mv = sb("mv", [P, NT, 2])
        vare = sb("vare", [P, NT])
        rstd = sb("rstd", [P, NT])
        mxa = sb("mxa", [P, GH, SB_])
        mxb = sb("mxb", [P, GH, SB_ - TPC])
        nm = sb("nm", [GH * SB_, 2, P], BF16)
        rz = sb("rz", [P, TPC, GH])
        lw = sb("lw", [P, 3, D])
        lws = sb("lws", [P, LORA_R + LORA_U + D])
        nmax = sb("nmax", [P, NS1, NB])
        zsum = sb("zsum", [P, NS1, NB])
        wt9 = sb("wt9", [P, NT, NE + 1])
        wtb = sb("wtb", [P, NT, 3, 32], BF16)
        wtf = sb("wtf", [P, NT, 3, 32])
        ownb = sb("ownb", [KFULL, 2, P], BF16)

        hid = big[:, :].rearrange("p (m t) -> p m t", m=NF)
        rtmp, kf = hid[:, 2, :], hid[:, 3, :]
        qf = xn[:, :, :].rearrange("p t d -> p (t d)")
        rf = att[:, :, :].rearrange("p t d -> p (t d)")
        qst = big[:, 0:3 * GH * S // 2].bitcast(BF16).rearrange("p (u h t) -> p u h t", u=3, h=GH)
        prob = pbuf[:, :].rearrange("p (u h t) -> p u h t", u=3, h=GH)
        pparts = pbuf[:, :].bitcast(BF16).rearrange("p (x k t) -> p x k t", x=2, k=3)
        parts = {"k": kp[:, :, :], "q": pparts[:, 0], "r": pparts[:, 1]}
        whole = {"k": kf, "q": qf, "r": rf}
        mw = vst[:, :, :, :, :].rearrange("p u a b c -> p (u a b c)")[:, 0:2 * 4 * P].rearrange("p (u d) -> p u d", u=2)
        wT = kst[0:KFULL, 2, 0:T // S, :].rearrange("p u t -> p (u t)")
        moeb = pbuf[:, 0:6 * CH].rearrange("p (x u t) -> p x u t", x=3, u=2)
        prob1 = pbuf[:, 0:BUF1 * S].rearrange("p (u t) -> p u t", u=BUF1)
        probT = pbuf[:, BUF1 * S:2 * BUF1 * S].rearrange("p (u t) -> p u t", u=BUF1)
        pairs = [actb[0], actb[1], ctxb]
        vh = [vtok[:, :, :], xn[:, :, :]]
        wr = kst[:, :, :, :].rearrange("p u h t -> p (u h t)").bitcast(F32)[:, 0:14 * NT * NE]\
            .rearrange("p (k t e) -> p k t e", k=14, t=NT)

        names = {}

        def s(name):
            if name not in names:
                names[name] = sem(name)
            return names[name]

        def vec_read(idx):
            return idx + 3

        act_read = vec_read

        def ln_count(n, b):
            return NB * 2 * LAYERS + 3 + b if n is LN_LAST else NB * n + b

        def alone(eng, name):
            eng.sem_inc(s(name), 1)

        block = ctx.enter_context(nc.Block())

        UNITS = [(b, w) for b in range(NB) for w in ("k", "q", "r")]
        NU, NW = len(UNITS), len(UNITS) // NB
        SCR = 3 * len(TERMS)

        def split(eng, l, b):
            col = slice(b * S, (b + 1) * S)
            for n in range(NW + 1):
                if n < NW:
                    w = UNITS[n][1]
                    eng.wait_ge(s("part1"), l * NU + b * NW + n + 1)
                    eng.tensor_tensor(whole[w][:, col], whole[w][:, col], parts[w][:, 0, col],
                                      ALU.subtract).then_inc(s(f"remainder{b}"), 1)
                if n:
                    w = UNITS[n - 1][1]
                    eng.wait_ge(s("part2"), l * NU + b * NW + n)
                    eng.tensor_tensor(parts[w][:, 2, col], whole[w][:, col], parts[w][:, 1, col],
                                      ALU.subtract).then_inc(s(f"part3_{b}"), 1)

        POS_DMAS = 1 + 3 * GH * len(TERMS)

        @block.sync
        def _(sp):
            def load(dst, src, name):
                sp.dma_start(dst, src).then_inc(s(name), 16)

            tok = "(t p) d -> p t d"
            load(h[:, :, :], x_d.rearrange(tok, p=P), "x_in")
            load(res[:, :, :], x_d.rearrange(tok, p=P), "res_in")
            load(kf[0:HD0, 0:S], pos_d, "pos_in")
            for dst, src in ((vc[:, :], vc_d), (wa[:, :, :], wa_d), (w1[:, :], w1_d)):
                load(dst, src[0], "weights_in")
            load(rot[:, :, :], rot_d, "rot_in")
            load(lws[0:LORA_D, 0:LORA_R], ld_d, "lora_in")
            load(lws[0:LORA_R, LORA_R:LORA_R + LORA_U], lu_d, "lora_in")
            load(lws[0:LORA_U, LORA_R + LORA_U:], ua_d, "lora_in")
            load(lw[0:LORA_D, 0, :], da_d, "lora_in")
            load(w2[:, 0, :], wt_d, "lora_in")
            load(vb[:, 0, :], fb_d.partition_broadcast(P), "lora_in")
            sp.wait_ge(s("pos_part3"), 1)
            load(p_scr.rearrange("k d t -> d k t"), kp[0:HD0, :, 0:S], "pos_out")
            sp.wait_ge(s("pos_out"), 16)
            for t, (_, kpart) in enumerate(TERMS):
                for u in range(3):
                    for r in range(GH):
                        load(kst[t * HD0:(t + 1) * HD0, u, r, :], p_scr[kpart], "pos_in")

            def stack_load(g):
                u, (b, hg) = g % 3, divmod(g, GPB)
                hs = slice(hg * GH, (hg + 1) * GH)
                load(qst[0:KROWS, u], q_scr[b, hs].rearrange("h r t -> r h t"), f"stack_in{u}")
                load(kst[HALF:KROWS, u], k_scr[b, hs].rearrange("h r t -> r h t"), f"stack_in{u}")

            sp.wait_ge(s("vec_read"), V_START + 2)
            load(vb[:, :, :], vb_d[0], "weights_in")
            load(w2[:, :, :], w2_d[0], "w2_in")

            def next_weights(l):
                sp.wait_ge(s("vec_full"), V_START + l * V_LAYER + V_POST + O_AT[-1] + 1)
                load(wa[:, :, :], wa_d[l + 1], "weights_in")
                sp.wait_ge(s("bias_added"), 2 * l + 2)
                load(vb[:, :, :], vb_d[l + 1], "weights_in")
                sp.wait_ge(s("act_read"), act_read((l + 1) * A_LAYER - 1))
                load(vc[:, :], vc_d[l + 1], "weights_in")
                load(w1[:, :], w1_d[l + 1], "weights_in")
                sp.wait_ge(s("vec_full"), V_START + (l + 1) * V_LAYER)
                load(w2[:, :, :], w2_d[l + 1], "w2_in")

            def layer(l, last):
                for n, (b, w) in enumerate(UNITS):
                    col = slice(b * S, (b + 1) * S)
                    if n == NW:
                        sp.wait_ge(s("scr_out0"), 16 * SCR * (l + 1))
                        for g in range(2):
                            stack_load(g)
                        sp.wait_ge(s("vec_read"), vec_read(V_START + l * V_LAYER + V_LN + 2 * NC - 1))
                        stack_load(2)
                    for part in range(3):
                        if part < 2:
                            sp.wait_ge(s(("part1", "part2")[part]), l * NU + n + 1)
                        else:
                            sp.wait_ge(s(f"part3_{b}"), l * NW + n % NW + 1)
                        for t, (qpart, kpart) in enumerate(TERMS):
                            if (kpart if w == "k" else qpart) == part:
                                row = t * HD0 + (HALF if w == "q" else 0)
                                load((k_scr if w == "k" else q_scr)[b, :, row:row + HD0, :],
                                     parts[w][:, part, col], f"scr_out{b}")
                for g in range(NG):
                    sp.wait_ge(s("vec_read"), vec_read(V_START + l * V_LAYER + m_item(g)))
                    for k in range(2):
                        load(qst[KROWS + k:KROWS + k + 1, g % 3].rearrange("p h (i t) -> p (h i) t", t=P),
                             nm[:, k, :], "maxrow_in")
                    if 1 <= g and g + 2 < NG:
                        sp.wait_ge(s("act_full"), l * A_LAYER + A_K + g * A_B)
                        if g + 2 == GPB:
                            sp.wait_ge(s("scr_out1"), 16 * SCR * (l + 1))
                        stack_load(g + 2)
                if not last:
                    next_weights(l)

            with sp.Fori(0, LAYERS - 1) as l:
                layer(l, False)
            layer(LAYERS - 1, True)

            sp.wait_ge(s("vec_read"), vec_read(V_R - 1))
            load(vc[:, 0:NE], gate_d, "gate_in")
            for u in range(2):
                load(mw[:, u, :], moe_d[u], f"moe_in{u}")
            with sp.Fori(1, MOE_TURNS) as i:
                for u in range(2):
                    sp.wait_ge(s("vec_full"), V_MOE + (i - 1) * MOE_V + down_at((u + 1) * NC - 1) + 1)
                    load(mw[:, u, :], moe_d[i * 2 + u], f"moe_in{u}")

            def head_weights(hd, par):
                load(w1[:, par * 3 * HD1:(par + 1) * 3 * HD1], qkv1_d[hd], f"head_in{par}")

            def pair_weights(j, base, first, last):
                for u in range(2):
                    if not last:
                        sp.wait_ge(s("vec_full"), V_P0 if first and not u else
                                   base + place(first, last, "P", u - 1, V1_PROJ - 1) + 1)
                        head_weights(2 * j + u + 2, u)
                    if not u:
                        if not first:
                            sp.wait_ge(s("vec_full"), base + place(first, last, "Y", -1, HALVES + 1) + 1)
                        load(wa[:, 0, :], wo1_d[j], "wo_in")

            for u in range(2):
                head_weights(u, u)
            pair_weights(0, V_P0, True, False)
            with sp.Fori(1, H1 // 2 - 1) as j:
                pair_weights(j, V_P1 + (j - 1) * V_PAIR, False, False)
            pair_weights(H1 // 2 - 1, V_P1 + (H1 // 2 - 2) * V_PAIR, False, True)
            sp.wait_ge(s("vec_read"), vec_read(V_P1 + (H1 // 2 - 2) * V_PAIR + len(vec_only(pair_items(False, True))) - 1))
            load(out_d.rearrange(tok, p=P), res[:, :, :], "out_done")
            sp.wait_ge(s("out_done"), 16)

        @block.gpsimd
        def _(pool):
            pool.memset(ident[:, :], 0.0).then_inc(s("pool_zero"), 1)
            pool.memset(amask[:, :], 0.0).then_inc(s("pool_zero"), 1)
            pool.memset(vst[:, :, :, :, :], 0.0).then_inc(s("pool_zero"), 1)
            pool.memset(half[:, :], -0.5).then_inc(s("half_set"), 1)
            pool.memset(identb[:, :], 0.0).then_inc(s("pool_zero"), 1)
            pool.memset(bmask[:, :], 0.0).then_inc(s("pool_zero"), 1)
            pool.wait_ge(s("pool_zero"), 5)
            pool.affine_select(out=identb[:, :], in_=identb[:, :], compare_op=ALU.not_equal, fill=1.0, base=0,
                               pattern=[[-1, P]], channel_multiplier=1).then_inc(s("ident_set"), 1)
            pool.affine_select(out=bmask[:, :], in_=bmask[:, :], compare_op=ALU.is_ge, fill=NEG, base=0,
                               pattern=[[1, P]], channel_multiplier=-1).then_inc(s("ident_set"), 1)
            pool.affine_select(out=ident[:, :], in_=ident[:, :], compare_op=ALU.not_equal, fill=1.0, base=0,
                               pattern=[[-1, P]], channel_multiplier=1).then_inc(s("ident_set"), 1)
            pool.affine_select(out=amask[:, CH - P:CH], in_=amask[:, CH - P:CH], compare_op=ALU.is_ge, fill=NEG,
                               base=0, pattern=[[-1, P]], channel_multiplier=1).then_inc(s("amask_set"), 1)
            pool.memset(vst[:, :, :, :, HD0:HD0 + 1].rearrange("p u a h o -> p (u a h) o"), 1.0)\
                .then_inc(s("ones_set"), 1)
            pool.wait_ge(s("half_set"), 1)

            def ln_rstd(n, b, eps):
                k, tiles = ln_count(n, b), slice(b * NTB, (b + 1) * NTB)
                pool.wait_ge(s("ln_aggr"), NTB * (k + 1))
                alone(pool, "pool_seen")
                pool.tensor_scalar(vare[:, tiles], mv[:, tiles, 1], eps, None, ALU.add).then_inc(s("ln_eps"), 1)
                pool.wait_ge(s("ln_eps"), k + 1)
                pool.tensor_tensor(rstd[:, tiles], vare[:, tiles], half[:, tiles], ALU.pow)\
                    .then_inc(s("ln_rstd"), 1)

            for b in range(NB):
                ln_rstd(0, b, 1e-5)
            ln_rstd(1, 0, 1e-6)
            pool.wait_ge(s("pos_part1"), 1)
            pool.tensor_tensor(kf[0:HD0, 0:S], kf[0:HD0, 0:S], kp[0:HD0, 0, 0:S],
                               ALU.subtract).then_inc(s("pos_remainder"), 1)
            pool.wait_ge(s("pos_part2"), 1)
            pool.tensor_tensor(kp[0:HD0, 2, 0:S], kf[0:HD0, 0:S], kp[0:HD0, 1, 0:S],
                               ALU.subtract).then_inc(s("pos_part3"), 1)

            with pool.Fori(0, LAYERS) as l:
                ln_rstd(1 + 2 * l, 1, 1e-6)
                split(pool, l, 1)

                def add_row(which, n_ln):
                    pool.wait_ge(s("ln_xn"), NT * (n_ln + 1))
                    row = vb[:, which:which + 1, :].to_broadcast([P, NT, D])
                    pool.tensor_tensor(h[:, :, :], h[:, :, :], row, ALU.add).then_inc(s("bias_added"), 1)

                def stage_v(g):
                    b, hg = divmod(g, GPB)
                    pool.wait_ge(s("prob_read"), 3 + (l * NG + max(g - 1, 0)) * NS)
                    alone(pool, "pool_seen")
                    src = vtok[:, b * SB_:(b + 1) * SB_, hg * GH * HD0:(hg + 1) * GH * HD0]
                    pool.tensor_copy(vst[:, g % 2, :, :, 0:HD0],
                                     src.rearrange("p t (h d) -> p t h d", h=GH)).then_inc(s("vst_ready"), 1)

                pool.wait_ge(s("vec_read"), vec_read(V_START + l * V_LAYER + V_LN + V_PROJ - 1))
                for g in range(2):
                    stage_v(g)
                pool.wait_ge(s("weights_in"), 64 * (l + 1))
                add_row(VB["bo"], 1 + 2 * l)
                for g in range(2, NG):
                    stage_v(g)
                for b in range(NB):
                    ln_rstd(2 + 2 * l, b, 1e-6)
                add_row(VB["b2"], 2 + 2 * l)
                ln_rstd(3 + 2 * l, 0, 1e-6)
            for b in range(NB):
                ln_rstd(LN_LAST, b, 1e-5)

            with pool.Fori(0, MOE_TURNS) as i:
                for u in range(2):
                    pool.wait_ge(s(f"moe_in{u}"), 16 * (i + 1))
                    pool.wait_ge(s("act_full"), A_MOE + i * MOE_J - (1 - u) * NC)
                    alone(pool, "pool_seen")
                    pool.tensor_copy(ownb[:, u, :], mw[0:KFULL, u, 3 * P:4 * P]).then_inc(s("owner_ready"), 1)

        @block.scalar
        def _(act):
            act.sem_inc(s("act_read"), 2)
            act.sem_inc(s("ctx_read"), 2)
            act.wait_ge(s("pos_in"), 16)
            act.activation(kp[0:HD0, 0, 0:S], kf[0:HD0, 0:S], ACT.Copy).then_inc(s("pos_part1"), 1)
            act.wait_ge(s("pos_remainder"), 1)
            act.activation(kp[0:HD0, 1, 0:S], kf[0:HD0, 0:S], ACT.Copy).then_inc(s("pos_part2"), 1)
            act.wait_ge(s("pos_out"), 16)

            with act.Fori(0, LAYERS) as l:
                base = l * A_LAYER
                vbase = V_START + l * V_LAYER
                act.wait_ge(s("weights_in"), 64 * (l + 1))
                def first_part(b, w):
                    col = slice(b * S, (b + 1) * S)
                    if w == "k":
                        act.wait_ge(s("act_full"), base + b + 1)
                        act.activation(kf[:, col], actb[b % 2][:, :, :].rearrange("p a t -> p (a t)"),
                                       ACT.Identity, bias=vc[:, COL["bk"]:COL["bk"] + 1])\
                            .then_inc(s("act_read"), 1)
                        act.wait_ge(s("act_read"), act_read(base + b))
                    else:
                        act.wait_ge(s("vec_read"), vec_read(vbase + Q_AT[(b + 1) * CB - 1] + 1))
                    act.activation(parts[w][:, 0, col], whole[w][:, col], ACT.Copy).then_inc(s("part1"), 1)

                def second_part(n):
                    b, w = UNITS[n]
                    col = slice(b * S, (b + 1) * S)
                    act.wait_ge(s(f"remainder{b}"), l * NW + n % NW + 1)
                    act.activation(parts[w][:, 1, col], whole[w][:, col], ACT.Copy).then_inc(s("part2"), 1)

                for n in range(NU):
                    first_part(*UNITS[n])
                    if n % NW:
                        second_part(n - 1)
                    if n % NW == NW - 1:
                        second_part(n)

                act.wait_ge(s("scr_out1"), 16 * SCR * (l + 1))
                for g in range(NG):
                    def evacuate(c):
                        act.wait_ge(s("prob_read"), 3 + (l * NG + g) * NS + C_END[c] + 1)
                        if g:
                            act.wait_ge(s("vec_full"), vbase + t_item(g - 1, c) + 1)
                        act.activation(osb[:, c, :], ctxb[:, c, :], ACT.Copy).then_inc(s("ctx_read"), 1)

                    for st, (c, jb, i0, w) in enumerate(STEPS):
                        act.wait_ge(s("prob_read"), (l * NG + g) * NS + st + 1)
                        for pr in range(GH // 2):
                            k = A_K + g * A_B + st * (GH // 2) + pr
                            act.wait_ge(s("act_full"), base + k + 1)
                            act.activation(prob[:, (g * NS + st) % 3, 2 * pr:2 * pr + 2, 0:w],
                                           actb[k % 2][:, :, 0:w], ACT.Exp, scale=SCALE0).then_inc(s("act_read"), 1)
                        if st == C_END[0] + LAG:
                            evacuate(0)
                    evacuate(1)

                for n in range(A_G):
                    cp, m = divmod(n, NF)
                    k = A_K + NG * A_B + n
                    act.wait_ge(s("act_full"), base + k + 1)
                    act.activation(hid[:, m, cp * 2 * CH:(cp + 1) * 2 * CH],
                                   actb[k % 2][:, :, :].rearrange("p a t -> p (a t)"), ACT.Gelu,
                                   bias=vc[:, COL["b1_0"] + m:COL["b1_0"] + m + 1]).then_inc(s("act_read"), 1)

            act.wait_ge(s("route"), 3)
            act.activation(wr[:, 1], wr[:, 1], ACT.Exp).then_inc(s("route_exp"), 1)
            with act.Fori(0, MOE_TURNS) as i:
                for j in range(MOE_J):
                    act.wait_ge(s("act_full"), A_MOE + i * MOE_J + j + 1)
                    act.activation(moeb[:, 0, j % 2, :], actb[j % 2][:, 0, :], ACT.Silu).then_inc(s("silu"), 1)
                    act.activation(moeb[:, 1, j % 2, :], actb[j % 2][:, 1, :], ACT.Copy).then_inc(s("act_read"), 1)

            def pair_exp(j, base, first, last):
                for kind, u, n in pair_items(first, last):
                    if kind != "S":
                        continue
                    k = (2 * j + u) * NS1 + n
                    act.wait_ge(s("max1_ready"), k + 1)
                    if n >= BUF1 or u or not first:
                        un, m = u - (n < BUF1), (n - BUF1) % NS1
                        x = -(-len(blocks1(m)) // TPC) - 1
                        act.wait_ge(s("vec_full"), base + place(first, last, "T", un, (m, x)) + 1)
                    if u or not first:
                        act.wait_ge(s("vec_read"), vec_read(base + place(first, last, "V", u - 1, n)))
                    src, dst = pairs[n % BUF1][:, :, :].rearrange("p u t -> p (u t)"), prob1[:, n % BUF1, :]
                    for i, (b, ib) in enumerate(STEPS1[n]):
                        col = slice(i * CH, i * CH + (ib + 1) * P)
                        ins = act.activation(dst[:, col], src[:, col], ACT.Exp, bias=nmax[:, n, i:i + 1],
                                             accum_out=zsum[:, n, i:i + 1])
                    ins.then_inc(s("act_read"), 1)

            pair_exp(0, V_P0, True, False)
            with act.Fori(1, H1 // 2 - 1) as j:
                pair_exp(j, V_P1 + (j - 1) * V_PAIR, False, False)
            pair_exp(H1 // 2 - 1, V_P1 + (H1 // 2 - 2) * V_PAIR, False, True)

        @block.tensor
        def _(pe):
            pe.sem_inc(s("prob_read"), 3)
            pe.wait_ge(s("ident_set"), 3)

            def vec_bank(idx, par):
                pe.wait_ge(s("vec_read"), idx + 1)
                return vecb[par % 2]

            def transposes(idx, par, src, c, n_ln):
                pe.wait_ge(s("ln_xn"), NTB * ln_count(n_ln, 0) + TPC * (c + 1))
                bank = vec_bank(idx, par)
                for j in range(TPC):
                    mm = pe.transpose(bank[:, j * P:(j + 1) * P], src[:, c * TPC + j, :], ident[:, :])
                mm.then_inc(s("vec_full"), 1)

            def add_mask(scores):
                return pe.matmul(scores, identb[:, :], bmask[:, :], start=False, stop=True)

            for c in range(NC):
                transposes(c, c, h, c, 0)
            pe.wait_ge(s("lora_in"), 96)
            k = NC
            bank = vec_bank(k, k)
            pe.matmul(bank[0:LORA_R, 0:D], lws[0:LORA_D, 0:LORA_R], lw[0:LORA_D, 0, :], start=True,
                      stop=True).then_inc(s("vec_full"), 1)
            bank = vec_bank(k + 1, k + 1)
            pe.wait_ge(s("vec_read"), vec_read(k))
            pe.matmul(bank[0:LORA_U, 0:D], lws[0:LORA_R, LORA_R:LORA_R + LORA_U], lw[0:LORA_R, 1, :], start=True,
                      stop=True).then_inc(s("vec_full"), 1)
            bank = vec_bank(k + 2, k + 2)
            pe.wait_ge(s("vec_read"), vec_read(k + 1))
            pe.matmul(bank[:, 0:D], lw[0:LORA_U, 2, :], lws[0:LORA_U, LORA_R + LORA_U:], start=True,
                      stop=True).then_inc(s("vec_full"), 1)
            pe.wait_ge(s("vec_read"), vec_read(k + 2))
            for c in range(NC):
                idx = k + 3 + c
                bank = vec_bank(idx, idx)
                for j in range(TPC):
                    t = c * TPC + j
                    mm = pe.matmul(bank[:, j * P:(j + 1) * P], xnT[:, t * P:(t + 1) * P], lw[:, 0, :],
                                   start=True, stop=True)
                mm.then_inc(s("vec_full"), 1)
            pe.wait_ge(s("pos_in"), 16 * POS_DMAS)
            pe.wait_ge(s("ones_set"), 2)

            with pe.Fori(0, LAYERS) as l:
                vbase = V_START + l * V_LAYER
                abase = l * A_LAYER

                def vbank(k):
                    return vec_bank(vbase + k, V_START + k)

                def dense(k, w, c):
                    bank = vbank(k)
                    pe.matmul(bank[:, :], w, xnT[:, c * CH:(c + 1) * CH], start=True,
                              stop=True).then_inc(s("vec_full"), 1)

                pe.wait_ge(s("weights_in"), 64 * (l + 1))
                for b in range(NB):
                    for c in range(b * CB, (b + 1) * CB):
                        transposes(vbase + LN_AT[c], V_START + LN_AT[c], xn, c, 1 + 2 * l)
                    pe.wait_ge(s("vec_read"), vec_read(vbase + LN_AT[c]))
                    pe.wait_ge(s("act_read"), abase + b + 1)
                    for x in range(CB):
                        c = b * CB + x
                        mm = pe.matmul(actb[b % 2][:, x, :], wa[:, WK, :], xnT[:, c * CH:(c + 1) * CH],
                                       start=True, stop=True)
                    mm.then_inc(s("act_full"), 1)
                    for c in range(b * CB, (b + 1) * CB):
                        dense(Q_AT[c], wa[:, WQ, :], c)
                        dense(Q_AT[c] + 1, wa[:, WQS, :], c)
                for c in range(NC):
                    bank = vbank(V_LN + 2 * NC + c)
                    for j in range(TPC):
                        t = c * TPC + j
                        mm = pe.matmul(bank[:, j * P:(j + 1) * P], xnT[:, t * P:(t + 1) * P], wa[:, WV, :],
                                       start=True, stop=True)
                    mm.then_inc(s("vec_full"), 1)

                def pass_a(g, k, i):
                    r, ib, k0, w, _ = A_LIST[i]
                    if i == 0:
                        pe.wait_ge(s(f"stack_in{g % 3}"), 32 * (l * USES[g % 3] + g // 3 + 1))
                    bank = vbank(k)
                    pe.matmul(bank[:, 0:w], qst[0:KROWS, g % 3, r, ib * P:(ib + 1) * P],
                              kst[0:KROWS, g % 3, r, k0:k0 + w], start=True, stop=True).then_inc(s("vec_full"), 1)

                def maxima(g, k):
                    bank = vbank(k)
                    pe.wait_ge(s("max_ready"), l * NG + g + 1)
                    pe.transpose(bank[0:GH * SB_, 0:P], mxa[:, :, :].rearrange("p h i -> p (h i)"),
                                 ident[:, :]).then_inc(s("vec_full"), 1)

                def pass_b(g, st, pr):
                    c, jb, i0, w = STEPS[st]
                    if st == 0 and pr == 0:
                        pe.wait_ge(s("maxrow_in"), 32 * (l * NG + g + 1))
                    if True:
                        k = A_K + g * A_B + st * (GH // 2) + pr
                        pe.wait_ge(s("act_read"), abase + k + 1)
                        for x in range(2):
                            r = 2 * pr + x
                            mm = pe.matmul(actb[k % 2][:, x, 0:w], kst[0:KMAX, g % 3, r, jb * P:(jb + 1) * P],
                                           qst[0:KMAX, g % 3, r, i0:i0 + w], start=True, stop=not DIAG[st])
                            if DIAG[st]:
                                mm = add_mask(actb[k % 2][:, x, 0:P])
                        mm.then_inc(s("act_full"), 1)

                def pv(g, st):
                    c, jb, i0, w = STEPS[st]
                    if st == 0:
                        pe.wait_ge(s("vst_ready"), l * NG + g + 1)
                    if jb == 0:
                        pe.wait_ge(s("ctx_read"), (l * NG + g) * (S // CH) + c + 1)
                    pe.wait_ge(s("act_read"), act_read(abase + A_K + g * A_B + 2 * st + 1))
                    for r in range(GH):
                        mm = pe.matmul(ctxb[32 * r:32 * r + 32, c, i0 - c * CH:CH], vst[:, g % 2, jb, r, :],
                                       prob[:, (g * NS + st) % 3, r, 0:w], start=(jb == 0), stop=(st == C_END[c]))
                    mm.then_inc(s("prob_read"), 1)

                def turn(g, k, c):
                    bank = vbank(k)
                    pe.wait_ge(s("ctx_read"), 2 + (l * NG + g) * (S // CH) + c + 1)
                    for j in range(TPC):
                        mm = pe.transpose(bank[:, j * P:(j + 1) * P], osb[:, c, j * P:(j + 1) * P], ident[:, :])
                    mm.then_inc(s("vec_full"), 1)

                for i in range(NA):
                    pass_a(0, V_LN + V_PROJ + i, i)
                maxima(0, V_LN + V_PROJ + NA)
                for g in range(NG):
                    items = group_items(g == NG - 1)
                    for slot in range(SLOTS):
                        vec = [(k, kind, x) for k, (sl, kind, x) in enumerate(items) if sl == slot]

                        def vec_item(n):
                            for k, kind, x in vec[n:n + 1]:
                                k += V_G0 + g * V_GROUP
                                if kind == "A":
                                    pass_a(g + 1, k, x)
                                if kind == "M":
                                    maxima(g + 1, k)
                                if kind == "T":
                                    turn(g, k, x)

                        last_turn = bool(vec) and vec[-1][1:] == ("T", 1)
                        for pr in range(GH // 2):
                            if slot < NS:
                                pass_b(g, slot, pr)
                            vec_item(pr) if not (last_turn and pr == len(vec) - 1) else None
                        early = min(GH // 2, len(vec) - last_turn)
                        if not last_turn:
                            vec_item(2)
                        if slot >= LAG:
                            pv(g, slot - LAG)
                        for n in range(early + (not last_turn), len(vec)):
                            vec_item(n)

                for b in range(NB):
                    for c in range(b * CB, (b + 1) * CB):
                        bank = vbank(V_POST + X_AT[c])
                        if c == 0:
                            pe.wait_ge(s("vec_read"), vec_read(vbase + V_POST - 1))
                        for j in range(TPC):
                            mm = pe.transpose(bank[:, j * P:(j + 1) * P], att[:, c * TPC + j, :], ident[:, :])
                        mm.then_inc(s("vec_full"), 1)
                    for c in range(b * CB, (b + 1) * CB):
                        bank = vbank(V_POST + O_AT[c])
                        pe.wait_ge(s("vec_read"), vec_read(vbase + V_POST + X_AT[c]))
                        for j in range(TPC):
                            t = c * TPC + j
                            mm = pe.matmul(bank[:, j * P:(j + 1) * P], xnT[:, t * P:(t + 1) * P], wa[:, WO, :],
                                           start=True, stop=True)
                        mm.then_inc(s("vec_full"), 1)
                for cp in range(NB):
                    for c in range(cp * CB, (cp + 1) * CB):
                        k = V_POST + 2 * NC + c
                        transposes(vbase + k, V_START + k, xn, c, 2 + 2 * l)
                    pe.wait_ge(s("vec_read"), vec_read(vbase + V_POST + 2 * NC + 2 * cp + 1))
                    for m in range(NF):
                        k = A_K + NG * A_B + cp * NF + m
                        pe.wait_ge(s("act_read"), abase + k + 1)
                        for x in range(2):
                            c = 2 * cp + x
                            mm = pe.matmul(actb[k % 2][:, x, :], w1[:, m * P:(m + 1) * P],
                                           xnT[:, c * CH:(c + 1) * CH], start=True, stop=True)
                        mm.then_inc(s("act_full"), 1)
                for c in range(NC):
                    bank = vbank(V_POST + 3 * NC + c)
                    if c == 0:
                        pe.wait_ge(s("w2_in"), 16 * (l + 1))
                    pe.wait_ge(s("act_read"), act_read(abase + A_K + NG * A_B + (c // 2) * NF + NF - 1))
                    for j in range(TPC):
                        t = c * TPC + j
                        for m in range(NF):
                            mm = pe.matmul(bank[:, j * P:(j + 1) * P], hid[:, m, t * P:(t + 1) * P], w2[:, m, :],
                                           start=(m == 0), stop=(m == NF - 1))
                    mm.then_inc(s("vec_full"), 1)

            for c in range(NC):
                transposes(V_R + c, V_R + c, xn, c, LN_LAST)
            pe.wait_ge(s("vec_read"), vec_read(V_R + NC - 1))
            pe.wait_ge(s("gate_in"), 16)
            bank = vec_bank(V_R + NC, V_R + NC)
            for t in range(NT):
                mm = pe.matmul(bank[:, t * NE:(t + 1) * NE], xnT[:, t * P:(t + 1) * P], vc[:, 0:NE],
                               start=True, stop=True)
            mm.then_inc(s("vec_full"), 1)
            pe.wait_ge(s("route"), N_ROUTE)
            for c in range(NC):
                idx = V_R + NC + 1 + c
                bank = vec_bank(idx, idx)
                for j in range(TPC):
                    mm = pe.transpose(bank[0:KFULL, j * P:(j + 1) * P],
                                      wtf[:, c * TPC + j, :, :].rearrange("p k e -> p (k e)"), ident[:, :])
                mm.then_inc(s("vec_full"), 1)
            pe.wait_ge(s("vec_read"), vec_read(V_MOE - 1))

            with pe.Fori(0, MOE_TURNS) as i:
                def down(j):
                    u, c = divmod(j, NC)
                    k = down_at(j)
                    bank = vec_bank(V_MOE + i * MOE_V + k, V_MOE + k)
                    pe.wait_ge(s("vec_read"), vec_read(V_MOE + i * MOE_V + up_at(j)))
                    for x in range(TPC):
                        mm = pe.matmul(bank[:, x * P:(x + 1) * P], moeb[:, 2, j % 2, x * P:(x + 1) * P],
                                       mw[:, u, 2 * P:3 * P], start=True, stop=True)
                    mm.then_inc(s("vec_full"), 1)

                for j in range(MOE_J):
                    u, c = divmod(j, NC)
                    if c == 0:
                        pe.wait_ge(s(f"moe_in{u}"), 16 * (i + 1))
                    tokens = xnT[:, c * CH:(c + 1) * CH]
                    pe.wait_ge(s("act_read"), A_MOE + i * MOE_J + j + 1)
                    pe.matmul(actb[j % 2][:, 0, :], mw[:, u, 0:P], tokens, start=True, stop=True)
                    if c == 0:
                        pe.wait_ge(s("owner_ready"), i * 2 + u + 1)
                    pe.matmul(actb[j % 2][:, 1, :], ownb[:, u, :], wT[:, c * CH:(c + 1) * CH],
                              start=True, stop=True).then_inc(s("act_full"), 1)
                    k = up_at(j)
                    bank = vec_bank(V_MOE + i * MOE_V + k, V_MOE + k)
                    pe.matmul(bank[:, :], mw[:, u, P:2 * P], tokens, start=True, stop=True)\
                        .then_inc(s("vec_full"), 1)
                    if j:
                        down(j - 1)
                down(MOE_J - 1)

            def project(idx, par_v, par, turn, n):
                wt = w1[:, par * 3 * HD1:(par + 1) * 3 * HD1]
                if n == 0:
                    pe.wait_ge(s(f"head_in{par}"), 16 * (turn + 1))
                bank = vec_bank(idx, par_v)
                if n < NC:
                    mm = pe.matmul(bank[:, :], wt[:, 0:2 * HD1], xnT[:, n * CH:(n + 1) * CH], start=True, stop=True)
                else:
                    for j in range(V_TILES):
                        t = (n - NC) * V_TILES + j
                        mm = pe.matmul(bank[:, j * HD1:(j + 1) * HD1], xnT[:, t * P:(t + 1) * P],
                                       wt[:, 2 * HD1:3 * HD1], start=True, stop=True)
                mm.then_inc(s("vec_full"), 1)

            def scores1(k, par, n):
                pe.wait_ge(s("act_read"), A_H + k + 3 - BUF1)
                pair = pairs[n % BUF1][:, :, :].rearrange("p u t -> p (u t)")
                for i, (b, ib) in enumerate(STEPS1[n]):
                    q = hid[0:KFULL, 2 * par, b * S + ib * P:b * S + (ib + 1) * P]
                    for k0 in range(0, (ib + 1) * P, CH):
                        k1 = min(k0 + CH, (ib + 1) * P)
                        mm = pe.matmul(pair[:, i * CH + k0:i * CH + k1], q, hid[0:KFULL, 2 * par + 1, b * S + k0:b * S + k1],
                                       start=True, stop=k1 <= ib * P)
                    mm = pe.matmul(pair[:, i * CH + ib * P:i * CH + (ib + 1) * P], bmask[:, :], identb[:, :],
                                   start=False, stop=True)
                mm.then_inc(s("act_full"), 1)

            pe.wait_ge(s("zeros1_set"), 1)
            pe.wait_ge(s("ctx_read"), CX0)
            pe.wait_ge(s("act_read"), A_H + 2)
            for n in range(V1_PROJ):
                project(V_H + n, V_H + n, 0, 0, n)

            def pair(j, base, pbase, first, last):
                v = 0
                for kind, u, x in pair_items(first, last):
                    par = u % 2
                    if kind == "S":
                        if x == 0:
                            pe.wait_ge(s("vec_read"), vec_read(V_P0 - 1 if first and not u else
                                                               base + place(first, last, "P", u - 1, NC - 1)))
                        scores1((2 * j + u) * NS1 + x, par, x)
                        continue
                    bank = None if kind == "P" else vec_bank(base + v, pbase + v)
                    if kind == "P":
                        project(base + v, pbase + v, 1 - par, j + u, x)
                    if kind == "T":
                        n, part = x
                        pe.wait_ge(s("act_read"), act_read(A_H + (2 * j + u) * NS1 + n))
                        for i, (_, _, col) in enumerate(blocks1(n)[part * TPC:(part + 1) * TPC]):
                            mm = pe.transpose(bank[:, i * P:(i + 1) * P], prob1[:, n % BUF1, col:col + P], ident[:, :])
                        mm.then_inc(s("vec_full"), 1)
                    if kind == "V":
                        m = -(-len(blocks1(x)) // TPC) - 1
                        pe.wait_ge(s("vec_read"), vec_read(base + place(first, last, "T", u, (x, m))))
                        for i, (b, kb, _) in enumerate(blocks1(x)):
                            slot = [y for y, (bb, _) in enumerate(STEPS1[x]) if bb == b][0]
                            mm = pe.matmul(bank[:, slot * HD1:(slot + 1) * HD1], probT[:, x % BUF1, i * P:(i + 1) * P],
                                           vh[par][:, b * SB_ + kb, 0:HD1], start=(kb == 0),
                                           stop=(kb == STEPS1[x][slot][1]))
                        mm.then_inc(s("vec_full"), 1)
                    if kind == "X":
                        n = [n for n in range(NS1) for b, ib in STEPS1[n] if (b * SB_ + ib) // TPC == x][-1]
                        pe.wait_ge(s("vec_read"), vec_read(base + place(first, last, "V", u, n)))
                        for i in range(TPC):
                            mm = pe.transpose(bank[:, i * P:(i + 1) * P], att[:, x * TPC + i, :], ident[:, :])
                        mm.then_inc(s("vec_full"), 1)
                    if kind == "Y":
                        pe.wait_ge(s("vec_read"), vec_read(base + place(first, last, "X", u, x)))
                        if u > 0:
                            pe.wait_ge(s("wo_in"), 16 * (j + 1))
                        for i in range(TPC):
                            mm = pe.matmul(bank[:, i * P:(i + 1) * P], osb[:, X_BUF[x], i * P:(i + 1) * P], wa[:, 0, :],
                                           start=True, stop=True)
                        mm.then_inc(s("vec_full"), 1)
                    v += 1

            pair(0, V_P0, V_P0, True, False)
            with pe.Fori(1, H1 // 2 - 1) as j:
                pair(j, V_P1 + (j - 1) * V_PAIR, V_P1, False, False)
            pair(H1 // 2 - 1, V_P1 + (H1 // 2 - 2) * V_PAIR, V_P1, False, True)

        @block.vector
        def _(dve):
            dve.sem_inc(s("vec_read"), 2)
            dve.memset(kst[KROWS:KMAX, :, :, :].rearrange("p u h t -> p (u h t)"), 1.0).then_inc(s("ones_set"), 1)

            def full(idx):
                dve.wait_ge(s("vec_full"), idx + 1)

            def own(idx):
                dve.wait_ge(s("vec_read"), idx + 2)

            def ln_stats(n, b, src):
                k, tiles = ln_count(n, b), range(b * NTB, (b + 1) * NTB)
                if not isinstance(n, int) or n or b:
                    dve.wait_ge(s("ln_xn"), NTB * (k - b))
                for t in tiles:
                    dve.bn_stats(stats[:, t, :], src[:, t, :]).then_inc(s("ln_stat"), 1)
                dve.wait_ge(s("ln_stat"), NTB * (k + 1))
                alone(dve, "dve_seen")
                for t in tiles:
                    dve.bn_aggr(mv[:, t, :], stats[:, t, :]).then_inc(s("ln_aggr"), 1)

            def ln_apply(n, b, src, dst):
                dve.wait_ge(s("ln_rstd"), ln_count(n, b) + 1)
                for t in range(b * NTB, (b + 1) * NTB):
                    dve.tensor_scalar(dst[:, t, :], src[:, t, :], mv[:, t, 0:1], rstd[:, t:t + 1],
                                      ALU.subtract, ALU.mult).then_inc(s("ln_xn"), 1)

            dve.wait_ge(s("x_in"), 16)
            for b in range(NB):
                ln_stats(0, b, h)
                ln_apply(0, b, h, h)
            ln_stats(1, 0, h)
            ln_apply(1, 0, h, xn)
            for c in range(NC):
                full(c)
                dve.tensor_copy(xnT[:, c * CH:(c + 1) * CH], vecb[c % 2][:, :]).then_inc(s("vec_read"), 1)
            k = NC
            full(k)
            dve.tensor_copy(lw[0:LORA_R, 1, :], vecb[k % 2][0:LORA_R, 0:D]).then_inc(s("vec_read"), 1)
            full(k + 1)
            dve.tensor_copy(lw[0:LORA_U, 2, :], vecb[(k + 1) % 2][0:LORA_U, 0:D]).then_inc(s("vec_read"), 1)
            full(k + 2)
            dve.wait_ge(s("lora_in"), 96)
            dve.tensor_tensor(lw[:, 0, :], vecb[k % 2][:, 0:D], w2[:, 0, :], ALU.add).then_inc(s("vec_read"), 1)
            dve.wait_ge(s("res_in"), 16)
            dve.tensor_tensor(res[:, :, :], res[:, :, :], vb[:, 0:1, :].to_broadcast([P, NT, D]),
                              ALU.add).then_inc(s("res_bias"), 1)
            dve.wait_ge(s("res_bias"), 1)
            for c in range(NC):
                idx = k + 3 + c
                full(idx)
                part = res[:, c * TPC:(c + 1) * TPC, :]
                dve.tensor_tensor(part, vecb[idx % 2][:, :].rearrange("p (t d) -> p t d", t=TPC), part,
                                  ALU.add).then_inc(s("vec_read"), 1)
            dve.wait_ge(s("rot_in"), 16)
            dve.wait_ge(s("amask_set"), 1)

            def row_max(bank, out, w, diagonal, last):
                if diagonal:
                    alone(dve, "dve_seen")
                    return dve.tensor_tensor_reduce(bank[:, 0:w], bank[:, 0:w], amask[:, CH - w:CH], 1.0, NEG,
                                                    ALU.add, ALU.max, out)
                return dve.tensor_reduce(out, bank[:, 0:w], AX_X, ALU.max)

            with dve.Fori(0, LAYERS) as l:
                vbase = V_START + l * V_LAYER

                def bank_of(k):
                    return vecb[(V_START + k) % 2]

                def affine(k, c, w, b):
                    full(vbase + k)
                    dve.tensor_scalar(xnT[:, c * CH:(c + 1) * CH], bank_of(k)[:, :], vc[:, COL[w]:COL[w] + 1],
                                      vc[:, COL[b]:COL[b] + 1], ALU.mult, ALU.add).then_inc(s("vec_read"), 1)

                own(vbase)
                dve.wait_ge(s("weights_in"), 64 * (l + 1))
                for j, (x, y) in enumerate((("bq", "u"), ("bqs", "us"))):
                    dve.tensor_tensor(bu[:, j:j + 1], vc[:, COL[x]:COL[x] + 1], vc[:, COL[y]:COL[y] + 1],
                                      ALU.add).then_inc(s("bu_ready"), 1)
                dve.wait_ge(s("bu_ready"), 2 * (l + 1))
                for c in range(NC):
                    if c % CB == 0:
                        if c:
                            ln_apply(1 + 2 * l, 1, h, xn)
                        for x in range(c, c + CB):
                            affine(LN_AT[x], x, "ln1w", "ln1b")
                        if not c:
                            ln_stats(1 + 2 * l, 1, h)
                    k = Q_AT[c]
                    col = slice(c * CH, (c + 1) * CH)
                    pos = slice(c * CH % S, c * CH % S + CH)
                    full(vbase + k)
                    dve.tensor_scalar(qf[:, col], bank_of(k)[:, :], vc[:, COL["bq"]:COL["bq"] + 1], None, ALU.add)
                    dve.scalar_tensor_tensor(out=rf[:, col], in0=bank_of(k)[:, :], scalar=bu[:, 0:1],
                                             in1=rot[:, 0, pos], op0=ALU.add, op1=ALU.mult)\
                        .then_inc(s("vec_read"), 1)
                    full(vbase + k + 1)
                    dve.scalar_tensor_tensor(out=rtmp[:, col], in0=bank_of(k + 1)[:, :], scalar=bu[:, 1:2],
                                             in1=rot[:, 1, pos], op0=ALU.add, op1=ALU.mult)\
                        .then_inc(s("rot_half"), 1)
                    dve.wait_ge(s("rot_half"), l * NC + c + 1)
                    dve.tensor_tensor(rf[:, col], rf[:, col], rtmp[:, col], ALU.add).then_inc(s("vec_read"), 1)
                    if c == S // CH - 1:
                        split(dve, l, 0)
                for c in range(NC):
                    k = V_LN + 2 * NC + c
                    full(vbase + k)
                    dve.tensor_tensor(vtok[:, c * TPC:(c + 1) * TPC, :],
                                      bank_of(k)[:, :].rearrange("p (t d) -> p t d", t=TPC),
                                      vb[:, VB["bv"]:VB["bv"] + 1, :].to_broadcast([P, TPC, D]),
                                      ALU.add).then_inc(s("vec_read"), 1)

                def maximum(k, i):
                    r, ib, k0, w, diagonal = A_LIST[i]
                    full(vbase + k)
                    out = mxa[:, r, ib:ib + 1] if diagonal else mxb[:, r, ib - TPC:ib - TPC + 1]
                    row_max(bank_of(k), out, w, diagonal, False).then_inc(s("vec_read"), 1)

                def combine(g, k):
                    own(vbase + k)
                    dve.tensor_tensor(mxa[:, :, TPC:SB_], mxa[:, :, TPC:SB_], mxb[:, :, :],
                                      ALU.max).then_inc(s("max_ready"), 1)

                def negate(g, k):
                    full(vbase + k)
                    if g:
                        dve.wait_ge(s("maxrow_in"), 32 * (l * NG + g))
                    rows = bank_of(k)[0:GH * SB_, 0:P]
                    dve.tensor_scalar(nm[:, 0, :], rows, -1.0, None, ALU.mult).then_inc(s("nm_high"), 1)
                    dve.wait_ge(s("nm_high"), l * NG + g + 1)
                    dve.scalar_tensor_tensor(out=nm[:, 1, :], in0=rows, scalar=-1.0, in1=nm[:, 0, :],
                                             op0=ALU.mult, op1=ALU.subtract).then_inc(s("vec_read"), 1)

                def context(g, k, c):
                    full(vbase + k)
                    b, hg = divmod(g, GPB)
                    t = b * SB_ + c * TPC
                    v = bank_of(k)[:, :].rearrange("p (t h d) -> p t h d", t=TPC, h=GH)
                    own(vbase + k)
                    dve.reciprocal(rz[:, :, :], v[:, :, :, HD0]).then_inc(s("rz_ready"), 1)
                    dve.wait_ge(s("rz_ready"), (l * NG + g) * 2 + c + 1)
                    dve.tensor_tensor(
                        att[:, t:t + TPC, hg * GH * HD0:(hg + 1) * GH * HD0].rearrange("p t (h d) -> p t h d", h=GH),
                        v[:, :, :, 0:HD0], rz[:, :, :].unsqueeze(3).to_broadcast([P, TPC, GH, HD0]),
                        ALU.mult).then_inc(s("vec_read"), 1)

                for i in range(NA):
                    maximum(V_LN + V_PROJ + i, i)
                combine(0, V_LN + V_PROJ + NA)
                negate(0, V_LN + V_PROJ + NA)
                for g in range(NG):
                    for k, (_, kind, x) in enumerate(group_items(g == NG - 1)):
                        k += V_G0 + g * V_GROUP
                        if kind == "A":
                            maximum(k, x)
                        if kind == "M":
                            combine(g + 1, k)
                            negate(g + 1, k)
                        if kind == "T":
                            context(g, k, x)

                def add_to_h(k, c):
                    full(vbase + k)
                    part = h[:, c * TPC:(c + 1) * TPC, :]
                    dve.tensor_tensor(part, bank_of(k)[:, :].rearrange("p (t d) -> p t d", t=TPC), part,
                                      ALU.add).then_inc(s("vec_read"), 1)

                dve.wait_ge(s("bias_added"), 2 * l + 1)
                for b in range(NB):
                    for c in range(b * CB, (b + 1) * CB):
                        full(vbase + V_POST + X_AT[c])
                        dve.tensor_copy(xnT[:, c * CH:(c + 1) * CH], bank_of(V_POST + X_AT[c])[:, :])\
                            .then_inc(s("vec_read"), 1)
                    for c in range(b * CB, (b + 1) * CB):
                        add_to_h(V_POST + O_AT[c], c)
                    if b:
                        ln_apply(2 + 2 * l, 0, h, xn)
                    own(vbase + V_POST + O_AT[c] + 1)
                    ln_stats(2 + 2 * l, b, h)
                for b in range(NB):
                    if b:
                        ln_apply(2 + 2 * l, b, h, xn)
                    for c in range(b * CB, (b + 1) * CB):
                        affine(V_POST + 2 * NC + c, c, "ln2w", "ln2b")
                dve.wait_ge(s("bias_added"), 2 * l + 2)
                for c in range(NC):
                    add_to_h(V_POST + 3 * NC + c, c)
                    if c == CB - 1:
                        own(vbase + V_POST + 3 * NC + c + 1)
                        ln_stats(3 + 2 * l, 0, h)
                    if c == NC - 2:
                        ln_apply(3 + 2 * l, 0, h, xn)

            own(V_R)
            dve.tensor_tensor(res[:, :, :], res[:, :, :], h[:, :, :], ALU.add).then_inc(s("res_ready"), 1)
            dve.wait_ge(s("res_ready"), 1)
            for b in range(NB):
                ln_stats(LN_LAST, b, res)
            for b in range(NB):
                ln_apply(LN_LAST, b, res, xn)
            for c in range(NC):
                full(V_R + c)
                dve.tensor_copy(xnT[:, c * CH:(c + 1) * CH], vecb[(V_R + c) % 2][:, :]).then_inc(s("vec_read"), 1)

            n_route = [0]

            def route(ins):
                n_route[0] += 1
                ins.then_inc(s("route"), 1)
                dve.wait_ge(s("route"), n_route[0])

            idx = V_R + NC
            full(idx)
            lg, e, e2, rank, key, sel1, sel2 = (wr[:, i] for i in range(7))

            def one(i):
                return wr[:, 7 + i // NE, :, i % NE]

            def wide(x):
                return x.unsqueeze(2).to_broadcast([P, NT, NE])

            mx, sm, rs, m1, km, m2, ds, rd = (one(i) for i in range(8))
            dve.tensor_copy(lg, vecb[idx % 2][:, 0:NT * NE].rearrange("p (t e) -> p t e", e=NE))\
                .then_inc(s("vec_read"), 1)
            own(idx + 1)
            for x in range(NE):
                ins = dve.memset(rank[:, :, x:x + 1], float(NE - x))
            route(ins)
            route(dve.tensor_reduce(mx, lg, AX_X, ALU.max))
            route(dve.tensor_tensor(e, lg, wide(mx), ALU.subtract))
            dve.wait_ge(s("route_exp"), 1)
            route(dve.tensor_reduce(sm, e, AX_X, ALU.add))
            route(dve.reciprocal(rs, sm))
            route(dve.tensor_tensor(e, e, wide(rs), ALU.mult))
            route(dve.tensor_reduce(m1, e, AX_X, ALU.max))

            def first_of(sel, vals, mval):
                route(dve.tensor_tensor(sel, vals, wide(mval), ALU.is_equal))
                route(dve.tensor_tensor(key, sel, rank, ALU.mult))
                route(dve.tensor_reduce(km, key, AX_X, ALU.max))
                route(dve.tensor_tensor(sel, key, wide(km), ALU.is_equal))

            first_of(sel1, e, m1)
            route(dve.scalar_tensor_tensor(out=e2, in0=sel1, scalar=-2.0, in1=e, op0=ALU.mult, op1=ALU.add))
            route(dve.tensor_reduce(m2, e2, AX_X, ALU.max))
            first_of(sel2, e2, m2)
            route(dve.tensor_tensor(ds, m1, m2, ALU.add))
            route(dve.tensor_scalar(ds, ds, 1e-20, None, ALU.add))
            route(dve.reciprocal(rd, ds))
            route(dve.tensor_tensor(sel1, sel1, sel2, ALU.add))
            route(dve.tensor_tensor(e, e, wide(rd), ALU.mult))
            route(dve.tensor_tensor(wt9[:, :, 0:NE], e, sel1, ALU.mult))
            route(dve.memset(wt9[:, :, NE:NE + 1], 1.0))
            route(dve.memset(wtb[:, :, :, :], 0.0))
            for k in range(3):
                part = wtb[:, :, k, 0:NE + 1]
                route(dve.tensor_copy(part, wt9[:, :, :]))
                if k < 2:
                    route(dve.tensor_tensor(wt9[:, :, :], wt9[:, :, :], part, ALU.subtract))
            route(dve.tensor_copy(wtf[:, :, :, :], wtb[:, :, :, :]))
            assert n_route[0] == N_ROUTE, n_route[0]
            for c in range(NC):
                idx = V_R + NC + 1 + c
                full(idx)
                dve.tensor_copy(wT[:, c * CH:(c + 1) * CH], vecb[idx % 2][0:KFULL, :]).then_inc(s("vec_read"), 1)

            with dve.Fori(0, MOE_TURNS) as i:
                def add_down(j):
                    c = j % NC
                    k = down_at(j)
                    full(V_MOE + i * MOE_V + k)
                    part = res[:, c * TPC:(c + 1) * TPC, :]
                    own(V_MOE + i * MOE_V + k - 1)
                    dve.tensor_tensor(part, vecb[(V_MOE + k) % 2][:, :].rearrange("p (t d) -> p t d", t=TPC), part,
                                      ALU.add).then_inc(s("vec_read"), 1)

                for j in range(MOE_J):
                    k = up_at(j)
                    full(V_MOE + i * MOE_V + k)
                    dve.wait_ge(s("act_read"), act_read(A_MOE + i * MOE_J + j))
                    hb = moeb[:, 2, j % 2, :]
                    dve.tensor_tensor(hb, moeb[:, 0, j % 2, :], vecb[(V_MOE + k) % 2][:, :],
                                      ALU.mult).then_inc(s("moe_hidden"), 1)
                    dve.wait_ge(s("moe_hidden"), i * MOE_J + j + 1)
                    dve.tensor_tensor(hb, hb, moeb[:, 1, j % 2, :], ALU.mult).then_inc(s("vec_read"), 1)
                    if j:
                        add_down(j - 1)
                add_down(MOE_J - 1)

            own(V_H)
            dve.memset(hid[HD1:KFULL, :, :], 0.0).then_inc(s("zeros1_set"), 1)

            def project(idx, par_v, par, n):
                full(idx)
                bank = vecb[par_v % 2]
                if n < NC:
                    col = slice(n * CH, (n + 1) * CH)
                    dve.tensor_scalar(hid[0:HD1, 2 * par, col], bank[0:HD1, :], SCALE1, None, ALU.mult)
                    dve.tensor_copy(hid[0:HD1, 2 * par + 1, col], bank[HD1:2 * HD1, :]).then_inc(s("vec_read"), 1)
                else:
                    t = (n - NC) * V_TILES
                    dve.tensor_copy(vh[par][:, t:t + V_TILES, 0:HD1],
                                    bank[:, :].rearrange("p (t d) -> p t d", d=HD1)).then_inc(s("vec_read"), 1)

            for n in range(V1_PROJ):
                project(V_H + n, V_H + n, 0, n)
            att_bi = att[:, :, :].rearrange("p (b i) d -> p b i d", b=NB)

            def pair(j, base, pbase, first, last):
                v = 0
                for kind, u, x in pair_items(first, last):
                    par = u % 2
                    if kind == "S":
                        k = (2 * j + u) * NS1 + x
                        dve.wait_ge(s("act_full"), A_H + k + 1)
                        w = (STEPS1[x][0][1] + 1) * P
                        src = pairs[x % BUF1]
                        src = src[:, :, 0:w] if len(STEPS1[x]) > 1 else src[:, :, :].rearrange("p u t -> p (u t)")[:, 0:w]
                        dve.tensor_reduce(nmax[:, x, 0:len(STEPS1[x])], src, AX_X, ALU.max,
                                          negate=True).then_inc(s("max1_ready"), 1)
                        continue
                    idx, bank = base + v, vecb[(pbase + v) % 2]
                    if kind == "P":
                        project(idx, pbase + v, 1 - par, x)
                    if kind == "T":
                        full(idx)
                        n, part = x
                        w = len(blocks1(n)[part * TPC:(part + 1) * TPC]) * P
                        dve.tensor_copy(probT[:, n % BUF1, part * CH:part * CH + w],
                                        bank[:, 0:w]).then_inc(s("vec_read"), 1)
                    if kind == "V":
                        full(idx)
                        m, ib = len(STEPS1[x]), STEPS1[x][0][1]
                        b0 = STEPS1[x][0][0]
                        dve.reciprocal(zsum[:, x, 0:m], zsum[:, x, 0:m]).then_inc(s("rz1_ready"), 1)
                        dve.wait_ge(s("rz1_ready"), (2 * j + u) * NS1 + x + 1)
                        dve.tensor_tensor(att_bi[:, b0:b0 + m, ib, par * HD1:(par + 1) * HD1],
                                          bank[:, 0:m * HD1].rearrange("p (b d) -> p b d", b=m),
                                          zsum[:, x, 0:m].unsqueeze(2).to_broadcast([P, m, HD1]),
                                          ALU.mult).then_inc(s("vec_read"), 1)
                    if kind == "X":
                        full(idx)
                        dve.tensor_copy(osb[:, X_BUF[x], :], bank[:, :]).then_inc(s("vec_read"), 1)
                    if kind == "Y":
                        full(idx)
                        part = res[:, x * TPC:(x + 1) * TPC, :]
                        dve.tensor_tensor(part, bank[:, :].rearrange("p (t d) -> p t d", t=TPC), part,
                                          ALU.add).then_inc(s("vec_read"), 1)
                    v += 1

            pair(0, V_P0, V_P0, True, False)
            with dve.Fori(1, H1 // 2 - 1) as j:
                pair(j, V_P1 + (j - 1) * V_PAIR, V_P1, False, False)
            pair(H1 // 2 - 1, V_P1 + (H1 // 2 - 2) * V_PAIR, V_P1, False, True)


def _rotations():
    m = HD0 // 2
    inv = (1.0 / 10000.0 ** (np.arange(0, HD0, 2, dtype=np.float32) / np.float32(HD0))).astype(np.float32)
    angle = inv.astype(np.float64)[:, None] * np.arange(S)[None, :]
    sin, cos = np.sin(angle), np.cos(angle)
    queries = np.stack([np.concatenate([sin, sin]), np.concatenate([cos, -cos])], 1)
    queries = np.tile(queries, (P // HD0, 1, 1))
    assert m * 2 == HD0
    return queries.astype(np.float32), np.concatenate([cos, sin]).astype(np.float32)


def kernel(**inputs):
    import concourse.bacc as bacc
    from concourse.bass_utils import run_bass_kernel_spmd

    a = {k: np.asarray(v) for k, v in inputs.items()}
    swap = np.arange(D).reshape(H0, 2, HD0 // 2)[:, ::-1].reshape(-1)

    def turned(name):
        return np.transpose(a["L0_attn_" + name], (0, 2, 1))

    wq = turned("Wq")
    u = a["L0_attn_u_bias"].reshape(LAYERS, D)
    bq = a["L0_attn_bq"]
    rows = [bq, bq[:, swap], u, u[:, swap]] + [a["L0_attn_" + n] for n in ("bk", "ln1_w", "ln1_b", "ln2_w", "ln2_b")]
    b1 = a["L0_attn_b1"].reshape(LAYERS, NF, P)
    rows += [b1[:, m] for m in range(NF)]
    queries, keys = _rotations()

    def experts(w, shared):
        out = np.zeros((D, NHC * P), np.float32)
        out[:, :NE * INTER] = np.transpose(w, (1, 0, 2)).reshape(D, NE * INTER)
        out[:, NE * INTER:HID] = shared
        return out.reshape(D, NHC, P).transpose(1, 0, 2)

    moe = np.zeros((NHC, P, 4 * P), np.float32)
    moe[:, :, 0:P] = experts(a["L1_ffn_wg"], a["L1_ffn_swg"])
    moe[:, :, P:2 * P] = experts(a["L1_ffn_wu"], a["L1_ffn_swu"])
    down = np.zeros((NHC * P, D), np.float32)
    down[:NE * INTER] = a["L1_ffn_wd"].reshape(NE * INTER, D)
    down[NE * INTER:HID] = a["L1_ffn_swd"]
    moe[:, :, 2 * P:3 * P] = down.reshape(NHC, P, D)
    owner = np.zeros((NE + 1, NHC * P), np.float32)
    owner[np.minimum(np.arange(NHC * P) // INTER, NE), np.arange(NHC * P)] = 1.0
    for k in range(3):
        moe[:, 32 * k:32 * k + NE + 1, 3 * P:4 * P] = owner.reshape(NE + 1, NHC, P).transpose(1, 0, 2)

    qkv1 = np.concatenate([np.transpose(a["L1_attn_" + n], (0, 2, 1)) for n in ("wq", "wk", "wv")], 2)
    wo1 = a["L1_attn_wo"].T.reshape(H1 // 2, 2 * HD1, D)

    arrays = {
        "x": a["L0_attn_x"].reshape(T, D),
        "wa": np.stack([wq, wq[:, :, swap], turned("Wk"), turned("Wv"), turned("Wo")], 2),
        "w1": turned("W1"),
        "w2": turned("W2").reshape(LAYERS, NF, P, D).transpose(0, 2, 1, 3),
        "vc": np.stack(rows, 2),
        "vb": np.broadcast_to(np.stack([a["L0_attn_" + n] for n in ("bv", "bo", "b2")], 1)[:, None],
                              (LAYERS, P, 3, D)),
        "wt": a["L0_ffn_W"].T,
        "fb": a["L0_ffn_b"],
        "ld": a["L0_ffn_lora_down"].T,
        "da": a["L0_ffn_down_aux"],
        "lu": a["L0_ffn_lora_up"].T,
        "ua": a["L0_ffn_up_aux"].T,
        "rot": queries,
        "pos": keys,
        "qkv1": qkv1,
        "wo1": wo1,
        "gate": a["L1_ffn_gate_w"].T,
        "moe": moe,
    }
    nc = bacc.Bacc("TRN2", target_bir_lowering=False, num_devices=1)
    feeds, args = {}, []
    for name, array in arrays.items():
        array = np.ascontiguousarray(array)
        feeds[f"in_{name}"] = array
        args.append(nc.dram_tensor(f"in_{name}", array.shape, mybir.dt.from_np(array.dtype),
                                   kind="ExternalInput").ap())
    args.append(nc.dram_tensor("out", [T, D], F32, kind="ExternalOutput").ap())
    build(nc, *args)
    r = run_bass_kernel_spmd(nc, [feeds], core_ids=[0])
    return r.results[0]["out"].reshape(NB, S, D)
```
